# Optimizing a Trainium2 kernel written in Bass

```python
import numpy as np
import jax
import jax.numpy as jnp

def _softmax(x, axis=-1):
    return jax.nn.softmax(x, axis=axis)

def _gelu(x):
    return jax.nn.gelu(x, approximate=True)

def _silu(x):
    return jax.nn.silu(x)

def _sigmoid(x):
    return jax.nn.sigmoid(x)

def _layernorm(x, axis=-1, eps=1e-05):
    m = jnp.mean(x, axis=axis, keepdims=True)
    v = jnp.var(x, axis=axis, keepdims=True)
    return (x - m) / jnp.sqrt(v + eps)

def _scatter_add(tgt, idx, src, axis=0):
    return tgt.at[idx].add(src)

def _segment_sum(src, seg, n):
    return jax.ops.segment_sum(src, seg, n)
kernel_name = 'mk_vit_tower_cls_d1_tok_img512_r4_f68a9a'

def setup_inputs(seed: int=0):
    np.random.seed(seed)
    _w = jnp.asarray

    def _rec_inputs():
        import jax
        import jax.numpy as jnp
        _rk = jax.random.key(seed)
        x = -0.000477451 + 1.00034 * jax.random.normal(jax.random.fold_in(_rk, 1), (8, 32, 32, 29), jnp.float32)
        cls_tok = 0.02 * jax.random.normal(jax.random.fold_in(_rk, 5), (1, 1, 128), jnp.float32)
        return (x, cls_tok)
    x, cls_tok = _rec_inputs()

    def _L0_tok_setup():
        import jax, jax.numpy as jnp
        import numpy as np
        import math
        H, W_DIM, D_MODEL, B = (32, 32, 128, 128)
        F_TOTAL = 29
        SEQ_LEN = H * W_DIM

        def make_pe(seq_len: int, d_model: int) -> jnp.ndarray:
            position = np.arange(seq_len, dtype=np.float32)[:, None]
            div_term = np.exp(np.arange(0, d_model, 2, dtype=np.float32) * (-math.log(10000.0) / d_model))
            pe = np.zeros((seq_len, d_model), dtype=np.float32)
            pe[:, 0::2] = np.sin(position * div_term)
            pe[:, 1::2] = np.cos(position * div_term)
            return jnp.asarray(pe)
        key = jax.random.key(seed)
        k1, k2 = jax.random.split(key)
        state_tensor = jax.random.normal(k1, (B, H, W_DIM, F_TOTAL), dtype=jnp.float32)
        W = jax.random.normal(k2, (F_TOTAL, D_MODEL), dtype=jnp.float32) * 0.05
        return {'state_tensor': state_tensor, 'W': W}
    _L0_tok_all = _L0_tok_setup()
    _L0_tok_in = {k: v for k, v in _L0_tok_all.items() if k in ('W',)}
    del _L0_tok_all

    def _L0_attn_setup():
        import jax, jax.numpy as jnp
        import numpy as np
        N_HEADS = 8
        key = jax.random.key(seed)
        ks = jax.random.split(key, 5)
        b, s, d = (2, 1024, 128)
        return {'x': jax.random.normal(ks[0], (b, s, d), dtype=jnp.float32), 'qkv_w': jax.random.normal(ks[1], (3 * d, d), dtype=jnp.float32) * 0.02, 'qkv_b': jax.random.normal(ks[2], (3 * d,), dtype=jnp.float32) * 0.02, 'out_w': jax.random.normal(ks[3], (d, d), dtype=jnp.float32) * 0.02, 'out_b': jax.random.normal(ks[4], (d,), dtype=jnp.float32) * 0.02}
    _L0_attn_all = _L0_attn_setup()
    _L0_attn_in = {k: v for k, v in _L0_attn_all.items() if k in ('qkv_w', 'qkv_b', 'out_w', 'out_b')}
    del _L0_attn_all

    def _L0_ffn_setup():
        import jax, jax.numpy as jnp
        import numpy as np
        EPS = 1e-05
        NUM_HEADS = 8
        TOP_K = 2
        CAP_FACTOR = 2

        def layernorm(x, g, b):
            m = jnp.mean(x, axis=-1, keepdims=True)
            v = jnp.var(x, axis=-1, keepdims=True)
            return (x - m) * jax.lax.rsqrt(v + EPS) * g + b
        key = jax.random.key(seed)
        ks = jax.random.split(key, 16)
        B, S, H, E, F = (2, 512, 128, 64, 512)
        s = 0.02
        return {'x': jax.random.normal(ks[0], (B, S, H), jnp.float32), 'ln1_g': jnp.ones((H,), jnp.float32), 'ln1_b': jnp.zeros((H,), jnp.float32), 'wq': jax.random.normal(ks[1], (H, H), jnp.float32) * s, 'wk': jax.random.normal(ks[2], (H, H), jnp.float32) * s, 'wv': jax.random.normal(ks[3], (H, H), jnp.float32) * s, 'wo': jax.random.normal(ks[4], (H, H), jnp.float32) * s, 'ln2_g': jnp.ones((H,), jnp.float32), 'ln2_b': jnp.zeros((H,), jnp.float32), 'wr': jax.random.normal(ks[5], (H, E), jnp.float32) * s, 'w1': jax.random.normal(ks[6], (E, H, F), jnp.float32) * s, 'b1': jnp.zeros((E, F), jnp.float32), 'w2': jax.random.normal(ks[7], (E, F, H), jnp.float32) * s, 'b2': jnp.zeros((E, H), jnp.float32)}
    _L0_ffn_all = _L0_ffn_setup()
    _L0_ffn_in = {k: v for k, v in _L0_ffn_all.items() if k in ('ln1_g', 'ln1_b', 'wq', 'wk', 'wv', 'wo', 'ln2_g', 'ln2_b', 'wr', 'w1', 'b1', 'w2', 'b2')}
    del _L0_ffn_all
    return {'x': x, 'cls_tok': cls_tok, 'L0_tok_W': _L0_tok_in['W'], 'L0_attn_qkv_w': _L0_attn_in['qkv_w'], 'L0_attn_qkv_b': _L0_attn_in['qkv_b'], 'L0_attn_out_w': _L0_attn_in['out_w'], 'L0_attn_out_b': _L0_attn_in['out_b'], 'L0_ffn_ln1_g': _L0_ffn_in['ln1_g'], 'L0_ffn_ln1_b': _L0_ffn_in['ln1_b'], 'L0_ffn_wq': _L0_ffn_in['wq'], 'L0_ffn_wk': _L0_ffn_in['wk'], 'L0_ffn_wv': _L0_ffn_in['wv'], 'L0_ffn_wo': _L0_ffn_in['wo'], 'L0_ffn_ln2_g': _L0_ffn_in['ln2_g'], 'L0_ffn_ln2_b': _L0_ffn_in['ln2_b'], 'L0_ffn_wr': _L0_ffn_in['wr'], 'L0_ffn_w1': _L0_ffn_in['w1'], 'L0_ffn_b1': _L0_ffn_in['b1'], 'L0_ffn_w2': _L0_ffn_in['w2'], 'L0_ffn_b2': _L0_ffn_in['b2']}

def reference(x, cls_tok, L0_tok_W, L0_attn_qkv_w, L0_attn_qkv_b, L0_attn_out_w, L0_attn_out_b, L0_ffn_ln1_g, L0_ffn_ln1_b, L0_ffn_wq, L0_ffn_wk, L0_ffn_wv, L0_ffn_wo, L0_ffn_ln2_g, L0_ffn_ln2_b, L0_ffn_wr, L0_ffn_w1, L0_ffn_b1, L0_ffn_w2, L0_ffn_b2):
    import jax
    import jax.numpy as jnp

    def _L0_tok_ref(state_tensor, W):
        import jax, jax.numpy as jnp
        import numpy as np
        import math
        H, W_DIM, D_MODEL, B = (32, 32, 128, 128)
        F_TOTAL = 29
        SEQ_LEN = H * W_DIM

        def make_pe(seq_len: int, d_model: int) -> jnp.ndarray:
            position = np.arange(seq_len, dtype=np.float32)[:, None]
            div_term = np.exp(np.arange(0, d_model, 2, dtype=np.float32) * (-math.log(10000.0) / d_model))
            pe = np.zeros((seq_len, d_model), dtype=np.float32)
            pe[:, 0::2] = np.sin(position * div_term)
            pe[:, 1::2] = np.cos(position * div_term)
            return jnp.asarray(pe)
        b, h, w, f = state_tensor.shape
        s = h * w
        x = state_tensor.reshape(b, s, f)
        emb = jnp.einsum('bsf,fd->bsd', x, W)
        pe = make_pe(s * 2, W.shape[1])[:s]
        return emb + pe[None, :, :]

    def _L0_attn_ref(x, qkv_w, qkv_b, out_w, out_b):
        import jax, jax.numpy as jnp
        import numpy as np
        N_HEADS = 8
        b, s, d = x.shape
        h = N_HEADS
        c = d // h
        factor = 1.0 / jnp.sqrt(jnp.asarray(c, dtype=x.dtype))
        qkv = x @ qkv_w.T + qkv_b
        qkv = qkv.reshape(b, s, h, 3, c)
        q, k, v = (qkv[..., 0, :], qkv[..., 1, :], qkv[..., 2, :])
        scores = jnp.einsum('bshc,bthc->bhst', q, k) * factor
        attn = jax.nn.softmax(scores, axis=-1)
        ctx = jnp.einsum('bhst,bthc->bshc', attn, v).reshape(b, s, d)
        return ctx @ out_w.T + out_b

    def _L0_ffn_ref(x, ln1_g, ln1_b, wq, wk, wv, wo, ln2_g, ln2_b, wr, w1, b1, w2, b2):
        import jax, jax.numpy as jnp
        import numpy as np
        EPS = 1e-05
        NUM_HEADS = 8
        TOP_K = 2
        CAP_FACTOR = 2

        def layernorm(x, g, b):
            m = jnp.mean(x, axis=-1, keepdims=True)
            v = jnp.var(x, axis=-1, keepdims=True)
            return (x - m) * jax.lax.rsqrt(v + EPS) * g + b
        B, S, H = x.shape
        NH = NUM_HEADS
        dh = H // NH
        x1 = layernorm(x, ln1_g, ln1_b)
        q = (x1 @ wq).reshape(B, S, NH, dh)
        k = (x1 @ wk).reshape(B, S, NH, dh)
        v = (x1 @ wv).reshape(B, S, NH, dh)
        scores = jnp.einsum('bqhd,bkhd->bhqk', q, k) * dh ** (-0.5)
        p = jax.nn.softmax(scores, axis=-1)
        attn_out = jnp.einsum('bhqk,bkhd->bqhd', p, v).reshape(B, S, H) @ wo
        x = x + attn_out
        x2 = layernorm(x, ln2_g, ln2_b).reshape(B * S, H)
        T = B * S
        E = wr.shape[1]
        C = CAP_FACTOR * (T * TOP_K // E)
        probs = jax.nn.softmax(x2 @ wr, axis=-1)
        gate_v, gate_i = jax.lax.top_k(probs, TOP_K)
        gate_v = gate_v / jnp.sum(gate_v, axis=-1, keepdims=True)
        ef = gate_i.reshape(-1)
        gf = gate_v.reshape(-1)
        oh = jax.nn.one_hot(ef, E, dtype=x2.dtype)
        pos = jnp.sum((jnp.cumsum(oh, axis=0) - oh) * oh, axis=1).astype(jnp.int32)
        keep = (pos < C).astype(x2.dtype)
        posc = jnp.minimum(pos, C - 1)
        tok = jnp.repeat(x2, TOP_K, axis=0) * keep[:, None]
        buf = jnp.zeros((E, C, H), x2.dtype).at[ef, posc].add(tok)
        h = jax.nn.gelu(jnp.einsum('ech,ehf->ecf', buf, w1) + b1[:, None, :])
        y = jnp.einsum('ecf,efh->ech', h, w2) + b2[:, None, :]
        ys = y[ef, posc] * (gf * keep)[:, None]
        moe_out = ys.reshape(T, TOP_K, H).sum(axis=1).reshape(B, S, H)
        return x + moe_out
    h = _L0_tok_ref(x, L0_tok_W)
    h = jnp.concatenate([jnp.broadcast_to(cls_tok, (h.shape[0], 1, h.shape[2])), h], axis=1)
    h = h + _L0_attn_ref(_layernorm(h, axis=-1), L0_attn_qkv_w, L0_attn_qkv_b, L0_attn_out_w, L0_attn_out_b)
    h = h + _L0_ffn_ref(_layernorm(h, axis=-1), L0_ffn_ln1_g, L0_ffn_ln1_b, L0_ffn_wq, L0_ffn_wk, L0_ffn_wv, L0_ffn_wo, L0_ffn_ln2_g, L0_ffn_ln2_b, L0_ffn_wr, L0_ffn_w1, L0_ffn_b1, L0_ffn_w2, L0_ffn_b2)
    return h

_drawn_inputs = setup_inputs


def setup_inputs(seed=0):
    import zlib

    import numpy as np

    out = dict(_drawn_inputs(seed))
    spreads = {'L0_ffn_ln1_g': (1.0, 0.6),
     'L0_ffn_ln1_b': (0.0, 0.8),
     'L0_ffn_ln2_g': (1.0, 0.56),
     'L0_ffn_ln2_b': (0.0, 0.361),
     'L0_ffn_b1': (0.0, 0.8),
     'L0_ffn_b2': (0.0, 0.314)}
    factors = {'cls_tok': 4.817,
     'L0_attn_qkv_b': 6.887,
     'L0_ffn_wq': 8.0,
     'L0_ffn_wk': 8.0,
     'L0_ffn_wv': 3.138,
     'L0_ffn_wo': 3.031,
     'L0_ffn_w1': 2.985,
     'L0_ffn_w2': 2.754}
    for name, (base, spread) in spreads.items():
        noise = np.random.default_rng([zlib.crc32(name.encode()), seed]).standard_normal(out[name].shape)
        drawn = base * np.exp(spread * noise) if base else spread * noise
        out[name] = jnp.asarray(drawn.astype(out[name].dtype))
    for name, factor in factors.items():
        out[name] = (out[name] * factor).astype(out[name].dtype)
    return out
```

```python
from contextlib import ExitStack

import numpy as np

import concourse.bass as bass
from concourse import mybir

ALU = mybir.AluOpType
ACT = mybir.ActivationFunctionType
AX_X = mybir.AxisListType.X
F32 = mybir.dt.float32
F32R = mybir.dt.float32r
BF16 = mybir.dt.bfloat16
I32 = mybir.dt.int32
U32 = mybir.dt.uint32

P = 128
D = 128
H = 8
C = D // H
B = 8
S = 1024
NC = S // P
NT = NC + 1
F_IN = 29
E = 64
F = 512
FC = F // P
TOPK = 2
CAP = 2 * (B * (S + 1) * TOPK // E)
SLOTS = E * CAP
SC = CAP // P
EPS = 1e-5
SCALE = 1.0 / C ** 0.5
RSQRT_GUESS = 0x5F3759DF
OUT_OF_BOUNDS = float(1 << 20)
HALF = 64
GRP = 3 * C


def build(nc, x, cls_tok, pe, tokW, wq1, wk1, wv1, bq1, bk1, bv1, wo1, bo1,
          ln1g, ln1b, wq2, wk2, wv2, wo2, ln2g, ln2b, wr, w1, b1, w2, b2,
          ident_d, headmask_d, headmaskT_d, lower_d, iota_d, valid_d, out):
    ctx = ExitStack()
    with ctx:
        def sb(name, shape, dt=F32):
            return ctx.enter_context(nc.sbuf_tensor(name, shape, dt))

        def psum(name, shape):
            return ctx.enter_context(nc.psum_tensor(name, shape, F32))

        def sem(name):
            return ctx.enter_context(nc.semaphore(name))

        slots_in = nc.dram_tensor("slots_in", [SLOTS, D], F32).ap()
        slots_out = nc.dram_tensor("slots_out", [SLOTS, D], F32).ap()

        ident = sb("ident", [P, P])
        headmask = sb("headmask", [P, H])
        headmaskT = sb("headmaskT", [H, P])
        lower = sb("lower", [P, P], BF16)
        ones_bf = sb("ones_bf", [P, P], BF16)
        ones_f = sb("ones_f", [P, 1])
        iota1 = sb("iota1", [P, E])
        valid = sb("valid", [P, NT])
        pe_t = sb("pe_t", [P, NC, D])
        tokw = sb("tokw", [F_IN, D])
        wq = sb("wq", [P, 2, D])
        wk = sb("wk", [P, 2, D])
        wv = sb("wv", [P, 2, D])
        wo = sb("wo", [P, 2, D])
        bq = sb("bq", [P, 1])
        bk = sb("bk", [P, 1])
        bv = sb("bv", [P, D])
        bo = sb("bo", [P, D])
        g1 = sb("g1", [P, 1])
        c1 = sb("c1", [P, 1])
        g2 = sb("g2", [P, D])
        c2 = sb("c2", [P, D])
        wrt = sb("wrt", [P, E])
        b1t = sb("b1t", [P, FC, E])
        clst = sb("clst", [P, D])

        res = sb("res", [P, B, NT, D])
        gidx = sb("gidx", [P, B, NT, TOPK], U32)
        gate = sb("gate", [P, B, NT, TOPK])

        xT = sb("xT", [F_IN, S])
        hb = sb("hb", [P, NT, D])
        G = sb("G", [P, NT, D])
        N = sb("N", [P, NT, D])
        st = sb("st", [P, NT, 6])
        sm = sb("sm", [P, 8, NT])
        smi = sb("smi", [P, NT], I32)
        nT = sb("nT", [P, NT, P])
        qh = sb("qh", [P, S], F32R)
        ql = sb("ql", [P, S], F32R)
        kh = sb("kh", [P, S], F32R)
        kl = sb("kl", [P, S], F32R)
        qst = sb("qst", [P, H // 2, S], F32R)
        kst = sb("kst", [P, H, S], F32R)
        zrow = sb("zrow", [4 * NC, P])
        vt = sb("vt", [P, NC, H, 32])
        vcb = sb("vcb", [P, D])
        qkc = sb("qkc", [P, 2])
        bd = sb("bd", [P, 2, H])
        bdh = sb("bdh", [P, 2, H], F32R)
        bdl = sb("bdl", [P, 2, H], F32R)
        mxu = sb("mxu", [P, H, NC, 3])
        mr = sb("mr", [P, H, NC], F32R)
        mT = sb("mT", [NC, 2, P], F32R)
        pck = sb("pck", [P, H, NC])
        pr = sb("pr", [P, 4, S])
        avs = sb("avs", [P, 2, 256])
        U = sb("U", [P, NC, H, C])
        Ut = sb("Ut", [P, NC, H, C])
        den = sb("den", [P, NC, H])
        ctxT = sb("ctxT", [P, NT, P])
        csc = sb("csc", [H, 8])
        pc = sb("pc", [H, S])
        pcT = sb("pcT", [P, NC, H])
        cm = sb("cm", [H, D])
        x2 = sb("x2", [P, NT, D])
        lg = sb("lg", [P, NT, E])
        mv = sb("mv", [P, NT, 8])
        mi = sb("mi", [P, NT, 8], U32)
        e1 = sb("e1", [P, TOPK, NT])
        oh = sb("oh", [P, TOPK, NT, E])
        ohs = sb("ohs", [P, NT, E], BF16)
        run = sb("run", [P, NT + 1, E], BF16)
        pos = sb("pos", [P, NT, E])
        pk = sb("pk", [P, TOPK, NT])
        keep = sb("keep", [P, TOPK, NT])
        rt = sb("rt", [P, 12, NT])
        sidx = sb("sidx", [P, NT, TOPK], U32)

        zeros = N[:, 0:SC, :]
        w1t = [nT[:, 0:4, :].rearrange("p c s -> p (c s)"), nT[:, 4:8, :].rearrange("p c s -> p (c s)")]
        w2t = [ctxT[:, 0:4, :], ctxT[:, 4:8, :]]
        xin = [N[:, 0:4, :], N[:, 4:8, :]]
        xinT = [G[:, 0:4, :].rearrange("p c s -> p (c s)"), G[:, 4:8, :].rearrange("p c s -> p (c s)")]
        hid = [pr[:, 0:2, :].rearrange("p a (b s) -> p (a b) s", b=2),
               pr[:, 2:4, :].rearrange("p a (b s) -> p (a b) s", b=2)]
        b2t = [x2[:, 0, :], x2[:, 1, :]]
        yout = [hb[:, 0:4, :], hb[:, 4:8, :]]
        rows = [N, G, x2, nT]
        fin = [hb, ctxT]
        tick = sb("tick", [P, 1])
        gi = sb("gi", [P, 2, NT, TOPK], U32)
        gg = sb("gg", [P, 2, NT, TOPK])

        psS = psum("psS", [P, 2, S])
        psM = psum("psM", [P, 2, 512])
        psV = psum("psV", [P, 512])
        psX = psum("psX", [P, 512])
        m8 = psM[:, :, :].rearrange("p i (c d) -> p (i c) d", d=D)
        xc = psX[:, 0:1]
        xq, xk = psX[:, 2:3], psX[:, 3:4]
        xcc = psX[0:H, 4:5]
        xct = psX[:, 6:7]
        xpt = psX[:, 64:64 + NC * H]
        xvc = psX[:, 128:256]
        xck = psX[:, 256:256 + NC * H]
        xo = psX[0:H, 256:384]
        xm = psX[0:NC, 384:512]
        xav = psX[:, 128:384]
        xpr = psX[0:1, 384:512]
        xn9 = psX[:, 0:128]
        xlg = psX[:, 128:128 + E]
        xps = psX[:, 256:256 + E]

        names = """const clear minus cls init zeroed x emb embr chain n nt nT q k v hi qkl vt bd stk ckp ck cqp cm ce ctp
            ct co cmk ccp cc p1 p1u mr mtp mT mrow0 mrow1 p2 exp av avs avt u pd pe ctx cxp cxT o or x2 x2p x2T
            lgp oh pos rr gd ge sidx scat
            wa0 wa1 wb0 wb1 bb0 bb1 xi0 xi1 tp xt hp gl yp yo yst0 yst1 done
            tick gi ga0 ga1 fin out0 out1 outf x2f ysf""".split()
        s = {n: sem("s_" + n) for n in names}

        CHAIN = 142
        CONSTS = 26
        STK = 16 * (6 * H + 2)
        U_HEAD = 2 * NC
        T_ATT = H * NC

        block = ctx.enter_context(nc.Block())

        @block.sync
        def _(sp):
            loads = [(ident[:, :], ident_d), (headmask[:, :], headmask_d), (headmaskT[:, :], headmaskT_d),
                     (iota1[:, :], iota_d), (valid[:, :], valid_d), (pe_t[:, :, :], pe), (tokw[:, :], tokW),
                     (wq[:, 0, :], wq1), (wk[:, 0, :], wk1), (wv[:, 0, :], wv1), (wo[:, 0, :], wo1),
                     (wq[:, 1, :], wq2), (wk[:, 1, :], wk2), (wv[:, 1, :], wv2), (wo[:, 1, :], wo2),
                     (bq[:, :], bq1), (bk[:, :], bk1), (bv[:, :], bv1.broadcast_to([P, D])),
                     (bo[:, :], bo1.broadcast_to([P, D])), (g1[:, :], ln1g), (c1[:, :], ln1b),
                     (g2[:, :], ln2g.broadcast_to([P, D])), (c2[:, :], ln2b.broadcast_to([P, D])),
                     (wrt[:, :], wr), (lower[:, :], lower_d), (b1t[:, :, :], b1)]
            assert len(loads) == CONSTS
            for dst, src in loads:
                sp.dma_start(dst, src).then_inc(s["const"], 16)
            sp.wait_ge(s["clear"], 1)
            sp.dma_start(clst[0:1, :], cls_tok).then_inc(s["cls"], 16)
            for e in range(E):
                sp.dma_start(slots_in[e * CAP:(e + 1) * CAP, :].rearrange("(p c) d -> p (c d)", p=P),
                             zeros).then_inc(s["zeroed"], 16)
            sp.wait_ge(s["init"], 1)
            for h in range(H):
                p0 = HALF * (h % 2) + GRP
                sp.dma_start(kst[p0:p0 + 1, h, :].bitcast(F32), mT[:, 0, :].bitcast(F32)).then_inc(s["minus"], 16)
            with sp.Fori(0, B) as b:
                sp.wait_ge(s["emb"], b + 1)
                sp.dma_start(xT[:, :], x[:, bass.ds(b * S, S)]).then_inc(s["x"], 16)
                for a in range(2):
                    J = 2 * b + a
                    sp.wait_ge(s["hi"], 2 * J + 1)
                    for p0 in (GRP, HALF + GRP):
                        sp.dma_start(qst[p0:p0 + 1, :, :].bitcast(F32), zrow[:, :]).then_inc(s["stk"], 16)
                    for src, dst, parts, ready, n in ((qh, qst, (0, 1), "hi", 1), (ql, qst, (2,), "qkl", 1),
                                                      (kh, kst, (0, 2), "hi", 2), (kl, kst, (1,), "qkl", 2)):
                        sp.wait_ge(s[ready], 2 * J + n)
                        for h in range(H):
                            for r in parts:
                                p0 = HALF * (h % 2) + C * r
                                sp.dma_start(dst[p0:p0 + C, h if dst is kst else h // 2, :].bitcast(F32),
                                             src[C * h:C * h + C, :].bitcast(F32)).then_inc(s["stk"], 16)
                    for h in range(H):
                        if h % 2 == 0:
                            sp.wait_ge(s["mT"], J * H + h + 2)
                        p0 = HALF * (h % 2) + GRP
                        sp.dma_start(qst[p0:p0 + 1, h // 2, :].bitcast(F32),
                                     mT[:, h % 2, :].bitcast(F32)).then_inc(s["mrow%d" % (h % 2)], 16)
            sp.wait_ge(s["rr"], B + 1)
            sp.wait_ge(s["scat"], 16 * B * NT * TOPK)
            with sp.Fori(0, E // 2) as g:
                for i in range(2):
                    e = 2 * g + i
                    sp.wait_ge(s["tp"], e + 1)
                    sp.dma_start(xin[i], slots_in[bass.ds(e * CAP, CAP), :].rearrange("(c p) d -> p c d", p=P)
                                 ).then_inc(s["xi%d" % i], 16)
                    sp.wait_ge(s["hp"], FC * (e + 1))
                    sp.dma_start(w1t[i], w1[bass.ds(e * D, D), :]).then_inc(s["wa%d" % i], 16)
                for i in range(2):
                    e = 2 * g + i
                    sp.wait_ge(s["yp"], e + 1)
                    sp.wait_ge(s["yo"], e + 1)
                    sp.dma_start(w2t[i], w2[bass.ds(e * P, P), :].rearrange("p (f d) -> p f d", d=D)).then_inc(
                        s["wb%d" % i], 16)
                    sp.dma_start(b2t[i], b2[bass.ds(e, 1), :].broadcast_to([P, D])).then_inc(s["bb%d" % i], 16)
            sp.sem_inc(s["outf"], 2)
            with sp.Fori(0, B // 2) as g:
                for i in range(2):
                    b = 2 * g + i
                    sp.wait_ge(s["fin"], b + 3)
                    sp.dma_start(out[bass.ds(b, 1), 1:S + 1, :].rearrange("o (c p) d -> p (o c) d", p=P),
                                 fin[i][:, 1:NT, :]).then_inc(s["out%d" % i], 16)
                    sp.dma_start(out[bass.ds(b, 1), 0, :], fin[i][0:1, 0, :]).then_inc(s["out%d" % i], 16)
                for i in range(2):
                    sp.wait_ge(s["out%d" % i], 32 * g + 32)
                    sp.sem_inc(s["outf"], 1)
            for i in range(2):
                sp.wait_ge(s["out%d" % i], 32 * (B // 2))

        @block.tensor
        def _(pe_):
            pe_.wait_ge(s["const"], 16 * CONSTS)
            pe_.wait_ge(s["init"], 1)
            pe_.wait_ge(s["minus"], 16 * H)
            pe_.sem_inc(s["emb"], 1)
            with pe_.Fori(0, B) as b:
                pe_.wait_ge(s["x"], 16 * b + 16)
                pe_.wait_ge(s["rr"], b + 1)
                for c in range(NC):
                    mm = pe_.matmul(m8[:, c, :], xT[:, c * P:(c + 1) * P], tokw[:, :], start=True, stop=True)
                mm.then_inc(s["emb"], 1)
                for a in range(2):
                    J = 2 * b + a
                    pe_.wait_ge(s["n"], J + 1)
                    for c in range(NC):
                        pe_.transpose(psS[:, 0, c * P:(c + 1) * P], N[:, 1 + c, :], ident[:, :])
                    pe_.transpose(xc, N[0:1, 0, :], ident[0:1, 0:1]).then_inc(s["nt"], 1)
                    pe_.wait_ge(s["nT"], J + 1)
                    for ws, col, half, done in ((wq, xq, 1, "q"), (wk, xk, 0, "k")):
                        pe_.matmul(col, ws[:, a, :], nT[:, 0, 0:1], start=True, stop=True)
                        for i in range(2):
                            mm = pe_.matmul(psS[:, half, 512 * i:512 * i + 512], ws[:, a, :],
                                            nT[:, 1 + 4 * i:5 + 4 * i, :].rearrange("p c s -> p (c s)"),
                                            start=True, stop=True)
                        mm.then_inc(s[done], 1)
                    if a == 0:
                        pe_.wait_ge(s["embr"], b + 1)
                    for c in range(NC):
                        pe_.matmul(m8[:, c, :], nT[:, 1 + c, :], wv[:, a, :], start=True, stop=True)
                    pe_.wait_ge(s["bd"], J + 1)
                    pe_.matmul(xvc, nT[:, 0, 0:1].broadcast_to([P, P]), wv[:, a, :], start=True,
                               stop=True).then_inc(s["v"], 1)
                    pe_.wait_ge(s["vt"], J + 1)
                    pe_.wait_ge(s["hi"], 2 * J + 2)
                    pe_.wait_ge(s["qkl"], 2 * J + 2)
                    for c in range(NC):
                        o = xck[:, c * H:(c + 1) * H]
                        cs = slice(c * P, (c + 1) * P)
                        pe_.matmul(o, qh[:, cs], bdh[:, 1, :], start=True, stop=False)
                        pe_.matmul(o, qh[:, cs], bdl[:, 1, :], start=False, stop=False)
                        mm = pe_.matmul(o, ql[:, cs], bdh[:, 1, :], start=False, stop=True)
                    mm.then_inc(s["ckp"], 1)
                    for i in range(2):
                        cs = slice(512 * i, 512 * i + 512)
                        o = psM[0:H, i, :]
                        pe_.matmul(o, bdh[:, 0, :], kh[:, cs], start=True, stop=False)
                        pe_.matmul(o, bdh[:, 0, :], kl[:, cs], start=False, stop=False)
                        pe_.matmul(o, bdl[:, 0, :], kh[:, cs], start=False, stop=True)
                    pe_.wait_ge(s["ck"], J + 1)
                    pe_.matmul(xcc, bd[:, 0, :], qkc[:, 1:2], start=True, stop=True).then_inc(s["cqp"], 1)
                    pe_.wait_ge(s["ce"], J + 1)
                    for c in range(NC):
                        mm = pe_.matmul(xpt[:, c * H:(c + 1) * H], pc[:, c * P:(c + 1) * P], ident[0:H, 0:H],
                                        start=True, stop=True)
                    mm.then_inc(s["ctp"], 1)
                    pe_.wait_ge(s["ct"], J + 1)
                    for c in range(NC):
                        mm = pe_.matmul(xo, pcT[:, c, :], vt[:, c, :, 0:C], start=(c == 0), stop=(c == NC - 1))
                    mm.then_inc(s["co"], 1)
                    pe_.wait_ge(s["cmk"], J + 1)
                    pe_.matmul(xct, cm[:, :], ones_f[0:H, :], start=True, stop=True).then_inc(s["ccp"], 1)

                    pe_.wait_ge(s["cc"], J + 1)
                    pe_.wait_ge(s["stk"], STK * (J + 1))

                    def maxima(h, c):
                        for i in range(2):
                            u = U_HEAD * h + 2 * c + i
                            if u >= 2:
                                pe_.wait_ge(s["p1u"], J * (U_HEAD * H) + u - 1)
                            pe_.matmul(psM[:, i, :], qst[:, h // 2, c * P:(c + 1) * P],
                                       kst[:, h, 512 * i:512 * i + 512],
                                       start=True, stop=True).then_inc(s["p1"], 1)

                    def turn_maxima(h):
                        pe_.wait_ge(s["mr"], J * H + h + 1)
                        if h >= 4:
                            pe_.wait_ge(s["u"], J * H + h - 3)
                        pe_.transpose(xm, mr[:, h, :].bitcast(F32), ident[:, :]).then_inc(s["mtp"], 1)

                    def scores(h, c):
                        t = NC * h + c
                        if c == 0 and h % 2 == 0:
                            for i in range(2):
                                pe_.wait_ge(s["mrow%d" % i], 16 * (J * (H // 2) + h // 2 + 1))
                        if t >= 2:
                            pe_.wait_ge(s["exp"], J * T_ATT + t - 1)
                        for i in range(2):
                            mm = pe_.matmul(psS[:, t % 2, 512 * i:512 * i + 512],
                                            kst[:, h, c * P:(c + 1) * P],
                                            qst[:, h // 2, 512 * i:512 * i + 512],
                                            start=True, stop=True)
                        mm.then_inc(s["p2"], 1)

                    def values(h, c):
                        t = NC * h + c
                        pe_.wait_ge(s["exp"], J * T_ATT + t + 1)
                        if c == 0 and h >= 1:
                            pe_.wait_ge(s["avs"], J * H + h)
                        for j in range(4):
                            mm = pe_.matmul(psV[32 * j:32 * j + 32, 0:256], vt[:, c, h, :],
                                            pr[:, t % 4, 256 * j:256 * j + 256],
                                            start=(c == 0), stop=(c == NC - 1))
                        mm.then_inc(s["av"], 1)

                    def turn_values(h):
                        pe_.wait_ge(s["avs"], J * H + h + 1)
                        if h + 3 < H:
                            pe_.wait_ge(s["mT"], J * H + h + 4)
                        else:
                            pe_.wait_ge(s["u"], J * H + h)
                        pe_.transpose(xav[:, 0:P], avs[:, h % 2, 0:P], ident[:, :])
                        pe_.transpose(xav[:, P:2 * P], avs[:, h % 2, P:2 * P], ident[:, :]).then_inc(s["avt"], 1)

                    for c in range(NC):
                        maxima(0, c)
                    turn_maxima(0)
                    for c in range(NC):
                        maxima(1, c)
                    turn_maxima(1)
                    for c in range(NC):
                        maxima(2, c)
                    for h in range(H):
                        for c in range(NC):
                            if h + 3 < H:
                                maxima(h + 3, c)
                            scores(h, c)
                            if c >= 1:
                                values(h, c - 1)
                            elif h >= 1:
                                values(h - 1, NC - 1)
                            if c == 1 and h + 2 < H:
                                turn_maxima(h + 2)
                            if c == 3 and h >= 1:
                                turn_values(h - 1)
                    values(H - 1, NC - 1)
                    turn_values(H - 1)
                    pe_.wait_ge(s["ctx"], J + 1)
                    for c in range(NC):
                        mm = pe_.transpose(psS[:, 0, c * P:(c + 1) * P],
                                           U[:, c, :, :].rearrange("p h c -> p (h c)"), ident[:, :])
                    mm.then_inc(s["cxp"], 1)
                    pe_.wait_ge(s["cxT"], J + 1)
                    pe_.matmul(xpr, ctxT[:, 0, 0:1], wo[:, a, :], start=True, stop=True)
                    for c in range(NC):
                        mm = pe_.matmul(m8[:, c, :], ctxT[:, 1 + c, :], wo[:, a, :], start=True, stop=True)
                    mm.then_inc(s["o"], 1)
                pe_.wait_ge(s["x2"], b + 1)
                pe_.transpose(xn9, x2[:, 0, :], ident[:, :])
                for c in range(NC):
                    mm = pe_.transpose(psS[:, 1, c * P:(c + 1) * P], x2[:, 1 + c, :], ident[:, :])
                mm.then_inc(s["x2p"], 1)
                pe_.wait_ge(s["x2T"], b + 1)
                pe_.matmul(xlg, nT[:, 0, :], wrt[:, :], start=True, stop=True)
                for c in range(NC):
                    mm = pe_.matmul(psM[:, 0, c * E:(c + 1) * E], nT[:, 1 + c, :], wrt[:, :], start=True, stop=True)
                mm.then_inc(s["lgp"], 1)
                pe_.wait_ge(s["oh"], b + 1)
                for c in range(NT):
                    o = xps if c == 0 else psM[:, 1, (c - 1) * E:c * E]
                    pe_.matmul(o, lower[:, :], ohs[:, c, :], start=True, stop=False)
                    mm = pe_.matmul(o, ones_bf[:, :], run[:, c, :], start=False, stop=True)
                mm.then_inc(s["pos"], 1)
            pe_.wait_ge(s["rr"], B + 1)

            pe_.sem_inc(s["hp"], 2 * FC)
            pe_.sem_inc(s["tp"], 2)
            pe_.sem_inc(s["yp"], 2)

            def turn_slots(e, g, i):
                pe_.wait_ge(s["xi%d" % i], 16 * g + 16)
                pe_.wait_ge(s["xt"], e + 1)
                for c in range(SC):
                    mm = pe_.transpose(psX[:, c * P:(c + 1) * P], xin[i][:, c, :], ident[:, :])
                mm.then_inc(s["tp"], 1)

            def up(e, g, i):
                pe_.wait_ge(s["xt"], e + 2)
                pe_.wait_ge(s["wa%d" % i], 16 * g + 16)
                for f in range(FC):
                    pe_.wait_ge(s["gl"], FC * e + f + 1)
                    pe_.matmul(psS[:, f // 2, 512 * (f % 2):512 * (f % 2) + 512], w1t[i][:, f:F:FC], xinT[i],
                               start=True, stop=True).then_inc(s["hp"], 1)

            def down(e, g, i):
                pe_.wait_ge(s["gl"], FC * (e + 2))
                pe_.wait_ge(s["wb%d" % i], 16 * g + 16)
                pe_.wait_ge(s["yo"], e + 1)
                for c in range(SC):
                    for f in range(FC):
                        mm = pe_.matmul(psM[:, i, c * P:(c + 1) * P], hid[i][:, f, c * P:(c + 1) * P],
                                        w2t[i][:, f, :], start=(f == 0), stop=(f == FC - 1))
                mm.then_inc(s["yp"], 1)

            with pe_.Fori(0, E // 2) as g:
                turn_slots(2 * g, g, 0)
                up(2 * g, g, 0)
                turn_slots(2 * g + 1, g, 1)
                up(2 * g + 1, g, 1)
                down(2 * g, g, 0)
                down(2 * g + 1, g, 1)

        @block.scalar
        def _(act):
            act.wait_ge(s["const"], 16 * CONSTS)
            with act.Fori(0, B) as b:
                for a in range(2):
                    J = 2 * b + a
                    act.wait_ge(s["nt"], J + 1)
                    for dst, src in ((nT[:, 0, 0:1], xc), (nT[:, 1:NT, :].rearrange("p c s -> p (c s)"), psS[:, 0, :])):
                        if a == 0:
                            ins = act.activation(dst, src, ACT.Copy)
                        else:
                            ins = act.activation(dst, src, ACT.Identity, bias=c1[:, 0:1], scale=g1[:, 0:1])
                    ins.then_inc(s["nT"], 1)
                    act.wait_ge(s["q"], J + 1)
                    act.activation(qh[:, :], psS[:, 1, :], ACT.Identity,
                                   bias=bq[:, 0:1] if a == 0 else 0.0).then_inc(s["hi"], 1)
                    act.wait_ge(s["k"], J + 1)
                    act.activation(kh[:, :], psS[:, 0, :], ACT.Identity,
                                   bias=bk[:, 0:1] if a == 0 else 0.0).then_inc(s["hi"], 1)
                    act.wait_ge(s["cm"], J + 1)
                    act.activation(csc[:, 4:5], csc[:, 0:1], ACT.Exp, bias=csc[:, 2:3], scale=SCALE)
                    act.activation(pc[:, :], psM[0:H, :, :].rearrange("h i s -> h (i s)"), ACT.Exp,
                                   bias=csc[:, 2:3], scale=SCALE, accum_out=csc[:, 3:4]).then_inc(s["ce"], 1)
                    for t in range(T_ATT):
                        act.wait_ge(s["p2"], J * T_ATT + t + 1)
                        if t >= 4:
                            act.wait_ge(s["av"], J * T_ATT + t - 3)
                        act.activation(pr[:, t % 4, :], psS[:, t % 2, :], ACT.Exp, scale=SCALE).then_inc(s["exp"], 1)
                    act.wait_ge(s["pd"], J + 1)
                    act.activation(pck[:, :, :], pck[:, :, :], ACT.Exp, scale=SCALE).then_inc(s["pe"], 1)
                    act.wait_ge(s["cxp"], J + 1)
                    act.activation(ctxT[:, 1:NT, :].rearrange("p c s -> p (c s)"), psS[:, 0, :],
                                   ACT.Copy).then_inc(s["cxT"], 1)
                act.wait_ge(s["x2p"], b + 1)
                act.activation(nT[:, 0, :], xn9, ACT.Copy)
                act.activation(nT[:, 1:NT, :].rearrange("p c s -> p (c s)"), psS[:, 1, :],
                               ACT.Copy).then_inc(s["x2T"], 1)
                act.wait_ge(s["gd"], b + 1)
                act.activation(rt[:, 1, :], rt[:, 0, :], ACT.Exp).then_inc(s["ge"], 1)
            act.sem_inc(s["gl"], FC)
            with act.Fori(0, E // 2) as g:
                for i in range(2):
                    e = 2 * g + i
                    act.wait_ge(s["yp"], e + 1)
                    for f in range(FC):
                        act.wait_ge(s["hp"], FC * (e + 2) + f + 1)
                        act.activation(hid[i][:, f, :], psS[:, f // 2, 512 * (f % 2):512 * (f % 2) + 512],
                                       ACT.Gelu_apprx_tanh, bias=b1t[:, f, bass.ds(e, 1)]).then_inc(s["gl"], 1)

        @block.vector
        def _(dve):
            linked = [0, 0]

            def link(ins):
                linked[0] += 1
                ins.then_inc(s["chain"], 1)
                dve.wait_ge(s["chain"], linked[1] + linked[0])

            def norm(src, dst):
                for c in range(NT):
                    ins = dve.bn_stats(st[:, c, :], src[:, c, :])
                link(ins)
                v = [sm[:, i, :] for i in range(8)]
                dve.tensor_tensor(v[0], st[:, :, 1], st[:, :, 4], ALU.add)
                dve.tensor_tensor(v[1], st[:, :, 1], st[:, :, 4], ALU.subtract)
                link(dve.tensor_tensor(v[2], st[:, :, 2], st[:, :, 5], ALU.add))
                dve.tensor_scalar(v[6], v[0], 0.5, None, ALU.mult)
                link(dve.tensor_tensor(v[3], v[1], v[1], ALU.mult))
                link(dve.scalar_tensor_tensor(v[5], v[3], D / 4.0, v[2], ALU.mult, ALU.add))
                link(dve.tensor_scalar(v[2], v[5], 1.0 / D, EPS, ALU.mult, ALU.add))
                link(dve.tensor_scalar(smi[:, :], v[2].bitcast(I32), 1, None, ALU.logical_shift_right))
                link(dve.tensor_scalar(v[4].bitcast(I32), smi[:, :], -1.0, float(RSQRT_GUESS), ALU.mult, ALU.add))
                for _ in range(4):
                    link(dve.tensor_tensor(v[5], v[4], v[4], ALU.mult))
                    link(dve.tensor_tensor(v[7], v[5], v[2], ALU.mult))
                    link(dve.tensor_scalar(v[5], v[7], -0.5, 1.5, ALU.mult, ALU.add))
                    link(dve.tensor_tensor(v[4], v[4], v[5], ALU.mult))
                for c in range(NT):
                    ins = dve.tensor_scalar(dst[:, c, :], src[:, c, :], sm[:, 6, c:c + 1], sm[:, 4, c:c + 1],
                                            ALU.subtract, ALU.mult)
                return ins

            dve.memset(N[:, :, :], 0.0)
            dve.memset(clst[:, :], 0.0).then_inc(s["clear"], 1)
            dve.memset(ones_bf[:, :], 1.0)
            dve.memset(ones_f[:, :], 1.0)
            dve.memset(run[:, :, :], 0.0)
            dve.memset(vt[:, :, :, :], 0.0).then_inc(s["clear"], 1)
            dve.wait_ge(s["clear"], 2)
            dve.memset(vt[:, :, :, C:C + 1], 1.0)
            dve.memset(nT[:, 0, :], 0.0)
            dve.memset(ctxT[:, 0, :], 0.0)
            dve.memset(zrow[:, :], 0.0)
            dve.memset(mT[:, :, :].bitcast(F32), -1.0)
            dve.memset(qst[:, :, :].bitcast(F32), 0.0)
            dve.memset(kst[:, :, :].bitcast(F32), 0.0).then_inc(s["init"], 1)
            dve.wait_ge(s["const"], 16 * CONSTS)
            dve.wait_ge(s["cls"], 16)
            dve.wait_ge(s["minus"], 16 * H)
            dve.wait_ge(s["zeroed"], 16 * E)
            dve.sem_inc(s["rr"], 1)
            with dve.Fori(0, B) as b:
                linked[0], linked[1] = 0, b * CHAIN
                dve.wait_ge(s["emb"], b + 2)
                dve.tensor_copy(hb[:, 0, :], clst[:, :])
                link(dve.tensor_tensor(hb[:, 1:NT, :], m8, pe_t[:, :, :], ALU.add))
                dve.sem_inc(s["embr"], 1)
                for a in range(2):
                    J = 2 * b + a
                    if a == 0:
                        norm(hb, N).then_inc(s["n"], 1)
                        dve.wait_ge(s["n"], J + 1)
                        link(dve.tensor_tensor(hb[:, :, :], hb[:, :, :],
                                               bo[:, :].unsqueeze(1).broadcast_to([P, NT, D]), ALU.add))
                    else:
                        link(norm(hb, G))
                        norm(G, N).then_inc(s["n"], 1)
                    dve.wait_ge(s["q"], J + 1)
                    dve.wait_ge(s["hi"], 2 * J + 1)
                    dve.scalar_tensor_tensor(ql[:, :], psS[:, 1, :], bq[:, 0:1] if a == 0 else 0.0,
                                             qh[:, :].bitcast(F32), ALU.add, ALU.subtract).then_inc(s["qkl"], 1)
                    dve.wait_ge(s["k"], J + 1)
                    dve.tensor_scalar(qkc[:, 0:1], xq, bq[:, 0:1] if a == 0 else 0.0, None, ALU.add)
                    link(dve.tensor_scalar(qkc[:, 1:2], xk, bk[:, 0:1] if a == 0 else 0.0, None, ALU.add))
                    dve.tensor_scalar(bd[:, 0, :], headmask[:, :], qkc[:, 0:1], None, ALU.mult)
                    link(dve.tensor_scalar(bd[:, 1, :], headmask[:, :], qkc[:, 1:2], None, ALU.mult))
                    link(dve.tensor_copy(bdh[:, :, :], bd[:, :, :]))
                    dve.tensor_tensor(bdl[:, :, :], bd[:, :, :], bdh[:, :, :].bitcast(F32),
                                      ALU.subtract).then_inc(s["bd"], 1)
                    dve.wait_ge(s["hi"], 2 * J + 2)
                    dve.scalar_tensor_tensor(kl[:, :], psS[:, 0, :], bk[:, 0:1] if a == 0 else 0.0,
                                             kh[:, :].bitcast(F32), ALU.add, ALU.subtract).then_inc(s["qkl"], 1)
                    dve.wait_ge(s["v"], J + 1)
                    mv4 = m8.rearrange("p c (h e) -> p c h e", h=H)
                    if a == 0:
                        dve.tensor_tensor(vcb[:, :], xvc, bv[:, :], ALU.add)
                        for c in range(NC):
                            ins = dve.tensor_tensor(vt[:, c, :, 0:C], mv4[:, c], bv[:, :].rearrange(
                                "p (h e) -> p h e", h=H), ALU.add)
                    else:
                        dve.tensor_copy(vcb[:, :], xvc)
                        ins = dve.tensor_copy(vt[:, :, :, 0:C], mv4)
                    ins.then_inc(s["vt"], 1)
                    dve.wait_ge(s["ckp"], J + 1)
                    dve.tensor_copy(mxu[:, :, :, 2], xck.rearrange("p (c h) -> p h c", h=H)).then_inc(s["ck"], 1)
                    dve.wait_ge(s["cqp"], J + 1)
                    dve.tensor_copy(csc[:, 0:1], xcc)
                    link(dve.tensor_reduce(csc[:, 1:2], psM[0:H, :, :].rearrange("h i s -> h (i s)"), AX_X, ALU.max))
                    link(dve.tensor_tensor(csc[:, 5:6], csc[:, 1:2], csc[:, 0:1], ALU.max))
                    dve.tensor_scalar(csc[:, 2:3], csc[:, 5:6], -SCALE, None, ALU.mult).then_inc(s["cm"], 1)
                    dve.wait_ge(s["ce"], J + 1)
                    link(dve.tensor_tensor(csc[:, 6:7], csc[:, 3:4], csc[:, 4:5], ALU.add))
                    dve.reciprocal(csc[:, 7:8], csc[:, 6:7])
                    dve.wait_ge(s["ctp"], J + 1)
                    dve.tensor_copy(pcT[:, :, :], xpt.rearrange("p (c h) -> p c h", h=H)).then_inc(s["ct"], 1)
                    dve.wait_ge(s["co"], J + 1)
                    link(dve.scalar_tensor_tensor(cm[:, :], vcb[0:H, :], csc[:, 4:5], xo, ALU.mult, ALU.add))
                    dve.scalar_tensor_tensor(cm[:, :], cm[:, :], csc[:, 7:8], headmaskT[:, :], ALU.mult,
                                             ALU.mult).then_inc(s["cmk"], 1)
                    dve.wait_ge(s["ccp"], J + 1)
                    dve.tensor_copy(ctxT[:, 0, 0:1], xct).then_inc(s["cc"], 1)

                    def maxima(h, c):
                        for i in range(2):
                            u = U_HEAD * h + 2 * c + i
                            dve.wait_ge(s["p1"], J * (U_HEAD * H) + u + 1)
                            ins = dve.tensor_reduce(mxu[:, h, c, i:i + 1], psM[:, i, :], AX_X, ALU.max)
                            ins.then_inc(s["p1u"], 1)
                        if c == NC - 1:
                            dve.wait_ge(s["p1u"], J * (U_HEAD * H) + u + 1)
                            dve.tensor_reduce(mr[:, h, :], mxu[:, h, :, :], AX_X, ALU.max).then_inc(s["mr"], 1)

                    def turn_maxima(h):
                        dve.wait_ge(s["mtp"], J * H + h + 1)
                        if h >= 2:
                            dve.wait_ge(s["mrow%d" % (h % 2)], 16 * (J * (H // 2) + h // 2))
                        dve.tensor_copy(mT[:, h % 2, :], xm).then_inc(s["mT"], 1)

                    def take_values(h):
                        dve.wait_ge(s["av"], J * T_ATT + NC * (h + 1))
                        dve.tensor_copy(avs[:, h % 2, :], psV[:, 0:256]).then_inc(s["avs"], 1)

                    def split_values(h):
                        dve.wait_ge(s["avt"], J * H + h + 1)
                        v4 = xav.rearrange("p (i j e) -> p j i e", i=2, j=4)
                        dve.tensor_copy(U[:, :, h, :].rearrange("p (j i) e -> p j i e", i=2), v4[:, :, :, 0:C])
                        dve.tensor_copy(den[:, :, h].rearrange("p (j i) -> p j i", i=2),
                                        v4[:, :, :, C]).then_inc(s["u"], 1)

                    for c in range(NC):
                        maxima(0, c)
                    turn_maxima(0)
                    for c in range(NC):
                        maxima(1, c)
                    turn_maxima(1)
                    for c in range(NC):
                        maxima(2, c)
                    for h in range(H):
                        for c in range(NC):
                            if h + 3 < H:
                                maxima(h + 3, c)
                            if c == 1 and h + 2 < H:
                                turn_maxima(h + 2)
                            if c == 0 and h >= 1:
                                take_values(h - 1)
                            if c == 3 and h >= 1:
                                split_values(h - 1)
                    take_values(H - 1)
                    dve.tensor_tensor(pck[:, :, :], mxu[:, :, :, 2], mr[:, :, :].bitcast(F32),
                                      ALU.subtract).then_inc(s["pd"], 1)
                    split_values(H - 1)
                    dve.wait_ge(s["pe"], J + 1)
                    dve.wait_ge(s["u"], J * H + H)
                    dve.tensor_tensor(den[:, :, :], den[:, :, :], pck[:, :, :].rearrange("p h c -> p c h"), ALU.add)
                    for c in range(NC):
                        ins = dve.tensor_tensor(Ut[:, c, :, :], vcb[:, :].rearrange("p (h e) -> p h e", h=H),
                                                pck[:, :, c].unsqueeze(2).broadcast_to([P, H, C]), ALU.mult)
                    link(ins)
                    dve.tensor_tensor(U[:, :, :, :], U[:, :, :, :], Ut[:, :, :, :], ALU.add)
                    link(dve.reciprocal(den[:, :, :], den[:, :, :]))
                    dve.tensor_tensor(U[:, :, :, :].rearrange("p c h e -> p (c h) e"),
                                      U[:, :, :, :].rearrange("p c h e -> p (c h) e"),
                                      den[:, :, :].rearrange("p c h -> p (c h)").unsqueeze(2).broadcast_to(
                                          [P, NC * H, C]), ALU.mult).then_inc(s["ctx"], 1)
                    dve.wait_ge(s["o"], J + 1)
                    t = hb if a == 0 else G
                    dve.tensor_tensor(t[0:1, 0, :], xpr, t[0:1, 0, :], ALU.add)
                    link(dve.tensor_tensor(t[:, 1:NT, :], m8, t[:, 1:NT, :], ALU.add))
                dve.tensor_tensor(res[:, bass.ds(b, 1), :, :].rearrange("p o c d -> p (o c) d"), hb[:, :, :],
                                  G[:, :, :], ALU.add)
                link(norm(G, N))
                dve.wait_ge(s["x2f"], b + 1)
                link(dve.tensor_tensor(x2[:, :, :], N[:, :, :], g2[:, :].unsqueeze(1).broadcast_to([P, NT, D]),
                                       ALU.mult))
                dve.tensor_tensor(x2[:, :, :], x2[:, :, :], c2[:, :].unsqueeze(1).broadcast_to([P, NT, D]),
                                  ALU.add).then_inc(s["x2"], 1)
                dve.wait_ge(s["lgp"], b + 1)
                dve.tensor_copy(lg[:, 0, :], xlg)
                link(dve.tensor_copy(lg[:, 1:NT, :], psM[:, 0, :].rearrange("p (c e) -> p c e", e=E)))
                dve.tensor_copy(run[:, 0, :], run[:, NT, :])
                for c in range(NT):
                    ins = dve.max(mv[:, c, :], lg[:, c, :])
                link(ins)
                dve.tensor_tensor(rt[:, 0, :], mv[:, :, 1], mv[:, :, 0], ALU.subtract).then_inc(s["gd"], 1)
                for c in range(NT):
                    ins = dve.max_index(mi[:, c, :], mv[:, c, :], lg[:, c, :])
                link(ins)
                for k in range(TOPK):
                    ins = dve.scalar_tensor_tensor(e1[:, k, :], mi[:, :, k], 1.0, valid[:, :], ALU.add, ALU.mult)
                link(ins)
                for k in range(TOPK):
                    ins = dve.tensor_tensor(oh[:, k, :, :], iota1[:, :].unsqueeze(1).broadcast_to([P, NT, E]),
                                            e1[:, k, :].unsqueeze(2).broadcast_to([P, NT, E]), ALU.is_equal)
                link(ins)
                link(dve.tensor_tensor(ohs[:, :, :], oh[:, 0, :, :], oh[:, 1, :, :], ALU.add))
                for c in range(NT):
                    link(dve.tensor_tensor(run[:, c + 1, :], run[:, c, :], ohs[:, c, :], ALU.add))
                dve.sem_inc(s["oh"], 1)
                dve.wait_ge(s["pos"], b + 1)
                dve.tensor_copy(pos[:, 0, :], xps)
                link(dve.tensor_copy(pos[:, 1:NT, :], psM[:, 1, :].rearrange("p (c e) -> p c e", e=E)))
                dve.sem_inc(s["rr"], 1)
                for k in range(TOPK):
                    ins = dve.tensor_tensor(oh[:, k, :, :], oh[:, k, :, :], pos[:, :, :], ALU.mult)
                link(ins)
                link(dve.tensor_reduce(pk[:, :, :], oh[:, :, :, :], AX_X, ALU.add))
                link(dve.tensor_scalar(keep[:, :, :], pk[:, :, :], float(CAP), None, ALU.is_lt))
                for k in range(TOPK):
                    dve.tensor_tensor(rt[:, 2 + k, :], keep[:, k, :], valid[:, :], ALU.mult)
                    dve.scalar_tensor_tensor(rt[:, 4 + k, :], e1[:, k, :], float(CAP), pk[:, k, :], ALU.mult, ALU.add)
                    ins = dve.tensor_scalar(rt[:, 6 + k, :], pk[:, k, :], float(CAP - 1), None, ALU.min)
                link(ins)
                for k in range(TOPK):
                    dve.tensor_scalar(rt[:, 8 + k, :], rt[:, 2 + k, :], -OUT_OF_BOUNDS, OUT_OF_BOUNDS - CAP, ALU.mult,
                                      ALU.add)
                    ins = dve.scalar_tensor_tensor(rt[:, 10 + k, :], e1[:, k, :], float(CAP), rt[:, 6 + k, :],
                                                   ALU.mult, ALU.add)
                link(ins)
                for k in range(TOPK):
                    dve.tensor_tensor(sidx[:, :, k], rt[:, 4 + k, :], rt[:, 8 + k, :], ALU.add)
                    ins = dve.tensor_scalar(gidx[:, bass.ds(b, 1), :, k].rearrange("p o c -> p (o c)"),
                                            rt[:, 10 + k, :], -float(CAP), 0.0, ALU.add, ALU.max)
                ins.then_inc(s["sidx"], 1)
                dve.wait_ge(s["ge"], b + 1)
                link(dve.tensor_scalar(rt[:, 2, :], rt[:, 1, :], 1.0, None, ALU.add))
                link(dve.reciprocal(rt[:, 3, :], rt[:, 2, :]))
                link(dve.tensor_tensor(rt[:, 4, :], rt[:, 3, :], rt[:, 1, :], ALU.mult))
                for k in range(TOPK):
                    ins = dve.tensor_tensor(gate[:, bass.ds(b, 1), :, k].rearrange("p o c -> p (o c)"),
                                            rt[:, 3 + k, :], keep[:, k, :], ALU.mult)
                link(ins)
            assert linked[0] == CHAIN, linked
            dve.sem_inc(s["yo"], 2)
            dve.sem_inc(s["xt"], 1)
            with dve.Fori(0, E // 2) as g:
                for i in range(2):
                    e = 2 * g + i
                    dve.wait_ge(s["tp"], e + 3)
                    dve.wait_ge(s["hp"], FC * (e + 1))
                    dve.tensor_copy(xinT[i], psX[:, :]).then_inc(s["xt"], 1)
                for i in range(2):
                    e = 2 * g + i
                    dve.wait_ge(s["yp"], e + 3)
                    dve.wait_ge(s["bb%d" % i], 16 * g + 16)
                    dve.wait_ge(s["ysf"], e + 1)
                    dve.tensor_tensor(yout[i], psM[:, i, :].rearrange("p (c d) -> p c d", d=D),
                                      b2t[i].unsqueeze(1).broadcast_to([P, SC, D]), ALU.add).then_inc(s["yo"], 1)
            dve.sem_inc(s["fin"], 2)
            dve.wait_ge(s["yst0"], 16 * (E // 2))
            dve.wait_ge(s["yst1"], 16 * (E // 2))
            with dve.Fori(0, B // 2) as g:
                for i in range(2):
                    b = 2 * g + i
                    dve.wait_ge(s["fin"], 2 * g + 2)
                    dve.tensor_copy(gi[:, i, :, :], gidx[:, bass.ds(b, 1), :, :].rearrange("p o c k -> p (o c) k"))
                    dve.tensor_copy(gg[:, i, :, :], gate[:, bass.ds(b, 1), :, :].rearrange("p o c k -> p (o c) k")
                                    ).then_inc(s["gi"], 1)
                for i in range(2):
                    b = 2 * g + i
                    dve.wait_ge(s["gi"], b + 1)
                    dve.wait_ge(s["ga%d" % i], 16 * NT * TOPK * (g + 1))
                    dve.wait_ge(s["outf"], 2 * g + 2)
                    for c in range(NT):
                        ins = dve.scalar_tensor_tensor(
                            fin[i][:, c, :], rows[2 * i][:, c, :], gg[:, i, c, 0:1],
                            res[:, bass.ds(b, 1), c, :].rearrange("p o d -> p (o d)"), ALU.mult, ALU.add)
                    ins.then_inc(s["done"], 1)
                    dve.wait_ge(s["done"], b + 1)
                    for c in range(NT):
                        ins = dve.scalar_tensor_tensor(fin[i][:, c, :], rows[2 * i + 1][:, c, :], gg[:, i, c, 1:2],
                                                       fin[i][:, c, :], ALU.mult, ALU.add)
                    ins.then_inc(s["fin"], 1)

        @block.gpsimd
        def _(pool):
            pool.wait_ge(s["zeroed"], 16 * E)
            pool.memset(tick[:, :], 0.0).then_inc(s["tick"], 1)
            pool.wait_ge(s["tick"], 1)
            pool.sem_inc(s["x2f"], 1)
            pool.sem_inc(s["ysf"], 2)
            last_slot = pool.to_reg(SLOTS - 1)
            with pool.Fori(0, B) as b:
                pool.wait_ge(s["sidx"], b + 1)
                pool.wait_ge(s["tick"], b + 1)
                pool.tensor_tensor(tick[:, :], tick[:, :], tick[:, :], ALU.mult).then_inc(s["tick"], 1)
                for c in range(NT):
                    for k in range(TOPK):
                        pool.indirect_dma_start(
                            out=slots_in, out_offset=bass.IndirectOffsetOnAxis(ap=sidx[:, c, k:k + 1], axis=0),
                            in_=x2[:, c, :], in_offset=None, bounds_check=last_slot,
                            oob_is_err=False).then_inc(s["scat"], 16)
                pool.wait_ge(s["scat"], 16 * NT * TOPK * b + 16 * NT * TOPK)
                pool.sem_inc(s["x2f"], 1)
            with pool.Fori(0, E // 2) as g:
                for i in range(2):
                    e = 2 * g + i
                    pool.wait_ge(s["yo"], e + 3)
                    pool.dma_start(slots_out[bass.ds(e * CAP, CAP), :].rearrange("(c p) d -> p c d", p=P),
                                   yout[i]).then_inc(s["yst%d" % i], 16)
                for i in range(2):
                    pool.wait_ge(s["yst%d" % i], 16 * g + 16)
                    pool.sem_inc(s["ysf"], 1)
            pool.wait_ge(s["yst0"], 16 * (E // 2))
            pool.wait_ge(s["yst1"], 16 * (E // 2))
            with pool.Fori(0, B // 2) as g:
                for i in range(2):
                    b = 2 * g + i
                    pool.wait_ge(s["gi"], b + 1)
                    pool.wait_ge(s["fin"], 2 * g + 2)
                    pool.wait_ge(s["tick"], B + 1 + b)
                    pool.tensor_tensor(tick[:, :], tick[:, :], tick[:, :], ALU.mult).then_inc(s["tick"], 1)
                    for c in range(NT):
                        for k in range(TOPK):
                            pool.indirect_dma_start(
                                out=rows[2 * i + k][:, c, :], out_offset=None, in_=slots_out,
                                in_offset=bass.IndirectOffsetOnAxis(ap=gi[:, i, c, k:k + 1], axis=0),
                                bounds_check=last_slot, oob_is_err=False).then_inc(s["ga%d" % i], 16)


def position_encoding():
    import math
    position = np.arange(2 * S, dtype=np.float32)[:, None]
    div_term = np.exp(np.arange(0, D, 2, dtype=np.float32) * (-math.log(10000.0) / D))
    pe = np.zeros((2 * S, D), dtype=np.float32)
    pe[:, 0::2] = np.sin(position * div_term)
    pe[:, 1::2] = np.cos(position * div_term)
    return pe[:S]


def kernel(**inputs):
    import ml_dtypes
    import concourse.bacc as bacc
    from concourse.bass_utils import run_bass_kernel_spmd

    i = {k: np.asarray(v) for k, v in inputs.items()}

    def row(a):
        return a.reshape(1, -1)

    def col(a):
        return a.reshape(-1, 1)

    wqkv = i["L0_attn_qkv_w"].reshape(H, 3, C, D)
    bqkv = i["L0_attn_qkv_b"].reshape(H, 3, C)
    arrays = {
        "x": i["x"].reshape(B * S, F_IN).T,
        "cls_tok": i["cls_tok"].reshape(1, D),
        "pe": position_encoding().reshape(NC, P, D).transpose(1, 0, 2),
        "tokW": i["L0_tok_W"],
        "wq1": wqkv[:, 0].reshape(D, D).T, "wk1": wqkv[:, 1].reshape(D, D).T, "wv1": wqkv[:, 2].reshape(D, D).T,
        "bq1": col(bqkv[:, 0]), "bk1": col(bqkv[:, 1]), "bv1": row(bqkv[:, 2]),
        "wo1": i["L0_attn_out_w"].T, "bo1": row(i["L0_attn_out_b"]),
        "ln1g": col(i["L0_ffn_ln1_g"]), "ln1b": col(i["L0_ffn_ln1_b"]),
        "wq2": i["L0_ffn_wq"], "wk2": i["L0_ffn_wk"], "wv2": i["L0_ffn_wv"], "wo2": i["L0_ffn_wo"],
        "ln2g": row(i["L0_ffn_ln2_g"]), "ln2b": row(i["L0_ffn_ln2_b"]),
        "wr": i["L0_ffn_wr"],
        "w1": i["L0_ffn_w1"].reshape(E * D, F),
        "b1": i["L0_ffn_b1"].reshape(E, P, FC).transpose(1, 2, 0),
        "w2": i["L0_ffn_w2"].reshape(E * P, FC * D),
        "b2": i["L0_ffn_b2"],
        "ident_d": np.eye(P, dtype=np.float32),
        "headmask_d": np.repeat(np.eye(H, dtype=np.float32), C, axis=0),
        "headmaskT_d": np.repeat(np.eye(H, dtype=np.float32), C, axis=1),
        "lower_d": np.triu(np.ones((P, P), dtype=np.float32), 1).astype(ml_dtypes.bfloat16),
        "iota_d": np.tile(np.arange(1, E + 1, dtype=np.float32), (P, 1)),
        "valid_d": np.concatenate([np.eye(P, 1, dtype=np.float32), np.ones((P, NC), np.float32)], axis=1),
    }
    nc = bacc.Bacc("TRN2", target_bir_lowering=False, num_devices=1)
    named, args = {}, {}
    for name, a in arrays.items():
        a = np.ascontiguousarray(a)
        named["in_" + name] = a
        args[name] = nc.dram_tensor("in_" + name, a.shape, mybir.dt.from_np(a.dtype), kind="ExternalInput").ap()
    args["out"] = nc.dram_tensor("out_0", (B, S + 1, D), F32, kind="ExternalOutput").ap()
    build(nc, **args)
    r = run_bass_kernel_spmd(nc, [named], core_ids=[0])
    return r.results[0]["out_0"]
```

```python
from contextlib import ExitStack

import numpy as np

import concourse.bass as bass
from concourse import mybir

ALU = mybir.AluOpType
ACT = mybir.ActivationFunctionType
AX_X = mybir.AxisListType.X
F32 = mybir.dt.float32
F32R = mybir.dt.float32r
BF16 = mybir.dt.bfloat16
I32 = mybir.dt.int32
U32 = mybir.dt.uint32

P = 128
D = 128
H = 8
C = D // H
B = 8
S = 1024
NC = S // P
NT = NC + 1
F_IN = 29
E = 64
F = 512
FC = F // P
TOPK = 2
CAP = 2 * (B * (S + 1) * TOPK // E)
SLOTS = E * CAP
SC = CAP // P
EPS = 1e-5
SCALE = 1.0 / C ** 0.5


def later(n):
    return not (isinstance(n, int) and n == 0)

OUT_OF_BOUNDS = float(1 << 20)
HALF = 64
GRP = 3 * C

STEP = {
    "tv7": 2, "ctxa": 3, "ctxb": 4, "ct0": 4, "ct1": 5, "oc": 6, "o0": 7, "o1": 8,
    "stat0a": 8, "stat0b": 9, "stat0c": 10, "norm0a": 14, "norm0b": 15, "norm0c": 16,
    "e0": 14, "e1": 15, "stat1a": 16, "stat1b": 17, "stat1c": 18, "norm1a": 22, "norm1b": 23, "norm1c": 24,
    "nt0": 24, "nt1": 26, "q0": 28, "q1": 29, "k0": 31, "k1": 32, "ntc": 34, "qc": 36, "ck": 37,
    "v0": 38, "v1": 39, "vc": 40,
    "cq0": 42, "cq1": 44, "cc": 45, "cmax": 46, "cexp": 48, "pt": 53, "co": 55, "cf": 58,
    "xa": 46, "xb": 47, "xc": 48, "lga": 50, "lgb": 52, "rmax": 53, "rexp": 56, "ridx": 54, "re": 55, "roh": 55,
    "rohs": 56, "posa": 60, "posb": 61, "rpk": 61, "rred": 62, "rout": 62,
}
FINISH = ("tv7", "ct0", "ct1", "oc", "o0", "o1")
EMBED = ("e0", "e1")
PREPARE = ("nt0", "nt1", "q0", "q1", "k0", "k1", "ntc", "qc", "ck", "v0", "v1", "vc",
           "cq0", "cq1", "cc", "pt", "co", "cf")
ROUTE = ("xa", "xb", "xc", "lga", "lgb", "posa", "posb")


def turns(k, prev, nxt):
    names = []
    if prev:
        names += FINISH + (ROUTE if k in (3, 0) else ())
    if nxt:
        names += (EMBED if k in (3, 0) else ()) + PREPARE
    order = [(STEP[n], 1, n) for n in names]
    order += [(NC * h + 1, 0, "tm%d" % (h + 2)) for h in range(H) if nxt or h + 2 < H]
    order += [(NC * h + 3, 0, "tv%d" % (h - 1)) for h in range(1, H)]
    rank = {n: i for i, n in enumerate(FINISH + EMBED + PREPARE + ROUTE)}
    order.sort(key=lambda o: (o[0], o[1], rank.get(o[2], 0)))
    return [o[2] for o in order]


PROLOGUE = list(EMBED + PREPARE) + ["tm0", "tm1"]
FIRST = turns(0, False, True)
CYCLE = [turns(k, True, True) for k in range(4)]
LAST = turns(3, True, False)
TAIL = list(FINISH + ROUTE)


class Slot:

    def __init__(self, pair, k, prev=True, nxt=True):
        self.start = False
        self.pair, self.k, self.prev, self.nxt = pair, k, prev, nxt
        self.n = 4 * pair + k
        self.names = CYCLE[k] if prev and nxt else LAST if prev else FIRST
        before = sum(len(c) for c in CYCLE)
        if prev:
            self.base = before * pair + (sum(len(c) for c in CYCLE[:k]) + len(PROLOGUE) + len(FIRST) - len(CYCLE[0]))
        else:
            self.base = len(PROLOGUE)

    def turn(self, name):
        return self.base + self.names.index(name)


class Outside(Slot):

    def __init__(self, n):
        self.n, self.start = n, n < 0
        self.names = PROLOGUE if n < 0 else TAIL
        self.base = 0 if n < 0 else Slot(B // 2 - 1, 3).base + len(LAST)
        self.pair, self.k = (0, -1) if n < 0 else (B // 2, 0)
        self.prev, self.nxt = n >= 0, n < 0


def build(nc, x, cls_tok, pe, tokW, wq1, wk1, wv1, bq1, bk1, bv1, wo1, bo1,
          ln1g, ln1b, wq2, wk2, wv2, wo2, ln2g, ln2b, wr, w1, b1, w2, b2,
          ident_d, headmask_d, headmaskT_d, lower_d, iota_d, valid_d, out):
    ctx = ExitStack()
    with ctx:
        def sb(name, shape, dt=F32):
            return ctx.enter_context(nc.sbuf_tensor(name, shape, dt))

        def psum(name, shape):
            return ctx.enter_context(nc.psum_tensor(name, shape, F32))

        def sem(name):
            return ctx.enter_context(nc.semaphore(name))

        slots_in = nc.dram_tensor("slots_in", [SLOTS, D], F32).ap()
        stream = nc.dram_tensor("stream", [B * NT * P, D], F32).ap()
        slots_out = nc.dram_tensor("slots_out", [SLOTS, D], F32).ap()

        ident = sb("ident", [P, P])
        headmask = sb("headmask", [P, H])
        headmaskT = sb("headmaskT", [H, P])
        lower = sb("lower", [P, P], BF16)
        ones_bf = sb("ones_bf", [P, P], BF16)
        ones_f = sb("ones_f", [P, 1])
        iota1 = sb("iota1", [P, E])
        valid = sb("valid", [P, NT])
        pe_t = sb("pe_t", [P, NC, D])
        tokw = sb("tokw", [F_IN, D])
        wq = sb("wq", [P, 2, D])
        wk = sb("wk", [P, 2, D])
        wv = sb("wv", [P, 2, D])
        wo = sb("wo", [P, 2, D])
        bq = sb("bq", [P, 1])
        bk = sb("bk", [P, 1])
        bv = sb("bv", [P, 1])
        bo = sb("bo", [P, D])
        g1 = sb("g1", [P, 1])
        c1 = sb("c1", [P, 1])
        g2 = sb("g2", [P, D])
        c2 = sb("c2", [P, D])
        wrt = sb("wrt", [P, E])
        b1t = sb("b1t", [P, FC, E])
        clst = sb("clst", [P, D])

        gidx = sb("gidx", [P, B, NT, TOPK], U32)
        gate = sb("gate", [P, B, NT, TOPK])

        xT = sb("xT", [F_IN, S])
        hb = sb("hb", [P, 2, NT, D])
        G = sb("G", [P, 2, NT, D])
        N = sb("N", [P, NT, D])
        st = sb("st", [P, NT, 6])
        sm = sb("sm", [P, 8, NT])
        nT = sb("nT", [P, NT, P])
        qh = sb("qh", [P, S], F32R)
        ql = sb("ql", [P, S], F32R)
        kh = sb("kh", [P, S], F32R)
        kl = sb("kl", [P, S], F32R)
        qst = sb("qst", [P, H // 2, S], F32R)
        kst = sb("kst", [P, H, S], F32R)
        zrow = sb("zrow", [NC, P])
        vt = sb("vt", [P, 2, NC, H, 32])
        vcb = sb("vcb", [P, 2, D])
        qkc = sb("qkc", [P, 2])
        bd = sb("bd", [P, 2, H])
        bdp = sb("bdp", [P, 2, 2, H], F32R)
        mxu = sb("mxu", [P, 2, H, NC, 3])
        mr = sb("mr", [P, H, NC], F32R)
        mT = sb("mT", [NC, 2, P], F32R)
        pck = sb("pck", [P, H, NC])
        pr = sb("pr", [P, 4, S])
        avs = sb("avs", [P, 2, 256])
        U = sb("U", [P, 2, NC, H, C])
        Ut = sb("Ut", [P, NC, H, C])
        den = sb("den", [P, 2, NC, H])
        clc = sb("clc", [P, 2])
        ctxT = sb("ctxT", [P, NT, P])
        csc = sb("csc", [H, 8])
        pc = sb("pc", [H, S])
        pcs = sb("pcs", [P, P])
        pcT = sb("pcT", [P, H, NC])
        cm = sb("cm", [H, D])
        x2 = sb("x2", [P, NT, D])
        lg = sb("lg", [P, NT, E])
        mv = sb("mv", [P, NT, 8])
        mi = sb("mi", [P, NT, 8], U32)
        e1 = sb("e1", [P, TOPK, NT])
        oh = sb("oh", [P, TOPK, NT, E])
        ohs = sb("ohs", [P, NT, E], BF16)
        run = sb("run", [P, NT + 1, E], BF16)
        pos = sb("pos", [P, NT, E])
        pk = sb("pk", [P, TOPK, NT])
        keep = sb("keep", [P, TOPK, NT])
        rt = sb("rt", [P, 12, NT])
        sidx = sb("sidx", [P, NT, TOPK], U32)

        zeros = N[:, 0:SC, :]
        w1t = [nT[:, 0:4, :].rearrange("p c s -> p (c s)"), nT[:, 4:8, :].rearrange("p c s -> p (c s)")]
        w2t = [ctxT[:, 0:4, :], ctxT[:, 4:8, :]]
        xin = [N[:, 0:4, :], N[:, 4:8, :]]
        xinT = [G[:, i, 0:4, :].rearrange("p c s -> p (c s)") for i in range(2)]
        hid = [pr[:, 0:2, :].rearrange("p a (b s) -> p (a b) s", b=2),
               pr[:, 2:4, :].rearrange("p a (b s) -> p (a b) s", b=2)]
        b2t = [x2[:, 0, :], x2[:, 1, :]]
        yout = [hb[:, 0, 0:4, :], hb[:, 1, 0:4, :]]
        rows = [N, G[:, 0], x2, nT]
        fin = [hb[:, 0], hb[:, 1]]
        vtick = sb("vtick", [P, 1])
        consts = sb("consts", [P, 5, NT])
        tick = sb("tick", [P, 1])
        gi = sb("gi", [P, 2, NT, TOPK], U32)
        gg = sb("gg", [P, 2, NT, TOPK])

        psS = psum("psS", [P, 2, S])
        psM = psum("psM", [P, 2, 512])
        psV = psum("psV", [P, 512])
        psX = psum("psX", [P, 512])
        x4 = psX[:, :].rearrange("p (c d) -> p c d", d=D)
        xcol = psX[:, 0:1]
        xhc = psX[:, 0:NC * H]
        xrow = psX[0:1, 0:D]
        xho = psX[0:H, 0:D]
        xm = psX[0:NC, 0:P]
        xav = psX[:, 0:2 * P]

        names = """const clear minus cls init zeroed attended x
            xfull xfree stk0 stk1 stk2 stk3 mrow0 mrow1 p1 p1u mr p2 exp av avs pd pe ut
            st ln lnlink biased hi qclink bd cm ce cmk ctx x2 gd ge rlink consts ohs runlink oh scat sidx gated rden x2g pcs normg normn x2f res resd0 resd1
            wa0 wa1 wb0 wb1 bb0 bb1 xi0 xi1 tp xt hp gl yp yo yst0 yst1 done
            tick gi ga0 ga1 rs0 rs1 fin out0 out1 outf ysf""".split()
        s = {n: sem("s_" + n) for n in names}

        LN_LINKS, QC_LINKS, R_LINKS, RUN_LINKS = 6, 6, 12, 10
        CONSTS = 26
        STK = 16 * (12 + 2)
        U_HEAD = 2 * NC
        T_ATT = H * NC

        def slots(eng, slot):
            slot(Slot(0, 0, prev=False))
            with eng.Fori(0, B // 2 - 1) as r:
                for k in (1, 2, 3):
                    slot(Slot(r, k))
                slot(Slot(r + 1, 0))
            for k in (1, 2, 3):
                slot(Slot(B // 2 - 1, k, nxt=k < 3))

        def chain(eng, name, links, count):
            seen = [0]

            def link(ins):
                seen[0] += 1
                assert seen[0] <= links
                ins.then_inc(s[name], 1)
                eng.wait_ge(s[name], links * count + seen[0])
            return link

        block = ctx.enter_context(nc.Block())

        @block.sync
        def _(sp):
            loads = [(ident[:, :], ident_d), (headmask[:, :], headmask_d), (headmaskT[:, :], headmaskT_d),
                     (iota1[:, :], iota_d), (valid[:, :], valid_d), (pe_t[:, :, :], pe), (tokw[:, :], tokW),
                     (wq[:, 0, :], wq1), (wk[:, 0, :], wk1), (wv[:, 0, :], wv1), (wo[:, 0, :], wo1),
                     (wq[:, 1, :], wq2), (wk[:, 1, :], wk2), (wv[:, 1, :], wv2), (wo[:, 1, :], wo2),
                     (bq[:, :], bq1), (bk[:, :], bk1), (bv[:, :], bv1),
                     (bo[:, :], bo1.broadcast_to([P, D])), (g1[:, :], ln1g), (c1[:, :], ln1b),
                     (g2[:, :], ln2g.broadcast_to([P, D])), (c2[:, :], ln2b.broadcast_to([P, D])),
                     (wrt[:, :], wr), (lower[:, :], lower_d), (b1t[:, :, :], b1)]
            assert len(loads) == CONSTS
            for dst, src in loads:
                sp.dma_start(dst, src).then_inc(s["const"], 16)
            sp.wait_ge(s["clear"], 1)
            sp.dma_start(clst[0:1, :], cls_tok).then_inc(s["cls"], 16)
            for e in range(E):
                sp.dma_start(slots_in[e * CAP:(e + 1) * CAP, :].rearrange("(p c) d -> p (c d)", p=P),
                             zeros).then_inc(s["zeroed"], 16)
            sp.wait_ge(s["init"], 1)
            for h in range(H):
                p0 = HALF * (h % 2) + GRP
                sp.dma_start(kst[p0:p0 + 1, h, :].bitcast(F32), mT[:, 0, :].bitcast(F32)).then_inc(s["minus"], 16)

            def load_tokens(b):
                sp.dma_start(xT[:, :], x[:, bass.ds(b * S, S)]).then_inc(s["x"], 16)

            def stack(p, z=None):
                for p0 in (GRP, HALF + GRP):
                    sp.dma_start(qst[p0:p0 + 1, p, :].bitcast(F32), zrow[:, :]).then_inc(s["stk%d" % p], 16)
                if z is not None:
                    sp.wait_ge(s["xfree"], z.turn("k1") + 1)
                for h in (2 * p, 2 * p + 1):
                    for src, dst, parts in ((qh, qst[:, p, :], (0, 1)), (ql, qst[:, p, :], (2,)),
                                            (kh, kst[:, h, :], (0, 2)), (kl, kst[:, h, :], (1,))):
                        for r in parts:
                            p0 = HALF * (h % 2) + C * r
                            sp.dma_start(dst[p0:p0 + C, :].bitcast(F32),
                                         src[C * h:C * h + C, :].bitcast(F32)).then_inc(s["stk%d" % p], 16)

            def maxima_rows(h):
                for i in range(2):
                    p0 = HALF * i + GRP
                    sp.dma_start(qst[p0:p0 + 1, h // 2, :].bitcast(F32),
                                 mT[:, i, :].bitcast(F32)).then_inc(s["mrow%d" % i], 16)

            def sp_slot(z):
                if z.nxt and z.k in (3, 0):
                    load_tokens(2 * (z.pair + 1) if z.k == 3 else 2 * z.pair + 1)
                if z.prev:
                    sp.wait_ge(s["p2"], T_ATT * z.n)
                    stack(3)
                sp.wait_ge(s["xfree"], z.turn("tm3") + 1)
                maxima_rows(2)
                if z.prev and z.k in (3, 0):
                    b = 2 * z.pair if z.k == 3 else 2 * z.pair - 1
                    sp.wait_ge(s["res"], b + 1)
                    sp.dma_start(stream[bass.ds(b * NT * P, NT * P), :].rearrange("(c p) d -> p c d", p=P),
                                 G[:, (z.k + 1) % 2, :, :]).then_inc(s["resd%d" % ((z.k + 1) % 2)], 16)
                sp.wait_ge(s["xfree"], z.turn("tm5") + 1)
                maxima_rows(4)
                if z.nxt:
                    for p in range(2):
                        sp.wait_ge(s["p2"], T_ATT * z.n + 2 * NC * (p + 1))
                        stack(p, z)
                sp.wait_ge(s["xfree"], z.turn("tm7") + 1)
                maxima_rows(6)
                if z.nxt:
                    spread_class(z.n + 1)
                    sp.wait_ge(s["p2"], T_ATT * z.n + 6 * NC)
                    stack(2)
                    sp.wait_ge(s["xfree"], z.turn("tm9") + 1)
                    maxima_rows(0)

            def spread_class(j):
                sp.wait_ge(s["ce"], j + 1)
                sp.dma_start(pcs[0:H * NC, :], pc[:, :]).then_inc(s["pcs"], 16)

            load_tokens(0)
            z = Outside(-1)
            sp.wait_ge(s["xfree"], z.turn("k1") + 1)
            for p in range(4):
                stack(p)
            spread_class(0)
            sp.wait_ge(s["xfree"], z.turn("tm1") + 1)
            maxima_rows(0)
            slots(sp, sp_slot)
            sp.wait_ge(s["res"], B)
            sp.dma_start(stream[(B - 1) * NT * P:, :].rearrange("(c p) d -> p c d", p=P),
                         G[:, 1, :, :]).then_inc(s["resd1"], 16)
            sp.wait_ge(s["resd0"], 16 * (B // 2))
            sp.wait_ge(s["resd1"], 16 * (B // 2))
            sp.wait_ge(s["attended"], 1)
            sp.wait_ge(s["scat"], 16 * B * NT * TOPK)
            with sp.Fori(0, E // 2) as g:
                for i in range(2):
                    e = 2 * g + i
                    sp.wait_ge(s["tp"], e + 1)
                    sp.dma_start(xin[i], slots_in[bass.ds(e * CAP, CAP), :].rearrange("(c p) d -> p c d", p=P)
                                 ).then_inc(s["xi%d" % i], 16)
                    sp.wait_ge(s["hp"], FC * (e + 1))
                    sp.dma_start(w1t[i], w1[bass.ds(e * D, D), :]).then_inc(s["wa%d" % i], 16)
                for i in range(2):
                    e = 2 * g + i
                    sp.wait_ge(s["yp"], e + 1)
                    sp.wait_ge(s["yo"], e + 1)
                    sp.dma_start(w2t[i], w2[bass.ds(e * P, P), :].rearrange("p (f d) -> p f d", d=D)).then_inc(
                        s["wb%d" % i], 16)
                    sp.dma_start(b2t[i], b2[bass.ds(e, 1), :].broadcast_to([P, D])).then_inc(s["bb%d" % i], 16)
            sp.sem_inc(s["outf"], 2)
            sp.wait_ge(s["yst0"], 16 * (E // 2))
            sp.wait_ge(s["yst1"], 16 * (E // 2))
            with sp.Fori(0, B // 2) as g:
                for i in range(2):
                    sp.dma_start(fin[i], stream[bass.ds((2 * g + i) * NT * P, NT * P), :].rearrange(
                        "(c p) d -> p c d", p=P)).then_inc(s["rs%d" % i], 16)
                for i in range(2):
                    b = 2 * g + i
                    sp.wait_ge(s["fin"], b + 3)
                    sp.dma_start(out[bass.ds(b, 1), 1:S + 1, :].rearrange("o (c p) d -> p (o c) d", p=P),
                                 fin[i][:, 1:NT, :]).then_inc(s["out%d" % i], 16)
                    sp.dma_start(out[bass.ds(b, 1), 0, :], fin[i][0:1, 0, :]).then_inc(s["out%d" % i], 16)
                for i in range(2):
                    sp.wait_ge(s["out%d" % i], 32 * g + 32)
                    sp.sem_inc(s["outf"], 1)
            for i in range(2):
                sp.wait_ge(s["out%d" % i], 32 * (B // 2))

        @block.tensor
        def _(pe_):
            pe_.wait_ge(s["const"], 16 * CONSTS)
            pe_.wait_ge(s["init"], 1)
            pe_.wait_ge(s["minus"], 16 * H)

            def turn(z, name):
                v = z.turn(name)
                if later(v):
                    pe_.wait_ge(s["xfree"], v)

            def maxima(n, h, c, i):
                if h % 2 == 0 and c == 0 and i == 0:
                    pe_.wait_ge(s["stk%d" % (h // 2)], STK * (n + 1))
                u = U_HEAD * h + 2 * c + i
                if u >= 2 or later(n):
                    pe_.wait_ge(s["p1u"], n * (U_HEAD * H) + u - 1)
                pe_.matmul(psM[:, i, :], qst[:, h // 2, c * P:(c + 1) * P], kst[:, h, 512 * i:512 * i + 512],
                           start=True, stop=True).then_inc(s["p1"], 1)

            def turn_maxima(z, n, h, name):
                turn(z, name)
                pe_.wait_ge(s["mr"], n * H + h + 1)
                pe_.transpose(xm, mr[:, h, :].bitcast(F32), ident[:, :]).then_inc(s["xfull"], 1)

            def scores(n, h, c):
                t = NC * h + c
                if c == 0 and h % 2 == 0:
                    for i in range(2):
                        pe_.wait_ge(s["mrow%d" % i], 16 * (n * (H // 2) + h // 2 + 1))
                if t >= 2 or later(n):
                    pe_.wait_ge(s["exp"], n * T_ATT + t - 1)
                for i in range(2):
                    mm = pe_.matmul(psS[:, t % 2, 512 * i:512 * i + 512], kst[:, h, c * P:(c + 1) * P],
                                    qst[:, h // 2, 512 * i:512 * i + 512], start=True, stop=True)
                mm.then_inc(s["p2"], 1)

            def values(n, w, h, c):
                t = NC * h + c
                pe_.wait_ge(s["exp"], n * T_ATT + t + 1)
                if c == 0 and (h >= 1 or later(n)):
                    pe_.wait_ge(s["avs"], n * H + h)
                for j in range(4):
                    mm = pe_.matmul(psV[32 * j:32 * j + 32, 0:256], vt[:, w, c, h, :],
                                    pr[:, t % 4, 256 * j:256 * j + 256], start=(c == 0), stop=(c == NC - 1))
                mm.then_inc(s["av"], 1)

            def turn_values(z, n, h, name):
                turn(z, name)
                pe_.wait_ge(s["avs"], n * H + h + 1)
                pe_.transpose(xav[:, 0:P], avs[:, h % 2, 0:P], ident[:, :])
                pe_.transpose(xav[:, P:2 * P], avs[:, h % 2, P:2 * P], ident[:, :]).then_inc(s["xfull"], 1)

            def prepare(z, name):
                j = z.n + 1
                a, w = (z.k + 1) % 4 // 2, (z.k + 1) % 2
                turn(z, name)
                if name in ("e0", "e1"):
                    i = int(name[1])
                    if i == 0:
                        pe_.wait_ge(s["x"], 16 * (2 * (z.pair + 1 if z.k == 3 else z.pair) + w + 1))
                    for c in range(4):
                        mm = pe_.matmul(x4[:, c, :], xT[:, (4 * i + c) * P:(4 * i + c + 1) * P], tokw[:, :],
                                        start=True, stop=True)
                elif name in ("nt0", "nt1"):
                    i = int(name[2])
                    pe_.wait_ge(s["normn"], 3 * j + 2 + i)
                    for c in range(4):
                        mm = pe_.transpose(x4[:, c, :], N[:, 1 + 4 * i + c, :], ident[:, :])
                elif name == "ntc":
                    mm = pe_.transpose(psX[:, 0:P], N[:, 0, :], ident[:, :])
                elif name == "qc":
                    pe_.matmul(psX[:, 0:1], wq[:, a, :], nT[:, 0, 0:1], start=True, stop=True)
                    mm = pe_.matmul(psX[:, 1:2], wk[:, a, :], nT[:, 0, 0:1], start=True, stop=True)
                elif name in ("q0", "q1", "k0", "k1"):
                    i = int(name[1])
                    mm = pe_.matmul(psX[:, :], (wq if name[0] == "q" else wk)[:, a, :],
                                    nT[:, 1 + 4 * i:5 + 4 * i, :].rearrange("p c s -> p (c s)"),
                                    start=True, stop=True)
                elif name == "ck":
                    pe_.wait_ge(s["bd"], j + 1)
                    for c in range(NC):
                        o = psX[:, 2 * c * H:2 * (c + 1) * H]
                        cs = slice(c * P, (c + 1) * P)
                        pe_.matmul(o, qh[:, cs], bdp[:, 1, :, :].rearrange("p i h -> p (i h)"), start=True,
                                   stop=False)
                        mm = pe_.matmul(o, ql[:, cs], bdp[:, 1, :, :].rearrange("p i h -> p (i h)"), start=False,
                                        stop=True)
                elif name in ("v0", "v1"):
                    for c in range(4):
                        mm = pe_.matmul(x4[:, c, :], nT[:, 1 + 4 * int(name[1]) + c, :], wv[:, a, :],
                                        start=True, stop=True)
                elif name == "vc":
                    mm = pe_.matmul(psX[:, 0:D], nT[:, 0, 0:1].broadcast_to([P, P]), wv[:, a, :], start=True,
                                    stop=True)
                elif name in ("cq0", "cq1"):
                    i = int(name[2])
                    cs = slice(512 * i, 512 * i + 512)
                    pe_.matmul(psX[0:H, :], bdp[:, 0, 0, :], kh[:, cs], start=True, stop=False)
                    pe_.matmul(psX[0:H, :], bdp[:, 0, 0, :], kl[:, cs], start=False, stop=False)
                    mm = pe_.matmul(psX[0:H, :], bdp[:, 0, 1, :], kh[:, cs], start=False, stop=True)
                elif name == "cc":
                    mm = pe_.matmul(psX[0:H, 0:1], bd[:, 0, :], qkc[:, 1:2], start=True, stop=True)
                elif name == "pt":
                    pe_.wait_ge(s["pcs"], 16 * (j + 1))
                    mm = pe_.transpose(psX[:, 0:P], pcs[:, :], ident[:, :])
                elif name == "co":
                    for c in range(NC):
                        mm = pe_.matmul(xho, pcT[:, :, c], vt[:, w, c, :, 0:C], start=(c == 0), stop=(c == NC - 1))
                elif name == "cf":
                    pe_.wait_ge(s["cmk"], j + 1)
                    mm = pe_.matmul(xcol, cm[:, :], ones_f[0:H, :], start=True, stop=True)
                mm.then_inc(s["xfull"], 1)

            def finish(z, name):
                a, w = (z.k - 1) % 4 // 2, (z.k - 1) % 2
                turn(z, name)
                if name in ("ct0", "ct1"):
                    i = int(name[2])
                    pe_.wait_ge(s["ctx"], 2 * z.n - 1 + i)
                    for c in range(4):
                        mm = pe_.transpose(x4[:, c, :], U[:, w, 4 * i + c, :, :].rearrange("p h c -> p (h c)"),
                                           ident[:, :])
                elif name == "oc":
                    mm = pe_.matmul(xrow, clc[:, w:w + 1], wo[:, a, :], start=True, stop=True)
                elif name in ("o0", "o1"):
                    for c in range(4):
                        mm = pe_.matmul(x4[:, c, :], ctxT[:, 1 + 4 * int(name[1]) + c, :], wo[:, a, :],
                                        start=True, stop=True)
                mm.then_inc(s["xfull"], 1)

            def route(z, name):
                b = 2 * z.pair if z.k == 3 else 2 * z.pair - 1
                turn(z, name)
                if name in ("xa", "xb"):
                    if name == "xa":
                        pe_.wait_ge(s["x2"], b + 1)
                    for c in range(4):
                        mm = pe_.transpose(x4[:, c, :], x2[:, (1 if name == "xa" else 5) + c, :], ident[:, :])
                elif name == "xc":
                    mm = pe_.transpose(psX[:, 0:P], x2[:, 0, :], ident[:, :])
                elif name == "lga":
                    for c in range(NC):
                        mm = pe_.matmul(psX[:, c * E:(c + 1) * E], nT[:, 1 + c, :], wrt[:, :], start=True, stop=True)
                elif name == "lgb":
                    mm = pe_.matmul(psX[:, 0:E], nT[:, 0, :], wrt[:, :], start=True, stop=True)
                elif name in ("posa", "posb"):
                    if name == "posa":
                        pe_.wait_ge(s["oh"], b + 1)
                    for i, c in enumerate(range(1, NT) if name == "posa" else (0,)):
                        o = psX[:, i * E:(i + 1) * E]
                        pe_.matmul(o, lower[:, :], ohs[:, c, :], start=True, stop=False)
                        mm = pe_.matmul(o, ones_bf[:, :], run[:, c, :], start=False, stop=True)
                mm.then_inc(s["xfull"], 1)

            def pe_slot(z):
                n = z.n
                w = z.k % 2
                for h in range(H):
                    for c in range(NC):
                        t = NC * h + c
                        if h + 3 < H:
                            maxima(n, h + 3, c, 0)
                        elif z.nxt:
                            maxima(z.n + 1, h + 3 - H, c, 0)
                        scores(n, h, c)
                        if h + 3 < H:
                            maxima(n, h + 3, c, 1)
                        elif z.nxt:
                            maxima(z.n + 1, h + 3 - H, c, 1)
                        if c >= 1:
                            values(n, w, h, c - 1)
                        elif h >= 1:
                            values(n, w, h - 1, NC - 1)
                        elif z.prev:
                            values(z.n - 1, 1 - w, H - 1, NC - 1)
                        if c == 1 and h + 2 < H:
                            turn_maxima(z, n, h + 2, "tm%d" % (h + 2))
                        elif c == 1 and z.nxt:
                            turn_maxima(z, z.n + 1, h + 2 - H, "tm%d" % (h + 2))
                        if c == 3 and h >= 1:
                            turn_values(z, n, h - 1, "tv%d" % (h - 1))
                        if z.prev and t == STEP["tv7"]:
                            turn_values(z, z.n - 1, H - 1, "tv7")
                        for name in FINISH[1:]:
                            if z.prev and t == STEP[name]:
                                finish(z, name)
                        for name in EMBED + PREPARE:
                            if name in z.names and t == STEP[name]:
                                prepare(z, name)
                        for name in ROUTE:
                            if name in z.names and t == STEP[name]:
                                route(z, name)

            z = Outside(-1)
            for name in EMBED + PREPARE:
                prepare(z, name)
            for h in range(3):
                for c in range(NC):
                    for i in range(2):
                        maxima(0, h, c, i)
                if h < 2:
                    turn_maxima(z, 0, h, "tm%d" % h)
            slots(pe_, pe_slot)
            z = Outside(2 * B)
            values(z.n - 1, 1, H - 1, NC - 1)
            turn_values(z, z.n - 1, H - 1, "tv7")
            for name in FINISH[1:]:
                finish(z, name)
            for name in ROUTE:
                route(z, name)
            pe_.wait_ge(s["attended"], 1)

            pe_.sem_inc(s["hp"], 2 * FC)
            pe_.sem_inc(s["tp"], 2)
            pe_.sem_inc(s["yp"], 2)

            def turn_slots(e, g, i):
                pe_.wait_ge(s["xi%d" % i], 16 * g + 16)
                pe_.wait_ge(s["xt"], e + 1)
                for c in range(SC):
                    mm = pe_.transpose(psX[:, c * P:(c + 1) * P], xin[i][:, c, :], ident[:, :])
                mm.then_inc(s["tp"], 1)

            def up(e, g, i):
                pe_.wait_ge(s["xt"], e + 2)
                pe_.wait_ge(s["wa%d" % i], 16 * g + 16)
                for f in range(FC):
                    pe_.wait_ge(s["gl"], FC * e + f + 1)
                    pe_.matmul(psS[:, f // 2, 512 * (f % 2):512 * (f % 2) + 512], w1t[i][:, f:F:FC], xinT[i],
                               start=True, stop=True).then_inc(s["hp"], 1)

            def down(e, g, i):
                pe_.wait_ge(s["gl"], FC * (e + 2))
                pe_.wait_ge(s["wb%d" % i], 16 * g + 16)
                pe_.wait_ge(s["yo"], e + 1)
                for c in range(SC):
                    for f in range(FC):
                        mm = pe_.matmul(psM[:, i, c * P:(c + 1) * P], hid[i][:, f, c * P:(c + 1) * P],
                                        w2t[i][:, f, :], start=(f == 0), stop=(f == FC - 1))
                mm.then_inc(s["yp"], 1)

            with pe_.Fori(0, E // 2) as g:
                turn_slots(2 * g, g, 0)
                up(2 * g, g, 0)
                turn_slots(2 * g + 1, g, 1)
                up(2 * g + 1, g, 1)
                down(2 * g, g, 0)
                down(2 * g + 1, g, 1)

        @block.scalar
        def _(act):
            act.wait_ge(s["const"], 16 * CONSTS)

            def class_exp(n, h):
                act.wait_ge(s["pd"], n * H + h + 1)
                act.activation(pck[:, h, :], pck[:, h, :], ACT.Exp, scale=SCALE).then_inc(s["pe"], 1)

            def normalise(src, dst, part):
                for c in range(3 * part, 3 * part + 3):
                    ins = act.activation(dst[:, c, :], src[:, c, :], ACT.Identity, bias=sm[:, 3, c:c + 1],
                                         scale=sm[:, 4, c:c + 1])
                return ins

            def turn_maxima(z, n, h, name):
                act.wait_ge(s["xfull"], z.turn(name) + 1)
                if h >= 2 or later(n):
                    act.wait_ge(s["mrow%d" % (h % 2)], 16 * (n * (H // 2) + h // 2))
                act.activation(mT[:, h % 2, :], xm, ACT.Copy).then_inc(s["xfree"], 1)

            def take_values(n, h):
                act.wait_ge(s["av"], n * T_ATT + NC * (h + 1))
                act.activation(avs[:, h % 2, :], psV[:, 0:256], ACT.Copy).then_inc(s["avs"], 1)

            def prepare(z, name):
                j = z.n + 1
                a, w = (z.k + 1) % 4 // 2, (z.k + 1) % 2
                if name.startswith("norm1"):
                    act.wait_ge(s["ln"], 2 * z.n + 2 if not z.start else 1)
                    normalise(hb[:, w] if a == 0 else G[:, w], N, "abc".index(name[5])).then_inc(s["normn"], 1)
                    return
                if name == "cexp":
                    act.wait_ge(s["cm"], j + 1)
                    act.activation(csc[:, 4:5], csc[:, 0:1], ACT.Exp, bias=csc[:, 2:3], scale=SCALE)
                    act.activation(pc[:, :], pc[:, :], ACT.Exp, bias=csc[:, 2:3], scale=SCALE,
                                   accum_out=csc[:, 3:4]).then_inc(s["ce"], 1)
                    return
                act.wait_ge(s["xfull"], z.turn(name) + 1)
                if name in ("nt0", "nt1", "ntc"):
                    if name == "ntc":
                        dst, src = nT[:, 0, 0:1], xcol
                    else:
                        i = int(name[2])
                        dst, src = nT[:, 1 + 4 * i:5 + 4 * i, :].rearrange("p c s -> p (c s)"), psX[:, :]
                    if a == 0:
                        ins = act.activation(dst, src, ACT.Copy)
                    else:
                        ins = act.activation(dst, src, ACT.Identity, bias=c1[:, 0:1], scale=g1[:, 0:1])
                    ins.then_inc(s["xfree"], 1)
                elif name in ("q0", "q1", "k0", "k1"):
                    if name == "q0" and not z.start:
                        for p in range(4):
                            act.wait_ge(s["stk%d" % p], STK * j)
                    i = int(name[1])
                    dst, bias = (qh, bq) if name[0] == "q" else (kh, bk)
                    act.activation(dst[:, 512 * i:512 * i + 512], psX[:, :], ACT.Identity,
                                   bias=bias[:, 0:1] if a == 0 else 0.0).then_inc(s["hi"], 1)
                elif name in ("v0", "v1"):
                    i = int(name[1])
                    act.activation(vt[:, w, 4 * i:4 * i + 4, :, 0:C], x4.rearrange("p c (h e) -> p c h e", h=H),
                                   ACT.Copy).then_inc(s["xfree"], 1)
                elif name == "vc":
                    act.activation(vcb[:, w, :], psX[:, 0:D], ACT.Copy).then_inc(s["xfree"], 1)
                elif name in ("cq0", "cq1"):
                    i = int(name[2])
                    act.activation(pc[:, 512 * i:512 * i + 512], psX[0:H, :], ACT.Copy).then_inc(s["xfree"], 1)
                elif name == "cf":
                    act.activation(clc[:, w:w + 1], xcol, ACT.Identity,
                                   bias=bv[:, 0:1] if a == 0 else 0.0).then_inc(s["xfree"], 1)

            def finish(z, name):
                if name.startswith("norm0"):
                    w = (z.k - 1) % 2
                    act.wait_ge(s["ln"], 2 * z.n + 1)
                    normalise(hb[:, w], G[:, w], "abc".index(name[5])).then_inc(s["normg"], 1)
                    return
                i = int(name[2])
                act.wait_ge(s["xfull"], z.turn(name) + 1)
                act.activation(ctxT[:, 1 + 4 * i:5 + 4 * i, :].rearrange("p c s -> p (c s)"), psX[:, :], ACT.Identity,
                               bias=bv[:, 0:1] if (z.k - 1) % 4 // 2 == 0 else 0.0).then_inc(s["xfree"], 1)

            def route(z, name):
                b = 2 * z.pair if z.k == 3 else 2 * z.pair - 1
                if name == "rexp":
                    act.wait_ge(s["gd"], b + 1)
                    act.activation(rt[:, 1, :], rt[:, 0, :], ACT.Exp).then_inc(s["ge"], 1)
                    return
                dst, src = {"xa": (nT[:, 1:5, :], x4), "xb": (nT[:, 5:9, :], x4), "xc": (nT[:, 0, :], psX[:, 0:P]),
                            "lga": (lg[:, 1:NT, :], psX[:, :].rearrange("p (c e) -> p c e", e=E)),
                            "lgb": (lg[:, 0, :], psX[:, 0:E]),
                            "posa": (pos[:, 1:NT, :], psX[:, :].rearrange("p (c e) -> p c e", e=E)),
                            "posb": (pos[:, 0, :], psX[:, 0:E])}[name]
                act.wait_ge(s["xfull"], z.turn(name) + 1)
                act.activation(dst, src, ACT.Copy).then_inc(s["xfree"], 1)

            ACT_PREPARE = ("norm1a", "norm1b", "norm1c", "nt0", "nt1", "q0", "q1", "k0", "k1", "ntc", "v0", "v1", "vc", "cq0", "cq1", "cexp", "cf")
            ACT_ROUTE = ("xa", "xb", "xc", "lga", "lgb", "rexp", "posa", "posb")

            def act_slot(z):
                n = z.n
                for h in range(H):
                    for c in range(NC):
                        t = NC * h + c
                        act.wait_ge(s["p2"], n * T_ATT + t + 1)
                        if t >= 4 or z.prev:
                            act.wait_ge(s["av"], n * T_ATT + t - 3)
                        act.activation(pr[:, t % 4, :], psS[:, t % 2, :], ACT.Exp, scale=SCALE).then_inc(s["exp"], 1)
                        if c == 3 and h + 2 < H:
                            class_exp(n, h + 2)
                        elif c == 3 and z.nxt:
                            class_exp(z.n + 1, h + 2 - H)
                        if c == 0 and h >= 1:
                            take_values(n, h - 1)
                        elif c == 0 and z.prev:
                            take_values(z.n - 1, H - 1)
                        if c == 1 and h + 2 < H:
                            turn_maxima(z, n, h + 2, "tm%d" % (h + 2))
                        elif c == 1 and z.nxt:
                            turn_maxima(z, z.n + 1, h + 2 - H, "tm%d" % (h + 2))
                        for name in ("ct0", "ct1") + (("norm0a", "norm0b", "norm0c") if z.k in (1, 2) else ()):
                            if z.prev and t == STEP[name]:
                                finish(z, name)
                        for name in ACT_PREPARE:
                            if z.nxt and t == STEP[name]:
                                prepare(z, name)
                        for name in ACT_ROUTE:
                            if z.prev and z.k in (3, 0) and t == STEP[name]:
                                route(z, name)

            z = Outside(-1)
            for name in ACT_PREPARE:
                prepare(z, name)
            for h in range(2):
                turn_maxima(z, 0, h, "tm%d" % h)
                class_exp(0, h)
            slots(act, act_slot)
            z = Outside(2 * B)
            take_values(z.n - 1, H - 1)
            for name in ("ct0", "ct1"):
                finish(z, name)
            for name in ACT_ROUTE:
                route(z, name)
            act.sem_inc(s["gl"], FC)
            with act.Fori(0, E // 2) as g:
                for i in range(2):
                    e = 2 * g + i
                    act.wait_ge(s["yp"], e + 1)
                    for f in range(FC):
                        act.wait_ge(s["hp"], FC * (e + 2) + f + 1)
                        act.activation(hid[i][:, f, :], psS[:, f // 2, 512 * (f % 2):512 * (f % 2) + 512],
                                       ACT.Gelu_apprx_tanh, bias=b1t[:, f, bass.ds(e, 1)]).then_inc(s["gl"], 1)

        @block.vector
        def _(dve):
            dve.memset(N[:, :, :], 0.0)
            dve.memset(clst[:, :], 0.0).then_inc(s["clear"], 1)
            dve.memset(ones_bf[:, :], 1.0)
            dve.memset(ones_f[:, :], 1.0)
            dve.memset(run[:, :, :], 0.0)
            dve.memset(vt[:, :, :, :, :], 0.0).then_inc(s["clear"], 1)
            dve.wait_ge(s["clear"], 2)
            dve.memset(vt[:, :, :, :, C:C + 1], 1.0)
            dve.memset(nT[:, 0, :], 0.0)
            dve.memset(ctxT[:, 0, :], 0.0)
            dve.memset(zrow[:, :], 0.0)
            dve.memset(pcs[:, :], 0.0)
            dve.memset(mT[:, :, :].bitcast(F32), -1.0)
            dve.memset(qst[:, :, :].bitcast(F32), 0.0)
            dve.memset(kst[:, :, :].bitcast(F32), 0.0).then_inc(s["init"], 1)
            dve.wait_ge(s["const"], 16 * CONSTS)
            dve.wait_ge(s["cls"], 16)
            dve.wait_ge(s["minus"], 16 * H)
            dve.wait_ge(s["zeroed"], 16 * E)

            def maxima(n, w, h, c, i):
                u = U_HEAD * h + 2 * c + i
                dve.wait_ge(s["p1"], n * (U_HEAD * H) + u + 1)
                dve.tensor_reduce(mxu[:, w, h, c, i:i + 1], psM[:, i, :], AX_X, ALU.max).then_inc(s["p1u"], 1)

            def row_maxima(n, w, h):
                dve.wait_ge(s["p1u"], n * (U_HEAD * H) + U_HEAD * (h + 1))
                dve.tensor_reduce(mr[:, h, :], mxu[:, w, h, :, :], AX_X, ALU.max).then_inc(s["mr"], 1)

            def class_key(n, w, h):
                dve.wait_ge(s["mr"], n * H + h + 1)
                dve.tensor_tensor(pck[:, h, :], mxu[:, w, h, :, 2], mr[:, h, :].bitcast(F32),
                                  ALU.subtract).then_inc(s["pd"], 1)

            def split_values(z, n, w, h, name):
                dve.wait_ge(s["xfull"], z.turn(name) + 1)
                dve.wait_ge(s["ut"], n * H + h + 1)
                v4 = xav.rearrange("p (i j e) -> p j i e", i=2, j=4)
                dve.tensor_tensor(U[:, w, :, h, :].rearrange("p (j i) e -> p j i e", i=2), v4[:, :, :, 0:C],
                                  Ut[:, :, h, :].rearrange("p (j i) e -> p j i e", i=2), ALU.add)
                dve.tensor_tensor(den[:, w, :, h].rearrange("p (j i) -> p j i", i=2), v4[:, :, :, C],
                                  pck[:, h, :].rearrange("p (j i) -> p j i", i=2), ALU.add).then_inc(s["xfree"], 1)

            def statistics(src, count, part):
                if part == 0 and later(count):
                    dve.wait_ge(s["ln"], count)
                for c in range(3 * part, 3 * part + 3):
                    ins = dve.bn_stats(st[:, c, :], src[:, c, :])
                if part == 2:
                    ins.then_inc(s["st"], 1)

            def prepare(z, name, link):
                j = z.n + 1
                a, w = (z.k + 1) % 4 // 2, (z.k + 1) % 2
                if name.startswith("stat1"):
                    part = "abc".index(name[5])
                    if a == 1:
                        dve.wait_ge(s["normg"], 3 * (2 * z.pair + w) + part + 1)
                    elif part == 0:
                        dve.wait_ge(s["xfree"], z.turn("e1") + 1)
                    statistics(hb[:, w] if a == 0 else G[:, w], 0 if z.start else 2 * z.n + 1, part)
                    return
                if name == "cmax":
                    dve.wait_ge(s["xfree"], z.turn("cc") + 1)
                    link(dve.tensor_reduce(csc[:, 1:2], pc[:, :], AX_X, ALU.max))
                    link(dve.tensor_tensor(csc[:, 5:6], csc[:, 1:2], csc[:, 0:1], ALU.max))
                    dve.tensor_scalar(csc[:, 2:3], csc[:, 5:6], -SCALE, None, ALU.mult).then_inc(s["cm"], 1)
                    return
                dve.wait_ge(s["xfull"], z.turn(name) + 1)
                if name in ("e0", "e1"):
                    i = int(name[1])
                    if i == 0:
                        if later(z.pair) or z.k == 3:
                            dve.wait_ge(s["res"], 2 * z.pair + 1 if z.k == 3 else 2 * z.pair)
                        dve.tensor_copy(hb[:, w, 0, :], clst[:, :])
                    dve.tensor_tensor(hb[:, w, 1 + 4 * i:5 + 4 * i, :], x4, pe_t[:, 4 * i:4 * i + 4, :],
                                      ALU.add).then_inc(s["xfree"], 1)
                elif name == "qc":
                    dve.tensor_scalar(qkc[:, 0:1], psX[:, 0:1], bq[:, 0:1] if a == 0 else 0.0, None, ALU.add)
                    ins = dve.tensor_scalar(qkc[:, 1:2], psX[:, 1:2], bk[:, 0:1] if a == 0 else 0.0, None, ALU.add)
                    ins.then_inc(s["xfree"], 1)
                    dve.wait_ge(s["xfree"], z.turn(name) + 1)
                    dve.tensor_scalar(bd[:, 0, :], headmask[:, :], qkc[:, 0:1], None, ALU.mult)
                    link(dve.tensor_scalar(bd[:, 1, :], headmask[:, :], qkc[:, 1:2], None, ALU.mult))
                    link(dve.tensor_copy(bdp[:, :, 0, :], bd[:, :, :]))
                    dve.tensor_tensor(bdp[:, :, 1, :], bd[:, :, :], bdp[:, :, 0, :].bitcast(F32),
                                      ALU.subtract).then_inc(s["bd"], 1)
                elif name in ("q0", "q1", "k0", "k1"):
                    i = int(name[1])
                    cs = slice(512 * i, 512 * i + 512)
                    hi, lo, bias = (qh, ql, bq) if name[0] == "q" else (kh, kl, bk)
                    dve.wait_ge(s["hi"], 4 * j + (1 if name[0] == "q" else 3) + i)
                    dve.scalar_tensor_tensor(lo[:, cs], psX[:, :], bias[:, 0:1] if a == 0 else 0.0,
                                             hi[:, cs].bitcast(F32), ALU.add, ALU.subtract).then_inc(s["xfree"], 1)
                elif name == "ck":
                    dve.tensor_reduce(mxu[:, w, :, :, 2], psX[:, 0:2 * NC * H].rearrange(
                        "p (c i h) -> p h c i", i=2, h=H), AX_X, ALU.add).then_inc(s["xfree"], 1)
                elif name == "cc":
                    dve.tensor_copy(csc[:, 0:1], psX[0:H, 0:1]).then_inc(s["xfree"], 1)
                elif name == "pt":
                    dve.tensor_copy(pcT[:, :, :].rearrange("p h c -> p (h c)"), xhc).then_inc(s["xfree"], 1)
                    link(dve.tensor_tensor(csc[:, 6:7], csc[:, 3:4], csc[:, 4:5], ALU.add))
                    link(dve.reciprocal(csc[:, 7:8], csc[:, 6:7]))
                elif name == "co":
                    dve.scalar_tensor_tensor(cm[:, :], vcb[0:H, w, :], csc[:, 4:5], xho, ALU.mult,
                                             ALU.add).then_inc(s["xfree"], 1)
                    dve.wait_ge(s["xfree"], z.turn(name) + 1)
                    dve.scalar_tensor_tensor(cm[:, :], cm[:, :], csc[:, 7:8], headmaskT[:, :], ALU.mult,
                                             ALU.mult).then_inc(s["cmk"], 1)

            def finish(z, name):
                a, w = (z.k - 1) % 4 // 2, (z.k - 1) % 2
                if name == "ctxa":
                    dve.wait_ge(s["xfree"], z.turn("tv7") + 1)
                    dve.reciprocal(den[:, w], den[:, w]).then_inc(s["rden"], 1)
                if name in ("ctxa", "ctxb"):
                    dve.wait_ge(s["rden"], z.n)
                    cs = slice(0, 4) if name == "ctxa" else slice(4, NC)
                    u = U[:, w, cs, :, :].rearrange("p c h e -> p (c h) e")
                    dve.tensor_tensor(u, u, den[:, w, cs, :].rearrange("p c h -> p (c h)").unsqueeze(2).broadcast_to(
                        [P, 4 * H, C]), ALU.mult).then_inc(s["ctx"], 1)
                    return
                t = (hb if a == 0 else G)[:, w]
                if name.startswith("stat0"):
                    part = "abc".index(name[5])
                    dve.wait_ge(s["xfree"], z.turn("o1" if part else "o0") + 1)
                    statistics(t, 2 * z.n - (1 if isinstance(z, Outside) else 0), part)
                    return
                dve.wait_ge(s["xfull"], z.turn(name) + 1)
                if name == "oc":
                    if a == 0:
                        dve.wait_ge(s["biased"], 2 * z.pair + w + 1)
                    ins = dve.tensor_tensor(t[0:1, 0, :], xrow, t[0:1, 0, :], ALU.add)
                else:
                    cs = slice(1 + 4 * int(name[1]), 5 + 4 * int(name[1]))
                    ins = dve.tensor_tensor(t[:, cs, :], x4, t[:, cs, :], ALU.add)
                ins.then_inc(s["xfree"], 1)

            def route(z, name, link):
                b = 2 * z.pair if z.k == 3 else 2 * z.pair - 1
                if name == "rmax":
                    dve.wait_ge(s["xfree"], z.turn("lgb") + 1)
                    dve.tensor_copy(vtick[:, :], ones_f[:, :])
                    for c in range(NT):
                        ins = dve.max(mv[:, c, :], lg[:, c, :])
                    link(ins)
                    dve.tensor_tensor(rt[:, 0, :], mv[:, :, 1], mv[:, :, 0], ALU.subtract).then_inc(s["gd"], 1)
                elif name == "ridx":
                    for c in range(NT):
                        ins = dve.max_index(mi[:, c, :], mv[:, c, :], lg[:, c, :])
                    link(ins)
                elif name == "re":
                    for k in range(TOPK):
                        ins = dve.scalar_tensor_tensor(e1[:, k, :], mi[:, :, k], 1.0, valid[:, :], ALU.add, ALU.mult)
                    link(ins)
                elif name == "roh":
                    for k in range(TOPK):
                        ins = dve.tensor_tensor(oh[:, k, :, :], iota1[:, :].unsqueeze(1).broadcast_to([P, NT, E]),
                                                e1[:, k, :].unsqueeze(2).broadcast_to([P, NT, E]), ALU.is_equal)
                    link(ins)
                elif name == "rohs":
                    dve.tensor_tensor(ohs[:, :, :], oh[:, 0, :, :], oh[:, 1, :, :], ALU.add).then_inc(s["ohs"], 1)
                elif name == "rpk":
                    dve.wait_ge(s["xfree"], z.turn("posb") + 1)
                    dve.wait_ge(s["ohs"], b + 1)
                    for k in range(TOPK):
                        ins = dve.tensor_tensor(oh[:, k, :, :], oh[:, k, :, :], pos[:, :, :], ALU.mult)
                    link(ins)
                elif name == "rred":
                    link(dve.tensor_reduce(pk[:, :, :], oh[:, :, :, :], AX_X, ALU.add))
                elif name == "rout":
                    link(dve.tensor_scalar(keep[:, :, :], pk[:, :, :], float(CAP), None, ALU.is_lt))
                    for k in range(TOPK):
                        dve.tensor_tensor(rt[:, 2 + k, :], keep[:, k, :], valid[:, :], ALU.mult)
                        dve.scalar_tensor_tensor(rt[:, 4 + k, :], e1[:, k, :], float(CAP), pk[:, k, :], ALU.mult,
                                                 ALU.add)
                        ins = dve.tensor_scalar(rt[:, 6 + k, :], pk[:, k, :], float(CAP - 1), None, ALU.min)
                    link(ins)
                    for k in range(TOPK):
                        dve.tensor_scalar(rt[:, 8 + k, :], rt[:, 2 + k, :], -OUT_OF_BOUNDS, OUT_OF_BOUNDS - CAP,
                                          ALU.mult, ALU.add)
                        ins = dve.scalar_tensor_tensor(rt[:, 10 + k, :], e1[:, k, :], float(CAP), rt[:, 6 + k, :],
                                                       ALU.mult, ALU.add)
                    link(ins)
                    dve.wait_ge(s["x2f"], b + 1)
                    for k in range(TOPK):
                        dve.tensor_tensor(sidx[:, :, k], rt[:, 4 + k, :], rt[:, 8 + k, :], ALU.add)
                        ins = dve.tensor_scalar(gidx[:, bass.ds(b, 1), :, k].rearrange("p o c -> p (o c)"),
                                                rt[:, 10 + k, :], -float(CAP), 0.0, ALU.add, ALU.max)
                    ins.then_inc(s["sidx"], 1)
                    dve.wait_ge(s["ge"], b + 1)
                    link(dve.tensor_scalar(rt[:, 2, :], rt[:, 1, :], 1.0, None, ALU.add))
                    link(dve.reciprocal(rt[:, 3, :], rt[:, 2, :]))
                    dve.wait_ge(s["sidx"], b + 1)
                    link(dve.tensor_tensor(rt[:, 4, :], rt[:, 3, :], rt[:, 1, :], ALU.mult))
                    for k in range(TOPK):
                        ins = dve.tensor_tensor(gate[:, bass.ds(b, 1), :, k].rearrange("p o c -> p (o c)"),
                                                rt[:, 3 + k, :], keep[:, k, :], ALU.mult)
                    ins.then_inc(s["gated"], 1)

            DVE_PREPARE = ("stat1a", "stat1b", "stat1c", "q0", "q1", "k0", "k1", "qc", "ck", "cc", "cmax", "pt", "co")
            DVE_ROUTE = ("rmax", "ridx", "re", "roh", "rohs", "rpk", "rred", "rout")

            def dve_slot(z):
                n = z.n
                w = z.k % 2
                qlink = chain(dve, "qclink", QC_LINKS, z.n + 1)
                rlink = chain(dve, "rlink", R_LINKS, 2 * z.pair if z.k == 3 else 2 * z.pair - 1)
                for h in range(H):
                    for c in range(NC):
                        t = NC * h + c - 1
                        if h + 3 < H:
                            maxima(n, w, h + 3, c, 0)
                        elif z.nxt:
                            maxima(z.n + 1, 1 - w, h + 3 - H, c, 0)
                        if c == 0 and h + 2 < H:
                            row_maxima(n, w, h + 2)
                        elif c == 0 and z.nxt:
                            row_maxima(z.n + 1, 1 - w, h + 2 - H)
                        if c == 1 and h + 2 < H:
                            class_key(n, w, h + 2)
                        elif c == 1 and z.nxt:
                            class_key(z.n + 1, 1 - w, h + 2 - H)
                        if c == 4 and h >= 1:
                            split_values(z, n, w, h - 1, "tv%d" % (h - 1))
                        if z.prev:
                            if t == STEP["tv7"]:
                                split_values(z, z.n - 1, 1 - w, H - 1, "tv7")
                            for name in ("ctxa", "ctxb", "oc", "o0", "o1", "stat0a", "stat0b", "stat0c"):
                                if t == STEP[name]:
                                    finish(z, name)
                        if z.nxt:
                            for name in (EMBED if z.k in (3, 0) else ()) + DVE_PREPARE:
                                if t == STEP[name]:
                                    prepare(z, name, qlink)
                        if z.prev and z.k in (3, 0):
                            for name in DVE_ROUTE:
                                if t == STEP[name]:
                                    route(z, name, rlink)
                        if h + 3 < H:
                            maxima(n, w, h + 3, c, 1)
                        elif z.nxt:
                            maxima(z.n + 1, 1 - w, h + 3 - H, c, 1)

            z = Outside(-1)
            qlink = chain(dve, "qclink", QC_LINKS, 0)
            for name in EMBED + DVE_PREPARE:
                prepare(z, name, qlink)
            for h in range(3):
                for c in range(NC):
                    for i in range(2):
                        maxima(0, 0, h, c, i)
                if h < 2:
                    row_maxima(0, 0, h)
                    class_key(0, 0, h)
            slots(dve, dve_slot)
            z = Outside(2 * B)
            split_values(z, z.n - 1, 1, H - 1, "tv7")
            for name in ("ctxa", "ctxb", "oc", "o0", "o1", "stat0a", "stat0b", "stat0c"):
                finish(z, name)
            rlink = chain(dve, "rlink", R_LINKS, B - 1)
            for name in DVE_ROUTE:
                route(z, name, rlink)
            dve.wait_ge(s["gated"], B)
            dve.sem_inc(s["attended"], 1)
            dve.sem_inc(s["yo"], 2)
            dve.sem_inc(s["xt"], 1)
            with dve.Fori(0, E // 2) as g:
                for i in range(2):
                    e = 2 * g + i
                    dve.wait_ge(s["tp"], e + 3)
                    dve.wait_ge(s["hp"], FC * (e + 1))
                    dve.tensor_copy(xinT[i], psX[:, :]).then_inc(s["xt"], 1)
                for i in range(2):
                    e = 2 * g + i
                    dve.wait_ge(s["yp"], e + 3)
                    dve.wait_ge(s["bb%d" % i], 16 * g + 16)
                    dve.wait_ge(s["ysf"], e + 1)
                    dve.tensor_tensor(yout[i], psM[:, i, :].rearrange("p (c d) -> p c d", d=D),
                                      b2t[i].unsqueeze(1).broadcast_to([P, SC, D]), ALU.add).then_inc(s["yo"], 1)
            dve.sem_inc(s["fin"], 2)
            dve.wait_ge(s["yst0"], 16 * (E // 2))
            dve.wait_ge(s["yst1"], 16 * (E // 2))
            with dve.Fori(0, B // 2) as g:
                for i in range(2):
                    b = 2 * g + i
                    dve.wait_ge(s["fin"], 2 * g + 2)
                    dve.tensor_copy(gi[:, i, :, :], gidx[:, bass.ds(b, 1), :, :].rearrange("p o c k -> p (o c) k"))
                    dve.tensor_copy(gg[:, i, :, :], gate[:, bass.ds(b, 1), :, :].rearrange("p o c k -> p (o c) k")
                                    ).then_inc(s["gi"], 1)
                for i in range(2):
                    b = 2 * g + i
                    dve.wait_ge(s["gi"], b + 1)
                    dve.wait_ge(s["ga%d" % i], 16 * NT * TOPK * (g + 1))
                    dve.wait_ge(s["rs%d" % i], 16 * g + 16)
                    for c in range(NT):
                        ins = dve.scalar_tensor_tensor(fin[i][:, c, :], rows[2 * i][:, c, :], gg[:, i, c, 0:1],
                                                       fin[i][:, c, :], ALU.mult, ALU.add)
                    ins.then_inc(s["done"], 1)
                    dve.wait_ge(s["done"], b + 1)
                    for c in range(NT):
                        ins = dve.scalar_tensor_tensor(fin[i][:, c, :], rows[2 * i + 1][:, c, :], gg[:, i, c, 1:2],
                                                       fin[i][:, c, :], ALU.mult, ALU.add)
                    ins.then_inc(s["fin"], 1)

        @block.gpsimd
        def _(pool):
            pool.wait_ge(s["zeroed"], 16 * E)
            pool.memset(tick[:, :], 0.0).then_inc(s["tick"], 1)
            pool.wait_ge(s["tick"], 1)
            pool.sem_inc(s["x2f"], 1)
            pool.sem_inc(s["ysf"], 2)
            last_slot = pool.to_reg(SLOTS - 1)
            for i, value in enumerate((-0.5, 0.5, 1.0 / D, EPS, -1.0)):
                pool.memset(consts[:, i, :], value).then_inc(s["consts"], 1)
            pool.wait_ge(s["consts"], 5)
            pool.wait_ge(s["const"], 16 * CONSTS)

            def norm(count, src=None, dst=None, add=None):
                link = chain(pool, "lnlink", LN_LINKS, count)
                pool.wait_ge(s["st"], count + 1)
                v = [sm[:, i, :] for i in range(8)]
                k = [consts[:, i, :] for i in range(5)]
                pool.tensor_tensor(v[0], st[:, :, 1], st[:, :, 4], ALU.add)
                pool.tensor_tensor(v[1], st[:, :, 1], st[:, :, 4], ALU.subtract)
                link(pool.tensor_tensor(v[2], st[:, :, 2], st[:, :, 5], ALU.add))
                pool.tensor_tensor(v[6], v[0], k[1], ALU.mult)
                pool.tensor_tensor(v[3], v[1], k[1], ALU.mult)
                link(pool.tensor_tensor(v[5], v[2], k[2], ALU.mult))
                pool.tensor_tensor(v[7], v[3], v[3], ALU.mult)
                link(pool.tensor_tensor(v[0], v[5], k[3], ALU.add))
                link(pool.tensor_tensor(v[2], v[0], v[7], ALU.add))
                link(pool.tensor_tensor(v[4], v[2], k[0], ALU.pow))
                if dst is None:
                    link(pool.tensor_tensor(v[5], v[6], v[4], ALU.mult))
                    pool.tensor_tensor(v[3], v[5], k[4], ALU.mult).then_inc(s["ln"], 1)
                    return
                link(pool.tensor_tensor(dst, src, v[6].unsqueeze(2).broadcast_to([P, NT, D]), ALU.subtract))
                pool.tensor_tensor(src, src, add, ALU.add).then_inc(s["res"], 1)
                pool.tensor_tensor(dst, dst, v[4].unsqueeze(2).broadcast_to([P, NT, D]), ALU.mult
                                   ).then_inc(s["ln"], 1)

            def norm_next(z):
                a, w = (z.k + 1) % 4 // 2, (z.k + 1) % 2
                count = 0 if z.start else 2 * z.n + 1
                norm(count)
                if a == 0:
                    pool.wait_ge(s["normn"], 3 * (z.n + 1) + 3)
                    pool.tensor_tensor(hb[:, w], hb[:, w], bo[:, :].unsqueeze(1).broadcast_to([P, NT, D]),
                                       ALU.add).then_inc(s["biased"], 1)

            def norm_last(z):
                a, w = (z.k - 1) % 4 // 2, (z.k - 1) % 2
                count = 2 * z.n - (1 if isinstance(z, Outside) else 0)
                if a == 0:
                    norm(count)
                    return
                norm(count, G[:, w], x2[:, :, :], hb[:, w])

            def expert_input(z):
                b = 2 * z.pair if z.k == 3 else 2 * z.pair - 1
                count = 2 * z.n - (1 if isinstance(z, Outside) else 0)
                pool.wait_ge(s["ln"], count + 1)
                pool.tensor_tensor(x2[:, :, :], x2[:, :, :], g2[:, :].unsqueeze(1).broadcast_to([P, NT, D]),
                                   ALU.mult).then_inc(s["x2g"], 1)
                pool.wait_ge(s["x2g"], b + 1)
                pool.tensor_tensor(x2[:, :, :], x2[:, :, :], c2[:, :].unsqueeze(1).broadcast_to([P, NT, D]),
                                   ALU.add).then_inc(s["x2"], 1)

            def class_share(n, w, h):
                pool.wait_ge(s["pe"], n * H + h + 1)
                pool.tensor_tensor(Ut[:, :, h, :], vcb[:, w, C * h:C * h + C].unsqueeze(1).broadcast_to([P, NC, C]),
                                   pck[:, h, :].unsqueeze(2).broadcast_to([P, NC, C]), ALU.mult).then_inc(s["ut"], 1)

            def running(b):
                link = chain(pool, "runlink", RUN_LINKS, b)
                pool.wait_ge(s["ohs"], b + 1)
                link(pool.tensor_tensor(run[:, 0, :], run[:, NT, :], ones_bf[:, 0:E], ALU.mult))
                for c in range(NT):
                    link(pool.tensor_tensor(run[:, c + 1, :], run[:, c, :], ohs[:, c, :], ALU.add))
                pool.sem_inc(s["oh"], 1)

            def scatter(b):
                pool.wait_ge(s["sidx"], b + 1)
                pool.wait_ge(s["tick"], b + 1)
                pool.tensor_tensor(tick[:, :], tick[:, :], tick[:, :], ALU.mult).then_inc(s["tick"], 1)
                for c in range(NT):
                    for k in range(TOPK):
                        pool.indirect_dma_start(
                            out=slots_in, out_offset=bass.IndirectOffsetOnAxis(ap=sidx[:, c, k:k + 1], axis=0),
                            in_=x2[:, c, :], in_offset=None, bounds_check=last_slot,
                            oob_is_err=False).then_inc(s["scat"], 16)
                pool.wait_ge(s["scat"], 16 * NT * TOPK * b + 16 * NT * TOPK)
                pool.sem_inc(s["x2f"], 1)

            def pool_slot(z):
                n = z.n
                w = z.k % 2
                for h in range(H):
                    if h + 2 < H:
                        class_share(n, w, h + 2)
                    elif z.nxt:
                        class_share(z.n + 1, 1 - w, h + 2 - H)
                    if h == 0 and z.prev:
                        norm_last(z)
                    if h == 0 and z.nxt:
                        norm_next(z)
                    if h == 0 and z.prev and z.k in (3, 0):
                        expert_input(z)
                    if h == 5 and z.prev and z.k in (3, 0):
                        running(2 * z.pair if z.k == 3 else 2 * z.pair - 1)
                if z.prev and z.k in (3, 0):
                    scatter(2 * z.pair if z.k == 3 else 2 * z.pair - 1)
                    if z.k == 0:
                        for i in range(2):
                            pool.wait_ge(s["resd%d" % i], 16 * z.pair)

            norm_next(Outside(-1))
            for h in range(2):
                class_share(0, 0, h)
            slots(pool, pool_slot)
            norm_last(Outside(2 * B))
            expert_input(Outside(2 * B))
            running(B - 1)
            scatter(B - 1)
            with pool.Fori(0, E // 2) as g:
                for i in range(2):
                    e = 2 * g + i
                    pool.wait_ge(s["yo"], e + 3)
                    pool.dma_start(slots_out[bass.ds(e * CAP, CAP), :].rearrange("(c p) d -> p c d", p=P),
                                   yout[i]).then_inc(s["yst%d" % i], 16)
                for i in range(2):
                    pool.wait_ge(s["yst%d" % i], 16 * g + 16)
                    pool.sem_inc(s["ysf"], 1)
            pool.wait_ge(s["yst0"], 16 * (E // 2))
            pool.wait_ge(s["yst1"], 16 * (E // 2))
            with pool.Fori(0, B // 2) as g:
                for i in range(2):
                    b = 2 * g + i
                    pool.wait_ge(s["gi"], b + 1)
                    pool.wait_ge(s["fin"], 2 * g + 2)
                    pool.wait_ge(s["tick"], B + 1 + b)
                    pool.tensor_tensor(tick[:, :], tick[:, :], tick[:, :], ALU.mult).then_inc(s["tick"], 1)
                    for c in range(NT):
                        for k in range(TOPK):
                            pool.indirect_dma_start(
                                out=rows[2 * i + k][:, c, :], out_offset=None, in_=slots_out,
                                in_offset=bass.IndirectOffsetOnAxis(ap=gi[:, i, c, k:k + 1], axis=0),
                                bounds_check=last_slot, oob_is_err=False).then_inc(s["ga%d" % i], 16)


def position_encoding():
    import math
    position = np.arange(2 * S, dtype=np.float32)[:, None]
    div_term = np.exp(np.arange(0, D, 2, dtype=np.float32) * (-math.log(10000.0) / D))
    pe = np.zeros((2 * S, D), dtype=np.float32)
    pe[:, 0::2] = np.sin(position * div_term)
    pe[:, 1::2] = np.cos(position * div_term)
    return pe[:S]


def kernel(**inputs):
    import ml_dtypes
    import concourse.bacc as bacc
    from concourse.bass_utils import run_bass_kernel_spmd

    i = {k: np.asarray(v) for k, v in inputs.items()}

    def row(a):
        return a.reshape(1, -1)

    def col(a):
        return a.reshape(-1, 1)

    wqkv = i["L0_attn_qkv_w"].reshape(H, 3, C, D)
    bqkv = i["L0_attn_qkv_b"].reshape(H, 3, C)
    arrays = {
        "x": i["x"].reshape(B * S, F_IN).T,
        "cls_tok": i["cls_tok"].reshape(1, D),
        "pe": position_encoding().reshape(NC, P, D).transpose(1, 0, 2),
        "tokW": i["L0_tok_W"],
        "wq1": wqkv[:, 0].reshape(D, D).T, "wk1": wqkv[:, 1].reshape(D, D).T, "wv1": wqkv[:, 2].reshape(D, D).T,
        "bq1": col(bqkv[:, 0]), "bk1": col(bqkv[:, 1]), "bv1": col(bqkv[:, 2]),
        "wo1": i["L0_attn_out_w"].T, "bo1": row(i["L0_attn_out_b"]),
        "ln1g": col(i["L0_ffn_ln1_g"]), "ln1b": col(i["L0_ffn_ln1_b"]),
        "wq2": i["L0_ffn_wq"], "wk2": i["L0_ffn_wk"], "wv2": i["L0_ffn_wv"], "wo2": i["L0_ffn_wo"],
        "ln2g": row(i["L0_ffn_ln2_g"]), "ln2b": row(i["L0_ffn_ln2_b"]),
        "wr": i["L0_ffn_wr"],
        "w1": i["L0_ffn_w1"].reshape(E * D, F),
        "b1": i["L0_ffn_b1"].reshape(E, P, FC).transpose(1, 2, 0),
        "w2": i["L0_ffn_w2"].reshape(E * P, FC * D),
        "b2": i["L0_ffn_b2"],
        "ident_d": np.eye(P, dtype=np.float32),
        "headmask_d": np.repeat(np.eye(H, dtype=np.float32), C, axis=0),
        "headmaskT_d": np.repeat(np.eye(H, dtype=np.float32), C, axis=1),
        "lower_d": np.triu(np.ones((P, P), dtype=np.float32), 1).astype(ml_dtypes.bfloat16),
        "iota_d": np.tile(np.arange(1, E + 1, dtype=np.float32), (P, 1)),
        "valid_d": np.concatenate([np.eye(P, 1, dtype=np.float32), np.ones((P, NC), np.float32)], axis=1),
    }
    nc = bacc.Bacc("TRN2", target_bir_lowering=False, num_devices=1)
    named, args = {}, {}
    for name, a in arrays.items():
        a = np.ascontiguousarray(a)
        named["in_" + name] = a
        args[name] = nc.dram_tensor("in_" + name, a.shape, mybir.dt.from_np(a.dtype), kind="ExternalInput").ap()
    args["out"] = nc.dram_tensor("out_0", (B, S + 1, D), F32, kind="ExternalOutput").ap()
    build(nc, **args)
    r = run_bass_kernel_spmd(nc, [named], core_ids=[0])
    return r.results[0]["out_0"]
```

```python
from contextlib import ExitStack

import numpy as np

import concourse.bass as bass
from concourse import mybir

ALU = mybir.AluOpType
ACT = mybir.ActivationFunctionType
AX_X = mybir.AxisListType.X
F32 = mybir.dt.float32
F32R = mybir.dt.float32r
BF16 = mybir.dt.bfloat16
I32 = mybir.dt.int32
U32 = mybir.dt.uint32

P = 128
D = 128
H = 8
C = D // H
B = 8
S = 1024
NC = S // P
NT = NC + 1
F_IN = 29
E = 64
F = 512
FC = F // P
TOPK = 2
CAP = 2 * (B * (S + 1) * TOPK // E)
SLOTS = E * CAP
SC = CAP // P
EPS = 1e-5
SCALE = 1.0 / C ** 0.5


def later(n):
    return not (isinstance(n, int) and n == 0)

OUT_OF_BOUNDS = float(1 << 20)
HALF = 64
GRP = 3 * C

STEP = {
    "tv7": 2, "ct0": 3, "ct1": 4, "oc": 5, "o0": 6, "o1": 7,
    "stat0a": 7, "stat0b": 8, "stat0c": 9, "norm0a": 13, "norm0b": 14, "norm0c": 15,
    "e0": 14, "e1": 15, "stat1a": 16, "stat1b": 17, "stat1c": 18, "norm1a": 22, "norm1b": 23, "norm1c": 25,
    "nt0": 24, "nt1": 26, "q0": 28, "q1": 29, "k0": 31, "k1": 32, "ntc": 34, "qc": 36, "ck": 38,
    "cc": 39, "vc": 47, "v0": 48, "v1": 50,
    "cq0": 52, "cmaxa": 52, "cq1": 53, "cmaxb": 53, "cexp": 55, "pt": 60, "co": 61, "cf": 63,
    "xa": 40, "xb": 42, "xc": 44, "lga": 45, "lgb": 46, "rmaxa": 46, "rmaxb": 47, "rexp": 50, "ridxa": 48,
    "ridxb": 49, "roha": 50, "rohb": 51, "posa": 55, "posb": 56, "rred": 58, "routa": 59, "routb": 60, "routc": 61,
}
FINISH = ("tv7", "ct0", "ct1", "oc", "o0", "o1")
EMBED = ("e0", "e1")
PREPARE = ("nt0", "nt1", "q0", "q1", "k0", "k1", "ntc", "qc", "ck", "cc", "vc", "v0", "v1",
           "cq0", "cq1", "pt", "co", "cf")
ROUTE = ("xa", "xb", "xc", "lga", "lgb", "posa", "posb")


def turns(k, prev, nxt):
    names = []
    if prev:
        names += FINISH + (ROUTE if k in (3, 0) else ())
    if nxt:
        names += (EMBED if k in (3, 0) else ()) + PREPARE
    order = [(STEP[n], 1, n) for n in names]
    order += [(NC * h + 1, 0, "tm%d" % (h + 2)) for h in range(H) if nxt or h + 2 < H]
    order += [(NC * h + 3, 0, "tv%d" % (h - 1)) for h in range(1, H)]
    rank = {n: i for i, n in enumerate(FINISH + EMBED + PREPARE + ROUTE)}
    order.sort(key=lambda o: (o[0], o[1], rank.get(o[2], 0)))
    return [o[2] for o in order]


PROLOGUE = list(EMBED + PREPARE) + ["tm0", "tm1"]
FIRST = turns(0, False, True)
CYCLE = [turns(k, True, True) for k in range(4)]
LAST = turns(3, True, False)
TAIL = list(FINISH + ROUTE)


class Slot:

    def __init__(self, pair, k, prev=True, nxt=True):
        self.start = False
        self.pair, self.k, self.prev, self.nxt = pair, k, prev, nxt
        self.n = 4 * pair + k
        self.names = CYCLE[k] if prev and nxt else LAST if prev else FIRST
        before = sum(len(c) for c in CYCLE)
        if prev:
            self.base = before * pair + (sum(len(c) for c in CYCLE[:k]) + len(PROLOGUE) + len(FIRST) - len(CYCLE[0]))
        else:
            self.base = len(PROLOGUE)

    def turn(self, name):
        return self.base + self.names.index(name)


class Outside(Slot):

    def __init__(self, n):
        self.n, self.start = n, n < 0
        self.names = PROLOGUE if n < 0 else TAIL
        self.base = 0 if n < 0 else Slot(B // 2 - 1, 3).base + len(LAST)
        self.pair, self.k = (0, -1) if n < 0 else (B // 2, 0)
        self.prev, self.nxt = n >= 0, n < 0


def build(nc, x, cls_tok, pe, tokW, wq1, wk1, wv1, bq1, bk1, bv1, wo1, bo1,
          ln1g, ln1b, wq2, wk2, wv2, wo2, ln2g, ln2b, wr, w1, b1, w2, b2,
          ident_d, headmask_d, headmaskT_d, lower_d, iota_d, valid_d, out):
    ctx = ExitStack()
    with ctx:
        def sb(name, shape, dt=F32):
            return ctx.enter_context(nc.sbuf_tensor(name, shape, dt))

        def psum(name, shape):
            return ctx.enter_context(nc.psum_tensor(name, shape, F32))

        def sem(name):
            return ctx.enter_context(nc.semaphore(name))

        slots_in = nc.dram_tensor("slots_in", [SLOTS, D], F32).ap()
        stream = nc.dram_tensor("stream", [B * NT * P, D], F32).ap()
        slots_out = nc.dram_tensor("slots_out", [SLOTS, D], F32).ap()

        ident = sb("ident", [P, P])
        headmask = sb("headmask", [P, H])
        headmaskT = sb("headmaskT", [P, P])
        lower = sb("lower", [P, P], BF16)
        ones_bf = sb("ones_bf", [P, P], BF16)
        ones_f = sb("ones_f", [P, 1])
        iota1 = sb("iota1", [P, E])
        valid = sb("valid", [P, NT])
        pe_t = sb("pe_t", [P, NC, D])
        tokw = sb("tokw", [F_IN, D])
        wq = sb("wq", [P, 2, D])
        wk = sb("wk", [P, 2, D])
        wv = sb("wv", [P, 2, D])
        wo = sb("wo", [P, 2, D])
        bq = sb("bq", [P, 1])
        bk = sb("bk", [P, 1])
        bv = sb("bv", [P, 1])
        bo = sb("bo", [P, D])
        g1 = sb("g1", [P, 1])
        c1 = sb("c1", [P, 1])
        g2 = sb("g2", [P, D])
        c2 = sb("c2", [P, D])
        wrt = sb("wrt", [P, E])
        b1t = sb("b1t", [P, FC, E])
        clst = sb("clst", [P, D])

        gidx = sb("gidx", [P, B, NT, TOPK], U32)
        gate = sb("gate", [P, B, NT, TOPK])

        xT = sb("xT", [F_IN, S])
        hb = sb("hb", [P, 2, NT, D])
        G = sb("G", [P, 2, NT, D])
        N = sb("N", [P, NT, D])
        st = sb("st", [P, NT, 6])
        sm = sb("sm", [P, 8, NT])
        nT = sb("nT", [P, NT, P])
        qh = sb("qh", [P, S], F32R)
        ql = sb("ql", [P, S], F32R)
        kh = sb("kh", [P, S], F32R)
        kl = sb("kl", [P, S], F32R)
        qst = sb("qst", [P, H // 2, S], F32R)
        kst = sb("kst", [P, H, S], F32R)
        zrow = sb("zrow", [NC, P])
        vt = sb("vt", [P, 2, NC, H, 32])
        vcb = sb("vcb", [P, 2, D])
        qkc = sb("qkc", [P, 2])
        bd = sb("bd", [P, 2, H])
        bdp = sb("bdp", [P, 2, 2, H], F32R)
        mxu = sb("mxu", [P, 2, H, NC, 3])
        mr = sb("mr", [P, H, NC], F32R)
        mT = sb("mT", [NC, 2, P], F32R)
        pck = sb("pck", [P, H, NC])
        pr = sb("pr", [P, 4, S])
        avs = sb("avs", [P, 2, 256])
        U = sb("U", [P, 2, NC, H, C])
        Ut = sb("Ut", [P, NC, H, C])
        den = sb("den", [P, 2, NC, H])
        clc = sb("clc", [P, 2])
        ctxT = sb("ctxT", [P, NT, P])
        csc = sb("csc", [H, 10])
        pc = sb("pc", [H, S])
        pcs = sb("pcs", [P, P])
        pcT = sb("pcT", [P, NC, 32])
        cm = sb("cm", [P, D])
        cmv = sb("cmv", [H, D])
        crd = sb("crd", [P, 1])
        x2 = sb("x2", [P, NT, D])
        lg = sb("lg", [P, NT, E])
        mv = sb("mv", [P, NT, 8])
        mi = sb("mi", [P, NT, 8], U32)
        e1 = sb("e1", [P, TOPK, NT])
        oh = sb("oh", [P, TOPK, NT, E])
        ohs = sb("ohs", [P, NT, E], BF16)
        run = sb("run", [P, NT + 1, E], BF16)
        pos = sb("pos", [P, NT, E])
        pk = sb("pk", [P, TOPK, NT])
        keep = sb("keep", [P, TOPK, NT])
        rt = sb("rt", [P, 12, NT])
        sidx = sb("sidx", [P, NT, TOPK], U32)

        w1t = [nT[:, 0:4, :].rearrange("p c s -> p (c s)"), nT[:, 4:8, :].rearrange("p c s -> p (c s)")]
        w2t = [ctxT[:, 0:4, :], ctxT[:, 4:8, :]]
        xin = [N[:, 0:4, :], N[:, 4:8, :]]
        xh, xl = ([t[:, 512 * i:512 * i + 512] for i in range(2)] for t in (kh, kl))
        w1h, w1l = ([t[:, 512 * i:512 * i + 512] for i in range(2)] for t in (qh, ql))
        hid = [pr[:, 0:2, :].rearrange("p a (b s) -> p (a b) s", b=2),
               pr[:, 2:4, :].rearrange("p a (b s) -> p (a b) s", b=2)]
        b2t = [x2[:, 0, :], x2[:, 1, :]]
        yout = [hb[:, 0, 0:4, :], hb[:, 1, 0:4, :]]
        rows = [N, G[:, 0], x2, nT]
        fin = [hb[:, 0], hb[:, 1], ctxT[:, :, :],
               oh[:, :, :, :].rearrange("p k c e -> p (k c e)").rearrange("p (c d) -> p c d", d=D)]
        vtick = sb("vtick", [P, 1])
        consts = sb("consts", [P, 5, NT])
        tick = sb("tick", [P, 1])
        gi = sb("gi", [P, 4, NT, TOPK], U32)
        gg = sb("gg", [P, 4, NT, TOPK])

        ps = psum("ps", [P, 6, 512])
        psV = psum("psV", [P, 512])
        psX = psum("psX", [P, 512])
        x4 = psX[:, :].rearrange("p (c d) -> p c d", d=D)
        xcol = psX[:, 0:1]
        xhc = psX[:, 0:NC * H]
        xrow = psX[0:1, 0:D]
        xm = psX[0:NC, 0:P]
        xav = psX[:, 0:2 * P]

        names = """const clear minus cls init zeroed attended x
            xfull xfree stk0 stk1 stk2 stk3 mrow0 mrow1 p1 p1u mr p2 exp av avs pd pe ut
            st ln lnlink biased hi qclink ohr ohp bd cm ce ctx x2 gd ge rlink consts ohs runlink oh scat sidx gated rden x2g pcs normg normn x2f res resd0 resd1
            wa0 wa1 wb0 wb1 bb0 bb1 xi0 xi1 tp xt xh wh ws hp gl yp yo yst0 yst1 done
            tick gi ga0 ga1 rs0 rs1 rs2 rs3 fin stored out0 out1 out2 out3 ysf""".split()
        s = {n: sem("s_" + n) for n in names}

        LN_LINKS, QC_LINKS, R_LINKS, RUN_LINKS = 6, 7, 10, 10
        CONSTS = 26
        STK = 16 * (12 + 2)
        U_HEAD = 2 * NC
        T_ATT = H * NC
        UNITS = 2 * T_ATT
        TAKEN_0 = 1024

        def bank_free(u):
            before = u - 3 if u >= 3 else max(v for v in range(UNITS) if v % 3 == u) - UNITS
            return before + 1


        def slots(eng, slot):
            slot(Slot(0, 0, prev=False))
            with eng.Fori(0, B // 2 - 1) as r:
                for k in (1, 2, 3):
                    slot(Slot(r, k))
                slot(Slot(r + 1, 0))
            for k in (1, 2, 3):
                slot(Slot(B // 2 - 1, k, nxt=k < 3))

        def chain(eng, name, links, count):
            seen = [0]

            def link(ins):
                seen[0] += 1
                assert seen[0] <= links
                ins.then_inc(s[name], 1)
                eng.wait_ge(s[name], links * count + seen[0])
            return link

        block = ctx.enter_context(nc.Block())

        @block.sync
        def _(sp):
            loads = [(ident[:, :], ident_d), (headmask[:, :], headmask_d), (headmaskT[:, :], headmaskT_d),
                     (iota1[:, :], iota_d), (valid[:, :], valid_d), (pe_t[:, :, :], pe), (tokw[:, :], tokW),
                     (wq[:, 0, :], wq1), (wk[:, 0, :], wk1), (wv[:, 0, :], wv1), (wo[:, 0, :], wo1),
                     (wq[:, 1, :], wq2), (wk[:, 1, :], wk2), (wv[:, 1, :], wv2), (wo[:, 1, :], wo2),
                     (bq[:, :], bq1), (bk[:, :], bk1), (bv[:, :], bv1),
                     (bo[:, :], bo1.broadcast_to([P, D])), (g1[:, :], ln1g), (c1[:, :], ln1b),
                     (g2[:, :], ln2g.broadcast_to([P, D])), (c2[:, :], ln2b.broadcast_to([P, D])),
                     (wrt[:, :], wr), (lower[:, :], lower_d), (b1t[:, :, :], b1)]
            assert len(loads) == CONSTS
            for dst, src in loads:
                sp.dma_start(dst, src).then_inc(s["const"], 16)
            sp.wait_ge(s["clear"], 1)
            sp.dma_start(clst[0:1, :], cls_tok).then_inc(s["cls"], 16)
            sp.dma_start(xT[:, :], x[:, 0:S]).then_inc(s["x"], 16)
            sp.wait_ge(s["init"], 3)
            for h in range(H):
                p0 = HALF * (h % 2) + GRP
                sp.dma_start(kst[p0:p0 + 1, h, :].bitcast(F32), mT[:, 0, :].bitcast(F32)).then_inc(s["minus"], 16)

            def load_tokens(b):
                sp.dma_start(xT[:, :], x[:, bass.ds(b * S, S)]).then_inc(s["x"], 16)

            def stack(p, z=None):
                for p0 in (GRP, HALF + GRP):
                    sp.dma_start(qst[p0:p0 + 1, p, :].bitcast(F32), zrow[:, :]).then_inc(s["stk%d" % p], 16)
                if z is not None:
                    sp.wait_ge(s["xfree"], z.turn("k1") + 1)
                for h in (2 * p, 2 * p + 1):
                    for src, dst, parts in ((qh, qst[:, p, :], (0, 1)), (ql, qst[:, p, :], (2,)),
                                            (kh, kst[:, h, :], (0, 2)), (kl, kst[:, h, :], (1,))):
                        for r in parts:
                            p0 = HALF * (h % 2) + C * r
                            sp.dma_start(dst[p0:p0 + C, :].bitcast(F32),
                                         src[C * h:C * h + C, :].bitcast(F32)).then_inc(s["stk%d" % p], 16)

            def maxima_rows(h):
                for i in range(2):
                    p0 = HALF * i + GRP
                    sp.dma_start(qst[p0:p0 + 1, h // 2, :].bitcast(F32),
                                 mT[:, i, :].bitcast(F32)).then_inc(s["mrow%d" % i], 16)

            def sp_slot(z):
                if z.nxt and z.k in (3, 0):
                    load_tokens(2 * (z.pair + 1) if z.k == 3 else 2 * z.pair + 1)
                if z.prev:
                    sp.wait_ge(s["p2"], UNITS * z.n)
                    stack(3)
                sp.wait_ge(s["xfree"], z.turn("tm3") + 1)
                maxima_rows(2)
                if z.prev and z.k in (3, 0):
                    b = 2 * z.pair if z.k == 3 else 2 * z.pair - 1
                    sp.wait_ge(s["res"], b + 1)
                    sp.dma_start(stream[bass.ds(b * NT * P, NT * P), :].rearrange("(c p) d -> p c d", p=P),
                                 G[:, (z.k + 1) % 2, :, :]).then_inc(s["resd%d" % ((z.k + 1) % 2)], 16)
                sp.wait_ge(s["xfree"], z.turn("tm5") + 1)
                maxima_rows(4)
                if z.nxt:
                    for p in range(2):
                        sp.wait_ge(s["p2"], UNITS * z.n + 4 * NC * (p + 1))
                        stack(p, z)
                sp.wait_ge(s["xfree"], z.turn("tm7") + 1)
                maxima_rows(6)
                if z.nxt:
                    sp.wait_ge(s["p2"], UNITS * z.n + 12 * NC)
                    stack(2)
                    spread_class(z.n + 1)
                    sp.wait_ge(s["xfree"], z.turn("tm9") + 1)
                    maxima_rows(0)

            def spread_class(j):
                sp.wait_ge(s["ce"], j + 1)
                sp.dma_start(pcs[0:H * NC, :], pc[:, :]).then_inc(s["pcs"], 16)

            z = Outside(-1)
            sp.wait_ge(s["xfree"], z.turn("k1") + 1)
            for p in range(4):
                stack(p)
                if p == 0:
                    spread_class(0)
            sp.wait_ge(s["xfree"], z.turn("tm1") + 1)
            maxima_rows(0)
            slots(sp, sp_slot)
            sp.wait_ge(s["res"], B)
            sp.dma_start(stream[(B - 1) * NT * P:, :].rearrange("(c p) d -> p c d", p=P),
                         G[:, 1, :, :]).then_inc(s["resd1"], 16)
            sp.wait_ge(s["resd0"], 16 * (B // 2))
            sp.wait_ge(s["resd1"], 16 * (B // 2))
            sp.wait_ge(s["attended"], 1)
            sp.wait_ge(s["scat"], 16 * B * NT * TOPK)
            with sp.Fori(0, E // 2) as g:
                for i in range(2):
                    e = 2 * g + i
                    sp.wait_ge(s["tp"], e + 1)
                    sp.dma_start(xin[i], slots_in[bass.ds(e * CAP, CAP), :].rearrange("(c p) d -> p c d", p=P)
                                 ).then_inc(s["xi%d" % i], 16)
                    sp.wait_ge(s["ws"], e + 1)
                    sp.dma_start(w1t[i], w1[bass.ds(e * D, D), :]).then_inc(s["wa%d" % i], 16)
                for i in range(2):
                    e = 2 * g + i
                    sp.wait_ge(s["yp"], e + 1)
                    sp.wait_ge(s["yo"], e + 1)
                    sp.dma_start(w2t[i], w2[bass.ds(e * P, P), :].rearrange("p (f d) -> p f d", d=D)).then_inc(
                        s["wb%d" % i], 16)
                    sp.dma_start(b2t[i], b2[bass.ds(e, 1), :].broadcast_to([P, D])).then_inc(s["bb%d" % i], 16)
            sp.wait_ge(s["yst0"], 16 * (E // 2))
            sp.wait_ge(s["yst1"], 16 * (E // 2))

            def load_stream(b, i):
                sp.dma_start(fin[i], stream[bass.ds(b * NT * P, NT * P), :].rearrange("(c p) d -> p c d", p=P)
                             ).then_inc(s["rs%d" % i], 16)

            with sp.Fori(0, B // 4) as g:
                for m in range(4):
                    load_stream(4 * g + m, m)
                for m in range(4):
                    b = 4 * g + m
                    sp.wait_ge(s["fin"], b + 3)
                    sp.dma_start(out[bass.ds(b, 1), 1:S + 1, :].rearrange("o (c p) d -> p (o c) d", p=P),
                                 fin[m][:, 1:NT, :]).then_inc(s["out%d" % m], 16)
                    sp.dma_start(out[bass.ds(b, 1), 0, :], fin[m][0:1, 0, :]).then_inc(s["out%d" % m], 16)
                for m in range(4):
                    sp.wait_ge(s["out%d" % m], 32 * g + 32)
                    sp.sem_inc(s["stored"], 1)

        @block.tensor
        def _(pe_):
            pe_.wait_ge(s["const"], 16 * CONSTS)
            pe_.wait_ge(s["init"], 3)

            def turn(z, name):
                v = z.turn(name)
                if later(v):
                    pe_.wait_ge(s["xfree"], v)

            def maxima(n, h, c, i):
                if h % 2 == 0 and c == 0 and i == 0:
                    pe_.wait_ge(s["stk%d" % (h // 2)], STK * (n + 1))
                u = U_HEAD * h + 2 * c + i
                if u >= 3 or later(n):
                    pe_.wait_ge(s["p1u"], UNITS * n + (TAKEN_0 + bank_free(u)))
                pe_.matmul(ps[:, 3 + u % 3, :], qst[:, h // 2, c * P:(c + 1) * P], kst[:, h, 512 * i:512 * i + 512],
                           start=True, stop=True).then_inc(s["p1"], 1)

            def turn_maxima(z, n, h, name):
                turn(z, name)
                pe_.wait_ge(s["mr"], n * H + h + 1)
                pe_.transpose(xm, mr[:, h, :].bitcast(F32), ident[:, :]).then_inc(s["xfull"], 1)

            def scores(n, h, c, i):
                u = U_HEAD * h + 2 * c + i
                if c == 0 and i == 0 and h % 2 == 0:
                    for r in range(2):
                        pe_.wait_ge(s["mrow%d" % r], 16 * (n * (H // 2) + h // 2 + 1))
                if u >= 3 or later(n):
                    pe_.wait_ge(s["exp"], UNITS * n + bank_free(u))
                pe_.matmul(ps[:, u % 3, :], kst[:, h, c * P:(c + 1) * P],
                           qst[:, h // 2, 512 * i:512 * i + 512], start=True, stop=True).then_inc(s["p2"], 1)

            def values(n, w, h, c):
                t = NC * h + c
                pe_.wait_ge(s["exp"], UNITS * n + 2 * t + 2)
                if c == 0 and (h >= 1 or later(n)):
                    pe_.wait_ge(s["avs"], n * H + h)
                for j in range(4):
                    mm = pe_.matmul(psV[32 * j:32 * j + 32, 0:256], vt[:, w, c, h, :],
                                    pr[:, t % 4, 256 * j:256 * j + 256], start=(c == 0), stop=(c == NC - 1))
                mm.then_inc(s["av"], 1)

            def turn_values(z, n, h, name):
                turn(z, name)
                pe_.wait_ge(s["avs"], n * H + h + 1)
                pe_.transpose(xav[:, 0:P], avs[:, h % 2, 0:P], ident[:, :])
                pe_.transpose(xav[:, P:2 * P], avs[:, h % 2, P:2 * P], ident[:, :]).then_inc(s["xfull"], 1)

            def prepare(z, name):
                j = z.n + 1
                a, w = (z.k + 1) % 4 // 2, (z.k + 1) % 2
                turn(z, name)
                if name in ("e0", "e1"):
                    i = int(name[1])
                    if i == 0:
                        pe_.wait_ge(s["x"], 16 * (2 * (z.pair + 1 if z.k == 3 else z.pair) + w + 1))
                    for c in range(4):
                        mm = pe_.matmul(x4[:, c, :], xT[:, (4 * i + c) * P:(4 * i + c + 1) * P], tokw[:, :],
                                        start=True, stop=True)
                elif name in ("nt0", "nt1"):
                    i = int(name[2])
                    pe_.wait_ge(s["normn"], 3 * j + 2 + i)
                    for c in range(4):
                        mm = pe_.transpose(x4[:, c, :], N[:, 1 + 4 * i + c, :], ident[:, :])
                elif name == "ntc":
                    mm = pe_.transpose(psX[:, 0:P], N[:, 0, :], ident[:, :])
                elif name == "qc":
                    pe_.matmul(psX[:, 0:1], wq[:, a, :], nT[:, 0, 0:1], start=True, stop=True)
                    mm = pe_.matmul(psX[:, 1:2], wk[:, a, :], nT[:, 0, 0:1], start=True, stop=True)
                elif name in ("q0", "q1", "k0", "k1"):
                    i = int(name[1])
                    mm = pe_.matmul(psX[:, :], (wq if name[0] == "q" else wk)[:, a, :],
                                    nT[:, 1 + 4 * i:5 + 4 * i, :].rearrange("p c s -> p (c s)"),
                                    start=True, stop=True)
                elif name == "ck":
                    pe_.wait_ge(s["bd"], j + 1)
                    for c in range(NC):
                        o = psX[:, 2 * c * H:2 * (c + 1) * H]
                        cs = slice(c * P, (c + 1) * P)
                        pe_.matmul(o, qh[:, cs], bdp[:, 1, :, :].rearrange("p i h -> p (i h)"), start=True,
                                   stop=False)
                        mm = pe_.matmul(o, ql[:, cs], bdp[:, 1, :, :].rearrange("p i h -> p (i h)"), start=False,
                                        stop=True)
                elif name in ("v0", "v1"):
                    for c in range(4):
                        mm = pe_.matmul(x4[:, c, :], nT[:, 1 + 4 * int(name[1]) + c, :], wv[:, a, :],
                                        start=True, stop=True)
                elif name == "vc":
                    mm = pe_.matmul(psX[:, 0:D], nT[:, 0, 0:1].broadcast_to([P, P]), wv[:, a, :], start=True,
                                    stop=True)
                elif name in ("cq0", "cq1"):
                    i = int(name[2])
                    cs = slice(512 * i, 512 * i + 512)
                    pe_.matmul(psX[0:H, :], bdp[:, 0, 0, :], kh[:, cs], start=True, stop=False)
                    pe_.matmul(psX[0:H, :], bdp[:, 0, 0, :], kl[:, cs], start=False, stop=False)
                    mm = pe_.matmul(psX[0:H, :], bdp[:, 0, 1, :], kh[:, cs], start=False, stop=True)
                elif name == "cc":
                    mm = pe_.matmul(psX[0:H, 0:1], bd[:, 0, :], qkc[:, 1:2], start=True, stop=True)
                elif name == "pt":
                    pe_.wait_ge(s["pcs"], 16 * (j + 1))
                    mm = pe_.transpose(psX[:, 0:P], pcs[:, :], ident[:, :])
                elif name == "co":
                    for r in range(2):
                        for q in range(4):
                            mm = pe_.matmul(psX[32 * q:32 * q + 32, 0:D], pcT[:, 4 * r + q, :],
                                            vt[:, w, 4 * r + q, :, 0:C], start=(r == 0), stop=(r == 1))
                elif name == "cf":
                    pe_.matmul(xcol, cm[:, :], crd[:, :], start=True, stop=False)
                    mm = pe_.matmul(xcol, cmv[:, :], crd[0:H, :], start=False, stop=True)
                mm.then_inc(s["xfull"], 1)

            def finish(z, name):
                a, w = (z.k - 1) % 4 // 2, (z.k - 1) % 2
                turn(z, name)
                if name in ("ct0", "ct1"):
                    i = int(name[2])
                    pe_.wait_ge(s["ctx"], H * z.n)
                    for c in range(4):
                        mm = pe_.transpose(x4[:, c, :], U[:, w, 4 * i + c, :, :].rearrange("p h c -> p (h c)"),
                                           ident[:, :])
                elif name == "oc":
                    mm = pe_.matmul(xrow, clc[:, w:w + 1], wo[:, a, :], start=True, stop=True)
                elif name in ("o0", "o1"):
                    for c in range(4):
                        mm = pe_.matmul(x4[:, c, :], ctxT[:, 1 + 4 * int(name[1]) + c, :], wo[:, a, :],
                                        start=True, stop=True)
                mm.then_inc(s["xfull"], 1)

            def route(z, name):
                b = 2 * z.pair if z.k == 3 else 2 * z.pair - 1
                turn(z, name)
                if name in ("xa", "xb"):
                    if name == "xa":
                        pe_.wait_ge(s["x2"], b + 1)
                    for c in range(4):
                        mm = pe_.transpose(x4[:, c, :], x2[:, (1 if name == "xa" else 5) + c, :], ident[:, :])
                elif name == "xc":
                    mm = pe_.transpose(psX[:, 0:P], x2[:, 0, :], ident[:, :])
                elif name == "lga":
                    for c in range(NC):
                        mm = pe_.matmul(psX[:, c * E:(c + 1) * E], ctxT[:, 1 + c, :], wrt[:, :], start=True, stop=True)
                elif name == "lgb":
                    mm = pe_.matmul(psX[:, 0:E], ctxT[:, 0, :], wrt[:, :], start=True, stop=True)
                elif name in ("posa", "posb"):
                    if name == "posa":
                        pe_.wait_ge(s["oh"], b + 1)
                    for i, c in enumerate(range(1, NT) if name == "posa" else (0,)):
                        o = psX[:, i * E:(i + 1) * E]
                        pe_.matmul(o, lower[:, :], ohs[:, c, :], start=True, stop=False)
                        mm = pe_.matmul(o, ones_bf[:, :], run[:, c, :], start=False, stop=True)
                mm.then_inc(s["xfull"], 1)

            def pe_slot(z):
                n = z.n
                w = z.k % 2
                for h in range(H):
                    for c in range(NC):
                        t = NC * h + c
                        for i in range(2):
                            if h + 3 < H:
                                maxima(n, h + 3, c, i)
                            elif z.nxt:
                                maxima(z.n + 1, h + 3 - H, c, i)
                            scores(n, h, c, i)
                        if c >= 1:
                            values(n, w, h, c - 1)
                        elif h >= 1:
                            values(n, w, h - 1, NC - 1)
                        elif z.prev:
                            values(z.n - 1, 1 - w, H - 1, NC - 1)
                        if c == 1 and h + 2 < H:
                            turn_maxima(z, n, h + 2, "tm%d" % (h + 2))
                        elif c == 1 and z.nxt:
                            turn_maxima(z, z.n + 1, h + 2 - H, "tm%d" % (h + 2))
                        if c == 3 and h >= 1:
                            turn_values(z, n, h - 1, "tv%d" % (h - 1))
                        if z.prev and t == STEP["tv7"]:
                            turn_values(z, z.n - 1, H - 1, "tv7")
                        for name in FINISH[1:]:
                            if z.prev and t == STEP[name]:
                                finish(z, name)
                        for name in EMBED + PREPARE:
                            if name in z.names and t == STEP[name]:
                                prepare(z, name)
                        for name in ROUTE:
                            if name in z.names and t == STEP[name]:
                                route(z, name)

            z = Outside(-1)
            for name in EMBED + PREPARE:
                prepare(z, name)
            pe_.wait_ge(s["minus"], 16 * H)
            for h in range(3):
                for c in range(NC):
                    for i in range(2):
                        maxima(0, h, c, i)
                if h < 2:
                    turn_maxima(z, 0, h, "tm%d" % h)
            slots(pe_, pe_slot)
            z = Outside(2 * B)
            values(z.n - 1, 1, H - 1, NC - 1)
            turn_values(z, z.n - 1, H - 1, "tv7")
            for name in FINISH[1:]:
                finish(z, name)
            for name in ROUTE:
                route(z, name)
            pe_.wait_ge(s["attended"], 1)

            pe_.sem_inc(s["hp"], 2 * FC)
            pe_.sem_inc(s["tp"], 2)
            pe_.sem_inc(s["yp"], 2)

            def turn_slots(e, g, i):
                pe_.wait_ge(s["xi%d" % i], 16 * g + 16)
                pe_.wait_ge(s["xt"], e + 1)
                for c in range(SC):
                    mm = pe_.transpose(psX[:, c * P:(c + 1) * P], xin[i][:, c, :], ident[:, :])
                mm.then_inc(s["tp"], 1)

            def up(e, g, i):
                pe_.wait_ge(s["xt"], e + 2)
                pe_.wait_ge(s["ws"], e + 3)
                for f in range(FC):
                    pe_.wait_ge(s["gl"], FC * e + f + 1)
                    pe_.matmul(ps[:, f, :], w1h[i][:, f:F:FC], xh[i], start=True, stop=False)
                    pe_.matmul(ps[:, f, :], w1l[i][:, f:F:FC], xh[i], start=False, stop=False)
                    pe_.matmul(ps[:, f, :], w1h[i][:, f:F:FC], xl[i], start=False, stop=True).then_inc(s["hp"], 1)

            def down(e, g, i):
                pe_.wait_ge(s["gl"], FC * (e + 2))
                pe_.wait_ge(s["wb%d" % i], 16 * g + 16)
                pe_.wait_ge(s["yo"], e + 1)
                for c in range(SC):
                    for f in range(FC):
                        mm = pe_.matmul(ps[:, 4 + i, c * P:(c + 1) * P], hid[i][:, f, c * P:(c + 1) * P],
                                        w2t[i][:, f, :], start=(f == 0), stop=(f == FC - 1))
                mm.then_inc(s["yp"], 1)

            turn_slots(0, 0, 0)
            turn_slots(1, 0, 1)
            up(0, 0, 0)
            up(1, 0, 1)
            down(0, 0, 0)
            with pe_.Fori(1, E // 2) as g:
                turn_slots(2 * g, g, 0)
                down(2 * g - 1, g - 1, 1)
                turn_slots(2 * g + 1, g, 1)
                up(2 * g, g, 0)
                up(2 * g + 1, g, 1)
                down(2 * g, g, 0)
            down(E - 1, E // 2 - 1, 1)

        @block.scalar
        def _(act):
            act.wait_ge(s["const"], 16 * CONSTS)

            def class_exp(n, h):
                act.wait_ge(s["pd"], n * H + h + 1)
                act.activation(pck[:, h, :], pck[:, h, :], ACT.Exp, scale=SCALE).then_inc(s["pe"], 1)

            def normalise(src, dst, part):
                for c in range(3 * part, 3 * part + 3):
                    ins = act.activation(dst[:, c, :], src[:, c, :], ACT.Identity, bias=sm[:, 3, c:c + 1],
                                         scale=sm[:, 4, c:c + 1])
                return ins

            def turn_maxima(z, n, h, name):
                act.wait_ge(s["xfull"], z.turn(name) + 1)
                if h >= 2 or later(n):
                    act.wait_ge(s["mrow%d" % (h % 2)], 16 * (n * (H // 2) + h // 2))
                act.activation(mT[:, h % 2, :], xm, ACT.Copy).then_inc(s["xfree"], 1)

            def take_values(n, h):
                act.wait_ge(s["av"], n * T_ATT + NC * (h + 1))
                act.activation(avs[:, h % 2, :], psV[:, 0:256], ACT.Copy).then_inc(s["avs"], 1)

            def prepare(z, name):
                j = z.n + 1
                a, w = (z.k + 1) % 4 // 2, (z.k + 1) % 2
                if name.startswith("norm1"):
                    act.wait_ge(s["ln"], 2 * z.n + 2 if not z.start else 1)
                    normalise(hb[:, w] if a == 0 else G[:, w], N, "abc".index(name[5])).then_inc(s["normn"], 1)
                    return
                if name == "cexp":
                    act.wait_ge(s["cm"], j + 1)
                    act.activation(csc[:, 4:5], csc[:, 0:1], ACT.Exp, bias=csc[:, 2:3], scale=SCALE)
                    act.activation(pc[:, :], pc[:, :], ACT.Exp, bias=csc[:, 2:3], scale=SCALE,
                                   accum_out=csc[:, 3:4]).then_inc(s["ce"], 1)
                    return
                act.wait_ge(s["xfull"], z.turn(name) + 1)
                if name in ("nt0", "nt1", "ntc"):
                    if name == "ntc":
                        dst, src = nT[:, 0, 0:1], xcol
                    else:
                        i = int(name[2])
                        dst, src = nT[:, 1 + 4 * i:5 + 4 * i, :].rearrange("p c s -> p (c s)"), psX[:, :]
                    if a == 0:
                        ins = act.activation(dst, src, ACT.Copy)
                    else:
                        ins = act.activation(dst, src, ACT.Identity, bias=c1[:, 0:1], scale=g1[:, 0:1])
                    ins.then_inc(s["xfree"], 1)
                elif name in ("q0", "q1", "k0", "k1"):
                    if name == "q0" and not z.start:
                        for p in range(4):
                            act.wait_ge(s["stk%d" % p], STK * j)
                    i = int(name[1])
                    dst, bias = (qh, bq) if name[0] == "q" else (kh, bk)
                    act.activation(dst[:, 512 * i:512 * i + 512], psX[:, :], ACT.Identity,
                                   bias=bias[:, 0:1] if a == 0 else 0.0).then_inc(s["hi"], 1)
                elif name in ("v0", "v1"):
                    i = int(name[1])
                    act.activation(vt[:, w, 4 * i:4 * i + 4, :, 0:C], x4.rearrange("p c (h e) -> p c h e", h=H),
                                   ACT.Copy).then_inc(s["xfree"], 1)
                elif name == "vc":
                    act.activation(vcb[:, w, :], psX[:, 0:D], ACT.Copy).then_inc(s["xfree"], 1)
                elif name in ("cq0", "cq1"):
                    i = int(name[2])
                    act.activation(pc[:, 512 * i:512 * i + 512], psX[0:H, :], ACT.Copy).then_inc(s["xfree"], 1)
                elif name == "cf":
                    act.activation(clc[:, w:w + 1], xcol, ACT.Identity,
                                   bias=bv[:, 0:1] if a == 0 else 0.0).then_inc(s["xfree"], 1)

            def finish(z, name):
                if name.startswith("norm0"):
                    w = (z.k - 1) % 2
                    act.wait_ge(s["ln"], 2 * z.n + 1)
                    normalise(hb[:, w], G[:, w], "abc".index(name[5])).then_inc(s["normg"], 1)
                    return
                i = int(name[2])
                act.wait_ge(s["xfull"], z.turn(name) + 1)
                act.activation(ctxT[:, 1 + 4 * i:5 + 4 * i, :].rearrange("p c s -> p (c s)"), psX[:, :], ACT.Identity,
                               bias=bv[:, 0:1] if (z.k - 1) % 4 // 2 == 0 else 0.0).then_inc(s["xfree"], 1)

            def route(z, name):
                b = 2 * z.pair if z.k == 3 else 2 * z.pair - 1
                if name == "rexp":
                    act.wait_ge(s["gd"], b + 1)
                    act.activation(rt[:, 1, :], rt[:, 0, :], ACT.Exp).then_inc(s["ge"], 1)
                    return
                dst, src = {"xa": (ctxT[:, 1:5, :], x4), "xb": (ctxT[:, 5:9, :], x4), "xc": (ctxT[:, 0, :], psX[:, 0:P]),
                            "lga": (lg[:, 1:NT, :], psX[:, :].rearrange("p (c e) -> p c e", e=E)),
                            "lgb": (lg[:, 0, :], psX[:, 0:E]),
                            "posa": (pos[:, 1:NT, :], psX[:, :].rearrange("p (c e) -> p c e", e=E)),
                            "posb": (pos[:, 0, :], psX[:, 0:E])}[name]
                act.wait_ge(s["xfull"], z.turn(name) + 1)
                act.activation(dst, src, ACT.Copy).then_inc(s["xfree"], 1)

            ACT_PREPARE = ("norm1a", "norm1b", "norm1c", "nt0", "nt1", "q0", "q1", "k0", "k1", "ntc", "vc", "v0", "v1", "cq0", "cq1", "cexp", "cf")
            ACT_ROUTE = ("xa", "xb", "xc", "lga", "lgb", "rexp", "posa", "posb")

            def act_slot(z):
                n = z.n
                for h in range(H):
                    for c in range(NC):
                        t = NC * h + c
                        for i in range(2):
                            act.wait_ge(s["p2"], UNITS * n + 2 * t + i + 1)
                            if i == 0 and (t >= 4 or z.prev):
                                act.wait_ge(s["av"], n * T_ATT + t - 3)
                            act.activation(pr[:, t % 4, 512 * i:512 * i + 512], ps[:, (2 * t + i) % 3, :], ACT.Exp,
                                           scale=SCALE).then_inc(s["exp"], 1)
                        if c == 3 and h + 2 < H:
                            class_exp(n, h + 2)
                        elif c == 3 and z.nxt:
                            class_exp(z.n + 1, h + 2 - H)
                        if c == 0 and h >= 1:
                            take_values(n, h - 1)
                        elif c == 0 and z.prev:
                            take_values(z.n - 1, H - 1)
                        if c == 1 and h + 2 < H:
                            turn_maxima(z, n, h + 2, "tm%d" % (h + 2))
                        elif c == 1 and z.nxt:
                            turn_maxima(z, z.n + 1, h + 2 - H, "tm%d" % (h + 2))
                        for name in ("ct0", "ct1") + (("norm0a", "norm0b", "norm0c") if z.k in (1, 2) else ()):
                            if z.prev and t == STEP[name]:
                                finish(z, name)
                        for name in ACT_PREPARE:
                            if z.nxt and t == STEP[name]:
                                prepare(z, name)
                        for name in ACT_ROUTE:
                            if z.prev and z.k in (3, 0) and t == STEP[name]:
                                route(z, name)

            z = Outside(-1)
            for name in ACT_PREPARE:
                prepare(z, name)
            for h in range(2):
                turn_maxima(z, 0, h, "tm%d" % h)
                class_exp(0, h)
            slots(act, act_slot)
            z = Outside(2 * B)
            take_values(z.n - 1, H - 1)
            for name in ("ct0", "ct1"):
                finish(z, name)
            for name in ACT_ROUTE:
                route(z, name)
            act.sem_inc(s["gl"], FC)
            with act.Fori(0, E // 2) as g:
                for i in range(2):
                    e = 2 * g + i
                    act.wait_ge(s["yp"], e + 1)
                    for f in range(FC):
                        act.wait_ge(s["hp"], FC * (e + 2) + f + 1)
                        act.activation(hid[i][:, f, :], ps[:, f, :],
                                       ACT.Gelu_apprx_tanh, bias=b1t[:, f, bass.ds(e, 1)]).then_inc(s["gl"], 1)

        @block.vector
        def _(dve):
            dve.sem_inc(s["p1u"], TAKEN_0)
            dve.memset(G[:, 0, 0:SC, :], 0.0)
            dve.memset(clst[:, :], 0.0).then_inc(s["clear"], 1)
            dve.memset(ones_bf[:, :], 1.0)
            dve.memset(ones_f[:, :], 1.0)
            dve.memset(run[:, :, :], 0.0)
            dve.memset(vt[:, :, :, :, :], 0.0).then_inc(s["clear"], 1)
            dve.wait_ge(s["clear"], 2)
            dve.memset(vt[:, :, :, :, C:C + 1], 1.0)
            dve.memset(nT[:, 0, :], 0.0)
            dve.memset(ctxT[:, 0, :], 0.0)
            dve.memset(zrow[:, :], 0.0)
            dve.memset(pcT[:, :, :], 0.0)
            dve.memset(crd[:, :], 0.0)
            dve.memset(pcs[:, :], 0.0)
            dve.memset(mT[:, :, :].bitcast(F32), -1.0).then_inc(s["init"], 1)
            dve.wait_ge(s["const"], 16 * CONSTS)
            dve.wait_ge(s["cls"], 16)

            def maxima(n, w, h, c, i):
                u = U_HEAD * h + 2 * c + i
                dve.wait_ge(s["p1"], UNITS * n + u + 1)
                dve.tensor_reduce(mxu[:, w, h, c, i:i + 1], ps[:, 3 + u % 3, :], AX_X, ALU.max).then_inc(s["p1u"], 1)

            def row_maxima(n, w, h):
                dve.wait_ge(s["p1u"], UNITS * n + (TAKEN_0 + U_HEAD * (h + 1)))
                dve.tensor_reduce(mr[:, h, :], mxu[:, w, h, :, :], AX_X, ALU.max).then_inc(s["mr"], 1)

            def class_key(n, w, h):
                dve.wait_ge(s["mr"], n * H + h + 1)
                dve.tensor_tensor(pck[:, h, :], mxu[:, w, h, :, 2], mr[:, h, :].bitcast(F32),
                                  ALU.subtract).then_inc(s["pd"], 1)

            def split_values(z, n, w, h, name):
                dve.wait_ge(s["xfull"], z.turn(name) + 1)
                dve.wait_ge(s["ut"], n * H + h + 1)
                v4 = xav.rearrange("p (i j e) -> p j i e", i=2, j=4)
                dve.tensor_tensor(U[:, w, :, h, :].rearrange("p (j i) e -> p j i e", i=2), v4[:, :, :, 0:C],
                                  Ut[:, :, h, :].rearrange("p (j i) e -> p j i e", i=2), ALU.add)
                dve.tensor_tensor(den[:, w, :, h].rearrange("p (j i) -> p j i", i=2), v4[:, :, :, C],
                                  pck[:, h, :].rearrange("p (j i) -> p j i", i=2), ALU.add).then_inc(s["xfree"], 1)

            def weigh(z, w, h, name):
                dve.wait_ge(s["xfree"], z.turn(name) + 1)
                dve.reciprocal(den[:, w, :, h], den[:, w, :, h]).then_inc(s["rden"], 1)

            def divide(n, w, h):
                dve.wait_ge(s["rden"], n * H + h + 1)
                dve.tensor_tensor(U[:, w, :, h, :], U[:, w, :, h, :], den[:, w, :, h].unsqueeze(2).broadcast_to(
                    [P, NC, C]), ALU.mult).then_inc(s["ctx"], 1)

            def statistics(src, count, part):
                if part == 0 and later(count):
                    dve.wait_ge(s["ln"], count)
                for c in range(3 * part, 3 * part + 3):
                    ins = dve.bn_stats(st[:, c, :], src[:, c, :])
                if part == 2:
                    ins.then_inc(s["st"], 1)

            def prepare(z, name, link):
                j = z.n + 1
                a, w = (z.k + 1) % 4 // 2, (z.k + 1) % 2
                if name.startswith("stat1"):
                    part = "abc".index(name[5])
                    if a == 1:
                        dve.wait_ge(s["normg"], 3 * (2 * z.pair + w) + part + 1)
                    elif part == 0:
                        dve.wait_ge(s["xfree"], z.turn("e1") + 1)
                    statistics(hb[:, w] if a == 0 else G[:, w], 0 if z.start else 2 * z.n + 1, part)
                    return
                if name == "cmaxa":
                    dve.wait_ge(s["xfree"], z.turn("cq0") + 1)
                    dve.tensor_reduce(csc[:, 1:2], pc[:, 0:512], AX_X, ALU.max)
                    return
                if name == "cmaxb":
                    dve.wait_ge(s["xfree"], z.turn("cq1") + 1)
                    link(dve.tensor_reduce(csc[:, 8:9], pc[:, 512:S], AX_X, ALU.max))
                    link(dve.tensor_tensor(csc[:, 9:10], csc[:, 1:2], csc[:, 0:1], ALU.max))
                    link(dve.tensor_tensor(csc[:, 5:6], csc[:, 9:10], csc[:, 8:9], ALU.max))
                    dve.tensor_scalar(csc[:, 2:3], csc[:, 5:6], -SCALE, None, ALU.mult).then_inc(s["cm"], 1)
                    return
                dve.wait_ge(s["xfull"], z.turn(name) + 1)
                if name in ("e0", "e1"):
                    i = int(name[1])
                    if i == 0:
                        if later(z.pair) or z.k == 3:
                            dve.wait_ge(s["res"], 2 * z.pair + 1 if z.k == 3 else 2 * z.pair)
                        dve.tensor_copy(hb[:, w, 0, :], clst[:, :])
                    dve.tensor_tensor(hb[:, w, 1 + 4 * i:5 + 4 * i, :], x4, pe_t[:, 4 * i:4 * i + 4, :],
                                      ALU.add).then_inc(s["xfree"], 1)
                elif name == "qc":
                    dve.tensor_scalar(qkc[:, 0:1], psX[:, 0:1], bq[:, 0:1] if a == 0 else 0.0, None, ALU.add)
                    ins = dve.tensor_scalar(qkc[:, 1:2], psX[:, 1:2], bk[:, 0:1] if a == 0 else 0.0, None, ALU.add)
                    ins.then_inc(s["xfree"], 1)
                    dve.wait_ge(s["xfree"], z.turn(name) + 1)
                    dve.tensor_scalar(bd[:, 0, :], headmask[:, :], qkc[:, 0:1], None, ALU.mult)
                    link(dve.tensor_scalar(bd[:, 1, :], headmask[:, :], qkc[:, 1:2], None, ALU.mult))
                    link(dve.tensor_copy(bdp[:, :, 0, :], bd[:, :, :]))
                    dve.tensor_tensor(bdp[:, :, 1, :], bd[:, :, :], bdp[:, :, 0, :].bitcast(F32),
                                      ALU.subtract).then_inc(s["bd"], 1)
                elif name in ("q0", "q1", "k0", "k1"):
                    i = int(name[1])
                    cs = slice(512 * i, 512 * i + 512)
                    hi, lo, bias = (qh, ql, bq) if name[0] == "q" else (kh, kl, bk)
                    dve.wait_ge(s["hi"], 4 * j + (1 if name[0] == "q" else 3) + i)
                    dve.scalar_tensor_tensor(lo[:, cs], psX[:, :], bias[:, 0:1] if a == 0 else 0.0,
                                             hi[:, cs].bitcast(F32), ALU.add, ALU.subtract).then_inc(s["xfree"], 1)
                elif name == "ck":
                    dve.tensor_reduce(mxu[:, w, :, :, 2], psX[:, 0:2 * NC * H].rearrange(
                        "p (c i h) -> p h c i", i=2, h=H), AX_X, ALU.add).then_inc(s["xfree"], 1)
                elif name == "cc":
                    dve.tensor_copy(csc[:, 0:1], psX[0:H, 0:1]).then_inc(s["xfree"], 1)
                elif name == "pt":
                    dve.tensor_copy(pcT[:, :, 0:H], xhc.rearrange("p (h c) -> p c h", c=NC)).then_inc(s["xfree"], 1)
                    link(dve.tensor_tensor(csc[:, 6:7], csc[:, 3:4], csc[:, 4:5], ALU.add))
                    dve.scalar_tensor_tensor(cmv[:, :], vcb[0:H, w, :], csc[:, 4:5], headmaskT[0:H, :], ALU.mult,
                                             ALU.mult)
                    link(dve.reciprocal(csc[:, 7:8], csc[:, 6:7]))
                    for q in range(4):
                        dve.tensor_copy(crd[32 * q:32 * q + H, :], csc[:, 7:8])
                elif name == "co":
                    dve.tensor_tensor(cm[:, :], psX[:, 0:D], headmaskT[:, :], ALU.mult).then_inc(s["xfree"], 1)

            def finish(z, name):
                a, w = (z.k - 1) % 4 // 2, (z.k - 1) % 2
                t = (hb if a == 0 else G)[:, w]
                if name.startswith("stat0"):
                    part = "abc".index(name[5])
                    dve.wait_ge(s["xfree"], z.turn("o1" if part else "o0") + 1)
                    statistics(t, 2 * z.n - (1 if isinstance(z, Outside) else 0), part)
                    return
                dve.wait_ge(s["xfull"], z.turn(name) + 1)
                if name == "oc":
                    if a == 0:
                        dve.wait_ge(s["biased"], 2 * z.pair + w + 1)
                    ins = dve.tensor_tensor(t[0:1, 0, :], xrow, t[0:1, 0, :], ALU.add)
                else:
                    cs = slice(1 + 4 * int(name[1]), 5 + 4 * int(name[1]))
                    ins = dve.tensor_tensor(t[:, cs, :], x4, t[:, cs, :], ALU.add)
                ins.then_inc(s["xfree"], 1)

            def route(z, name, link):
                b = 2 * z.pair if z.k == 3 else 2 * z.pair - 1
                if name == "rmaxa":
                    dve.wait_ge(s["xfree"], z.turn("lgb") + 1)
                    dve.tensor_copy(vtick[:, :], ones_f[:, :])
                    for c in range(4):
                        dve.max(mv[:, c, :], lg[:, c, :])
                elif name == "rmaxb":
                    for c in range(4, NT):
                        ins = dve.max(mv[:, c, :], lg[:, c, :])
                    link(ins)
                    dve.tensor_tensor(rt[:, 0, :], mv[:, :, 1], mv[:, :, 0], ALU.subtract).then_inc(s["gd"], 1)
                elif name == "ridxa":
                    for c in range(4):
                        dve.max_index(mi[:, c, :], mv[:, c, :], lg[:, c, :])
                elif name == "ridxb":
                    for c in range(4, NT):
                        ins = dve.max_index(mi[:, c, :], mv[:, c, :], lg[:, c, :])
                    link(ins)
                    for k in range(TOPK):
                        ins = dve.scalar_tensor_tensor(e1[:, k, :], mi[:, :, k], 1.0, valid[:, :], ALU.add, ALU.mult)
                    link(ins)
                elif name in ("roha", "rohb"):
                    k = "ab".index(name[3])
                    ins = dve.tensor_tensor(oh[:, k, :, :], iota1[:, :].unsqueeze(1).broadcast_to([P, NT, E]),
                                            e1[:, k, :].unsqueeze(2).broadcast_to([P, NT, E]), ALU.is_equal)
                    if k == 1:
                        ins.then_inc(s["ohr"], 1)
                elif name == "rred":
                    dve.wait_ge(s["ohp"], b + 1)
                    link(dve.tensor_reduce(pk[:, :, :], oh[:, :, :, :], AX_X, ALU.add))
                elif name == "routa":
                    link(dve.tensor_scalar(keep[:, :, :], pk[:, :, :], float(CAP), None, ALU.is_lt))
                    for k in range(TOPK):
                        dve.tensor_tensor(rt[:, 2 + k, :], keep[:, k, :], valid[:, :], ALU.mult)
                        dve.scalar_tensor_tensor(rt[:, 4 + k, :], e1[:, k, :], float(CAP), pk[:, k, :], ALU.mult,
                                                 ALU.add)
                        ins = dve.tensor_scalar(rt[:, 6 + k, :], pk[:, k, :], float(CAP - 1), None, ALU.min)
                    link(ins)
                    for k in range(TOPK):
                        dve.tensor_scalar(rt[:, 8 + k, :], rt[:, 2 + k, :], -OUT_OF_BOUNDS, OUT_OF_BOUNDS - CAP,
                                          ALU.mult, ALU.add)
                        ins = dve.scalar_tensor_tensor(rt[:, 10 + k, :], e1[:, k, :], float(CAP), rt[:, 6 + k, :],
                                                       ALU.mult, ALU.add)
                    link(ins)
                elif name == "routb":
                    dve.wait_ge(s["x2f"], b + 1)
                    for k in range(TOPK):
                        dve.tensor_tensor(sidx[:, :, k], rt[:, 4 + k, :], rt[:, 8 + k, :], ALU.add)
                        ins = dve.tensor_scalar(gidx[:, bass.ds(b, 1), :, k].rearrange("p o c -> p (o c)"),
                                                rt[:, 10 + k, :], -float(CAP), 0.0, ALU.add, ALU.max)
                    ins.then_inc(s["sidx"], 1)
                elif name == "routc":
                    dve.wait_ge(s["ge"], b + 1)
                    link(dve.tensor_scalar(rt[:, 2, :], rt[:, 1, :], 1.0, None, ALU.add))
                    link(dve.reciprocal(rt[:, 3, :], rt[:, 2, :]))
                    dve.wait_ge(s["sidx"], b + 1)
                    link(dve.tensor_tensor(rt[:, 4, :], rt[:, 3, :], rt[:, 1, :], ALU.mult))
                    for k in range(TOPK):
                        ins = dve.tensor_tensor(gate[:, bass.ds(b, 1), :, k].rearrange("p o c -> p (o c)"),
                                                rt[:, 3 + k, :], keep[:, k, :], ALU.mult)
                    ins.then_inc(s["gated"], 1)

            DVE_PREPARE = ("stat1a", "stat1b", "stat1c", "q0", "q1", "k0", "k1", "qc", "ck", "cc", "cmaxa", "cmaxb", "pt", "co")
            DVE_ROUTE = ("rmaxa", "rmaxb", "ridxa", "ridxb", "roha", "rohb", "rred", "routa", "routb", "routc")

            def dve_slot(z):
                n = z.n
                w = z.k % 2
                qlink = chain(dve, "qclink", QC_LINKS, z.n + 1)
                rlink = chain(dve, "rlink", R_LINKS, 2 * z.pair if z.k == 3 else 2 * z.pair - 1)
                for h in range(H):
                    for c in range(NC):
                        t = NC * h + c - 1
                        if h + 3 < H:
                            maxima(n, w, h + 3, c, 0)
                        elif z.nxt:
                            maxima(z.n + 1, 1 - w, h + 3 - H, c, 0)
                        if c == 0 and h + 2 < H:
                            row_maxima(n, w, h + 2)
                        elif c == 0 and z.nxt:
                            row_maxima(z.n + 1, 1 - w, h + 2 - H)
                        if c == 1 and h + 2 < H:
                            class_key(n, w, h + 2)
                        elif c == 1 and z.nxt:
                            class_key(z.n + 1, 1 - w, h + 2 - H)
                        if c == 4 and h >= 1:
                            split_values(z, n, w, h - 1, "tv%d" % (h - 1))
                        if c == 5 and h >= 1:
                            weigh(z, w, h - 1, "tv%d" % (h - 1))
                        if c == 6 and h >= 1:
                            divide(n, w, h - 1)
                        if z.prev:
                            if t == STEP["tv7"]:
                                split_values(z, z.n - 1, 1 - w, H - 1, "tv7")
                                weigh(z, 1 - w, H - 1, "tv7")
                                divide(z.n - 1, 1 - w, H - 1)
                            for name in ("oc", "o0", "o1", "stat0a", "stat0b", "stat0c"):
                                if t == STEP[name]:
                                    finish(z, name)
                        if z.nxt:
                            for name in (EMBED if z.k in (3, 0) else ()) + DVE_PREPARE:
                                if t == STEP[name]:
                                    prepare(z, name, qlink)
                        if z.prev and z.k in (3, 0):
                            for name in DVE_ROUTE:
                                if t == STEP[name]:
                                    route(z, name, rlink)
                        if h + 3 < H:
                            maxima(n, w, h + 3, c, 1)
                        elif z.nxt:
                            maxima(z.n + 1, 1 - w, h + 3 - H, c, 1)

            z = Outside(-1)
            qlink = chain(dve, "qclink", QC_LINKS, 0)
            for name in EMBED + DVE_PREPARE:
                prepare(z, name, qlink)
            for h in range(3):
                for c in range(NC):
                    for i in range(2):
                        maxima(0, 0, h, c, i)
                if h < 2:
                    row_maxima(0, 0, h)
                    class_key(0, 0, h)
            slots(dve, dve_slot)
            z = Outside(2 * B)
            split_values(z, z.n - 1, 1, H - 1, "tv7")
            weigh(z, 1, H - 1, "tv7")
            divide(z.n - 1, 1, H - 1)
            for name in ("oc", "o0", "o1", "stat0a", "stat0b", "stat0c"):
                finish(z, name)
            dve.wait_ge(s["ln"], 2 * z.n)
            for c in range(NT):
                ins = dve.tensor_scalar(x2[:, c, :], G[:, 1, c, :], sm[:, 4, c:c + 1], sm[:, 3, c:c + 1], ALU.mult,
                                        ALU.add)
            ins.then_inc(s["x2g"], 1)
            dve.wait_ge(s["x2g"], B)
            dve.tensor_tensor(x2[:, :, :], x2[:, :, :], g2[:, :].unsqueeze(1).broadcast_to([P, NT, D]),
                              ALU.mult).then_inc(s["x2g"], 1)
            dve.wait_ge(s["x2g"], B + 1)
            dve.tensor_tensor(x2[:, :, :], x2[:, :, :], c2[:, :].unsqueeze(1).broadcast_to([P, NT, D]),
                              ALU.add).then_inc(s["x2"], 1)
            rlink = chain(dve, "rlink", R_LINKS, B - 1)
            for name in DVE_ROUTE:
                route(z, name, rlink)
            dve.wait_ge(s["gated"], B)
            dve.sem_inc(s["attended"], 1)
            dve.sem_inc(s["yo"], 2)
            dve.sem_inc(s["xt"], 1)
            dve.sem_inc(s["ws"], 2)
            def take_slots(e, g, i):
                dve.wait_ge(s["tp"], e + 3)
                dve.wait_ge(s["hp"], FC * (e + 1))
                dve.tensor_copy(xh[i], psX[:, :]).then_inc(s["xh"], 1)
                dve.wait_ge(s["xh"], e + 1)
                dve.tensor_tensor(xl[i], psX[:, :], xh[i].bitcast(F32), ALU.subtract).then_inc(s["xt"], 1)
                dve.wait_ge(s["wa%d" % i], 16 * g + 16)
                dve.tensor_copy(w1h[i], w1t[i]).then_inc(s["wh"], 1)
                dve.wait_ge(s["wh"], e + 1)
                dve.tensor_tensor(w1l[i], w1t[i], w1h[i].bitcast(F32), ALU.subtract).then_inc(s["ws"], 1)

            def take_down(e, g, i):
                dve.wait_ge(s["yp"], e + 3)
                dve.wait_ge(s["bb%d" % i], 16 * g + 16)
                dve.wait_ge(s["ysf"], e + 1)
                dve.tensor_tensor(yout[i], ps[:, 4 + i, :].rearrange("p (c d) -> p c d", d=D),
                                  b2t[i].unsqueeze(1).broadcast_to([P, SC, D]), ALU.add).then_inc(s["yo"], 1)

            take_slots(0, 0, 0)
            take_slots(1, 0, 1)
            take_down(0, 0, 0)
            with dve.Fori(1, E // 2) as g:
                take_slots(2 * g, g, 0)
                take_down(2 * g - 1, g - 1, 1)
                take_slots(2 * g + 1, g, 1)
                take_down(2 * g, g, 0)
            take_down(E - 1, E // 2 - 1, 1)
            dve.sem_inc(s["fin"], 2)
            dve.wait_ge(s["yst0"], 16 * (E // 2))
            dve.wait_ge(s["yst1"], 16 * (E // 2))
            with dve.Fori(0, B // 4) as g:
                for m in range(4):
                    b = 4 * g + m
                    dve.wait_ge(s["fin"], 4 * g + 2)
                    dve.tensor_copy(gi[:, m, :, :], gidx[:, bass.ds(b, 1), :, :].rearrange("p o c k -> p (o c) k"))
                    dve.tensor_copy(gg[:, m, :, :], gate[:, bass.ds(b, 1), :, :].rearrange("p o c k -> p (o c) k")
                                    ).then_inc(s["gi"], 1)
                for m in range(4):
                    b, i = 4 * g + m, m % 2
                    dve.wait_ge(s["gi"], 4 * g + 4)
                    dve.wait_ge(s["ga%d" % i], 16 * NT * TOPK * (2 * g + m // 2 + 1))
                    dve.wait_ge(s["rs%d" % m], 16 * g + 16)
                    for c in range(NT):
                        ins = dve.scalar_tensor_tensor(fin[m][:, c, :], rows[2 * i][:, c, :], gg[:, m, c, 0:1],
                                                       fin[m][:, c, :], ALU.mult, ALU.add)
                    ins.then_inc(s["done"], 1)
                    dve.wait_ge(s["done"], b + 1)
                    for c in range(NT):
                        ins = dve.scalar_tensor_tensor(fin[m][:, c, :], rows[2 * i + 1][:, c, :], gg[:, m, c, 1:2],
                                                       fin[m][:, c, :], ALU.mult, ALU.add)
                    ins.then_inc(s["fin"], 1)

        @block.gpsimd
        def _(pool):
            pool.memset(kst[:, :, :].bitcast(F32), 0.0).then_inc(s["init"], 1)
            pool.memset(qst[:, :, :].bitcast(F32), 0.0).then_inc(s["init"], 1)
            pool.memset(tick[:, :], 0.0).then_inc(s["tick"], 1)
            pool.wait_ge(s["tick"], 1)
            pool.sem_inc(s["x2f"], 1)
            pool.sem_inc(s["ysf"], 2)
            last_slot = pool.to_reg(SLOTS - 1)
            for i, value in enumerate((-0.5, 0.5, 1.0 / D, EPS, -1.0)):
                pool.memset(consts[:, i, :], value).then_inc(s["consts"], 1)
            pool.wait_ge(s["consts"], 5)
            pool.wait_ge(s["clear"], 1)
            pool.wait_ge(s["const"], 16 * CONSTS)

            def norm(count, src=None, dst=None, add=None):
                link = chain(pool, "lnlink", LN_LINKS, count)
                pool.wait_ge(s["st"], count + 1)
                v = [sm[:, i, :] for i in range(8)]
                k = [consts[:, i, :] for i in range(5)]
                pool.tensor_tensor(v[0], st[:, :, 1], st[:, :, 4], ALU.add)
                pool.tensor_tensor(v[1], st[:, :, 1], st[:, :, 4], ALU.subtract)
                link(pool.tensor_tensor(v[2], st[:, :, 2], st[:, :, 5], ALU.add))
                pool.tensor_tensor(v[6], v[0], k[1], ALU.mult)
                pool.tensor_tensor(v[3], v[1], k[1], ALU.mult)
                link(pool.tensor_tensor(v[5], v[2], k[2], ALU.mult))
                if dst is not None:
                    link(pool.tensor_tensor(dst, src, v[6].unsqueeze(2).broadcast_to([P, NT, D]), ALU.subtract))
                    pool.tensor_tensor(src, src, add, ALU.add).then_inc(s["res"], 1)
                pool.tensor_tensor(v[7], v[3], v[3], ALU.mult)
                link(pool.tensor_tensor(v[0], v[5], k[3], ALU.add))
                link(pool.tensor_tensor(v[2], v[0], v[7], ALU.add))
                link(pool.tensor_tensor(v[4], v[2], k[0], ALU.pow))
                if dst is None:
                    link(pool.tensor_tensor(v[5], v[6], v[4], ALU.mult))
                    pool.tensor_tensor(v[3], v[5], k[4], ALU.mult).then_inc(s["ln"], 1)
                    return
                pool.tensor_tensor(dst, dst, v[4].unsqueeze(2).broadcast_to([P, NT, D]), ALU.mult
                                   ).then_inc(s["ln"], 1)

            def norm_next(z):
                a, w = (z.k + 1) % 4 // 2, (z.k + 1) % 2
                count = 0 if z.start else 2 * z.n + 1
                norm(count)
                if a == 0:
                    pool.wait_ge(s["normn"], 3 * (z.n + 1) + 3)
                    pool.tensor_tensor(hb[:, w], hb[:, w], bo[:, :].unsqueeze(1).broadcast_to([P, NT, D]),
                                       ALU.add).then_inc(s["biased"], 1)

            def norm_last(z):
                a, w = (z.k - 1) % 4 // 2, (z.k - 1) % 2
                if a == 0:
                    norm(2 * z.n)
                else:
                    norm(2 * z.n, G[:, w], x2[:, :, :], hb[:, w])

            def expert_input(z):
                b = 2 * z.pair if z.k == 3 else 2 * z.pair - 1
                pool.wait_ge(s["ln"], 2 * z.n + 1)
                pool.tensor_tensor(x2[:, :, :], x2[:, :, :], g2[:, :].unsqueeze(1).broadcast_to([P, NT, D]),
                                   ALU.mult).then_inc(s["x2g"], 1)
                pool.wait_ge(s["x2g"], b + 1)
                pool.tensor_tensor(x2[:, :, :], x2[:, :, :], c2[:, :].unsqueeze(1).broadcast_to([P, NT, D]),
                                   ALU.add).then_inc(s["x2"], 1)

            def class_share(n, w, h):
                pool.wait_ge(s["pe"], n * H + h + 1)
                pool.tensor_tensor(Ut[:, :, h, :], vcb[:, w, C * h:C * h + C].unsqueeze(1).broadcast_to([P, NC, C]),
                                   pck[:, h, :].unsqueeze(2).broadcast_to([P, NC, C]), ALU.mult).then_inc(s["ut"], 1)

            def running(b):
                link = chain(pool, "runlink", RUN_LINKS, b)
                pool.wait_ge(s["ohr"], b + 1)
                pool.tensor_tensor(ohs[:, :, :], oh[:, 0, :, :], oh[:, 1, :, :], ALU.add).then_inc(s["ohs"], 1)
                pool.wait_ge(s["ohs"], b + 1)
                link(pool.tensor_tensor(run[:, 0, :], run[:, NT, :], ones_bf[:, 0:E], ALU.mult))
                for c in range(NT):
                    link(pool.tensor_tensor(run[:, c + 1, :], run[:, c, :], ohs[:, c, :], ALU.add))
                pool.sem_inc(s["oh"], 1)

            def ranks(b, turn):
                pool.wait_ge(s["xfree"], turn + 1)
                for k in range(TOPK):
                    ins = pool.tensor_tensor(oh[:, k, :, :], oh[:, k, :, :], pos[:, :, :], ALU.mult)
                ins.then_inc(s["ohp"], 1)

            def scatter(b):
                pool.wait_ge(s["sidx"], b + 1)
                pool.wait_ge(s["tick"], b + 1)
                pool.tensor_tensor(tick[:, :], tick[:, :], tick[:, :], ALU.mult).then_inc(s["tick"], 1)
                for c in range(NT):
                    for k in range(TOPK):
                        pool.indirect_dma_start(
                            out=slots_in, out_offset=bass.IndirectOffsetOnAxis(ap=sidx[:, c, k:k + 1], axis=0),
                            in_=x2[:, c, :], in_offset=None, bounds_check=last_slot,
                            oob_is_err=False).then_inc(s["scat"], 16)
                pool.wait_ge(s["scat"], 16 * NT * TOPK * b + 16 * NT * TOPK)
                pool.sem_inc(s["x2f"], 1)

            def pool_slot(z):
                n = z.n
                w = z.k % 2
                for h in range(H):
                    if h + 2 < H:
                        class_share(n, w, h + 2)
                    elif z.nxt:
                        class_share(z.n + 1, 1 - w, h + 2 - H)
                    if not z.prev:
                        for e in range(h * E // H, (h + 1) * E // H):
                            pool.dma_start(slots_in[e * CAP:(e + 1) * CAP, :].rearrange("(c p) d -> p c d", p=P),
                                           G[:, 0, 0:SC, :]).then_inc(s["zeroed"], 16)
                    if h == 0 and z.prev:
                        norm_last(z)
                    if h == 0 and z.nxt:
                        norm_next(z)
                    if h == 0 and z.prev and z.k in (3, 0):
                        expert_input(z)
                    if h == 4 and z.prev and z.k in (3, 0):
                        running(2 * z.pair if z.k == 3 else 2 * z.pair - 1)
                        ranks(2 * z.pair if z.k == 3 else 2 * z.pair - 1, z.turn("posb"))
                if not z.prev:
                    pool.wait_ge(s["zeroed"], 16 * E)
                if z.prev and z.k in (3, 0):
                    scatter(2 * z.pair if z.k == 3 else 2 * z.pair - 1)
                    if z.k == 0:
                        for i in range(2):
                            pool.wait_ge(s["resd%d" % i], 16 * z.pair)

            norm_next(Outside(-1))
            for h in range(2):
                class_share(0, 0, h)
            slots(pool, pool_slot)
            norm(4 * B - 1)
            pool.wait_ge(s["x2"], B)
            pool.tensor_tensor(G[:, 1], G[:, 1], hb[:, 1], ALU.add).then_inc(s["res"], 1)
            running(B - 1)
            ranks(B - 1, Outside(2 * B).turn("posb"))
            scatter(B - 1)
            with pool.Fori(0, E // 2) as g:
                for i in range(2):
                    e = 2 * g + i
                    pool.wait_ge(s["yo"], e + 3)
                    pool.dma_start(slots_out[bass.ds(e * CAP, CAP), :].rearrange("(c p) d -> p c d", p=P),
                                   yout[i]).then_inc(s["yst%d" % i], 16)
                for i in range(2):
                    pool.wait_ge(s["yst%d" % i], 16 * g + 16)
                    pool.sem_inc(s["ysf"], 1)
            pool.wait_ge(s["yst0"], 16 * (E // 2))
            pool.wait_ge(s["yst1"], 16 * (E // 2))
            with pool.Fori(0, B // 4) as g:
                for m in range(4):
                    b, i = 4 * g + m, m % 2
                    pool.wait_ge(s["gi"], b + 1)
                    pool.wait_ge(s["fin"], b + 1)
                    pool.wait_ge(s["tick"], B + 1 + b)
                    pool.tensor_tensor(tick[:, :], tick[:, :], tick[:, :], ALU.mult).then_inc(s["tick"], 1)
                    for c in range(NT):
                        for k in range(TOPK):
                            pool.indirect_dma_start(
                                out=rows[2 * i + k][:, c, :], out_offset=None, in_=slots_out,
                                in_offset=bass.IndirectOffsetOnAxis(ap=gi[:, m, c, k:k + 1], axis=0),
                                bounds_check=last_slot, oob_is_err=False).then_inc(s["ga%d" % i], 16)


def position_encoding():
    import math
    position = np.arange(2 * S, dtype=np.float32)[:, None]
    div_term = np.exp(np.arange(0, D, 2, dtype=np.float32) * (-math.log(10000.0) / D))
    pe = np.zeros((2 * S, D), dtype=np.float32)
    pe[:, 0::2] = np.sin(position * div_term)
    pe[:, 1::2] = np.cos(position * div_term)
    return pe[:S]


def kernel(**inputs):
    import ml_dtypes
    import concourse.bacc as bacc
    from concourse.bass_utils import run_bass_kernel_spmd

    i = {k: np.asarray(v) for k, v in inputs.items()}

    def row(a):
        return a.reshape(1, -1)

    def col(a):
        return a.reshape(-1, 1)

    wqkv = i["L0_attn_qkv_w"].reshape(H, 3, C, D)
    bqkv = i["L0_attn_qkv_b"].reshape(H, 3, C)
    arrays = {
        "x": i["x"].reshape(B * S, F_IN).T,
        "cls_tok": i["cls_tok"].reshape(1, D),
        "pe": position_encoding().reshape(NC, P, D).transpose(1, 0, 2),
        "tokW": i["L0_tok_W"],
        "wq1": wqkv[:, 0].reshape(D, D).T, "wk1": wqkv[:, 1].reshape(D, D).T, "wv1": wqkv[:, 2].reshape(D, D).T,
        "bq1": col(bqkv[:, 0]), "bk1": col(bqkv[:, 1]), "bv1": col(bqkv[:, 2]),
        "wo1": i["L0_attn_out_w"].T, "bo1": row(i["L0_attn_out_b"]),
        "ln1g": col(i["L0_ffn_ln1_g"]), "ln1b": col(i["L0_ffn_ln1_b"]),
        "wq2": i["L0_ffn_wq"], "wk2": i["L0_ffn_wk"], "wv2": i["L0_ffn_wv"], "wo2": i["L0_ffn_wo"],
        "ln2g": row(i["L0_ffn_ln2_g"]), "ln2b": row(i["L0_ffn_ln2_b"]),
        "wr": i["L0_ffn_wr"],
        "w1": i["L0_ffn_w1"].reshape(E * D, F),
        "b1": i["L0_ffn_b1"].reshape(E, P, FC).transpose(1, 2, 0),
        "w2": i["L0_ffn_w2"].reshape(E * P, FC * D),
        "b2": i["L0_ffn_b2"],
        "ident_d": np.eye(P, dtype=np.float32),
        "headmask_d": np.repeat(np.eye(H, dtype=np.float32), C, axis=0),
        "headmaskT_d": np.tile(np.repeat(np.eye(32, H, dtype=np.float32), C, axis=1), (4, 1)),
        "lower_d": np.triu(np.ones((P, P), dtype=np.float32), 1).astype(ml_dtypes.bfloat16),
        "iota_d": np.tile(np.arange(1, E + 1, dtype=np.float32), (P, 1)),
        "valid_d": np.concatenate([np.eye(P, 1, dtype=np.float32), np.ones((P, NC), np.float32)], axis=1),
    }
    nc = bacc.Bacc("TRN2", target_bir_lowering=False, num_devices=1)
    named, args = {}, {}
    for name, a in arrays.items():
        a = np.ascontiguousarray(a)
        named["in_" + name] = a
        args[name] = nc.dram_tensor("in_" + name, a.shape, mybir.dt.from_np(a.dtype), kind="ExternalInput").ap()
    args["out"] = nc.dram_tensor("out_0", (B, S + 1, D), F32, kind="ExternalOutput").ap()
    build(nc, **args)
    r = run_bass_kernel_spmd(nc, [named], core_ids=[0])
    return r.results[0]["out_0"]
```
